# Optimizing a Trainium2 kernel written in Bass

```python
import numpy as np
import jax
import jax.numpy as jnp

def _softmax(x, axis=-1):
    return jax.nn.softmax(x, axis=axis)

def _gelu(x):
    return jax.nn.gelu(x, approximate=True)

def _silu(x):
    return jax.nn.silu(x)

def _sigmoid(x):
    return jax.nn.sigmoid(x)

def _layernorm(x, axis=-1, eps=1e-05):
    m = jnp.mean(x, axis=axis, keepdims=True)
    v = jnp.var(x, axis=axis, keepdims=True)
    return (x - m) / jnp.sqrt(v + eps)

def _scatter_add(tgt, idx, src, axis=0):
    return tgt.at[idx].add(src)

def _segment_sum(src, seg, n):
    return jax.ops.segment_sum(src, seg, n)
kernel_name = 'mk_gnn_resnorm_d2_gnn_r8_3ecc0a'

def setup_inputs(seed: int=0):
    np.random.seed(seed)
    _w = jnp.asarray

    def _rec_inputs():
        import jax
        import jax.numpy as jnp
        _gk = jax.random.key(seed)
        x = -0.000202 + 1 * jax.random.normal(jax.random.fold_in(_gk, 1), (6250, 128), jnp.float32)
        _s = jax.random.randint(jax.random.fold_in(_gk, 2), (100000,), 0, 6250, jnp.int32)
        _d = jax.random.randint(jax.random.fold_in(_gk, 3), (100000,), 0, 6250, jnp.int32)
        _loop = jnp.arange(6250, dtype=jnp.int32)
        src = jnp.concatenate([_s, _d, _loop])
        dst = jnp.concatenate([_d, _s, _loop])
        _o = jnp.argsort(dst, stable=True)
        src = src[_o]
        dst = dst[_o]
        edge_attr_128 = -4.21973e-05 + 0.999841 * jax.random.normal(jax.random.fold_in(_gk, 11), (206250, 128), jnp.float32)
        edge_attr_16 = 0.000196303 + 1.00016 * jax.random.normal(jax.random.fold_in(_gk, 12), (206250, 16), jnp.float32)
        edge_weight1 = jax.random.uniform(jax.random.fold_in(_gk, 14), (206250, 1), jnp.float32, 0.0, 0.999999)
        return (x, src, dst, edge_attr_128, edge_attr_16, edge_weight1)
    x, src, dst, edge_attr_128, edge_attr_16, edge_weight1 = _rec_inputs()

    def _L0_gnn_setup():
        import jax, jax.numpy as jnp
        import numpy as np
        H, C = (4, 32)
        NEG_SLOPE = 0.2
        LN_EPS = 1e-05
        N_NODES = 6250
        N_EDGES = 200000
        IN_CH = 128
        EDGE_DIM = 16
        key = jax.random.key(seed)
        ks = jax.random.split(key, 10)
        sc = 0.1
        return {'x': jax.random.normal(ks[0], (N_NODES, IN_CH), jnp.float32), 'edge_index': jax.random.randint(ks[1], (2, N_EDGES), 0, N_NODES, jnp.int32), 'edge_attr': jax.random.normal(ks[2], (N_EDGES, EDGE_DIM), jnp.float32), 'W_lin': jax.random.normal(ks[3], (H * C, IN_CH), jnp.float32) * sc, 'W_edge': jax.random.normal(ks[4], (H * C, EDGE_DIM), jnp.float32) * sc, 'att_src': jax.random.normal(ks[5], (1, H, C), jnp.float32) * sc, 'att_dst': jax.random.normal(ks[6], (1, H, C), jnp.float32) * sc, 'att_edge': jax.random.normal(ks[7], (1, H, C), jnp.float32) * sc, 'bias': jnp.zeros((H * C,), jnp.float32), 'ln_gamma': jnp.ones((H * C,), jnp.float32), 'ln_beta': jnp.zeros((H * C,), jnp.float32)}
    _L0_gnn_all = _L0_gnn_setup()
    _L0_gnn_in = {k: v for k, v in _L0_gnn_all.items() if k in ('W_lin', 'W_edge', 'att_src', 'att_dst', 'att_edge', 'bias', 'ln_gamma', 'ln_beta')}
    del _L0_gnn_all

    def _L1_gnn_setup():
        import jax, jax.numpy as jnp
        import numpy as np
        N_NODES = 6250
        N_EDGES = 75000
        HIDDEN = 128
        N_HEADS = 8
        HEAD_DIM = HIDDEN // N_HEADS
        key = jax.random.key(seed)
        ks = jax.random.split(key, 7)
        x = jax.random.normal(ks[0], (N_NODES, HIDDEN), dtype=jnp.float32)
        w_ij = jax.random.normal(ks[1], (N_EDGES, HIDDEN), dtype=jnp.float32)
        edge_index = jax.random.randint(ks[2], (2, N_EDGES), 0, N_NODES, dtype=jnp.int64)
        cutoff = jax.random.uniform(ks[3], (N_EDGES, 1), dtype=jnp.float32)
        scale = 1.0 / np.sqrt(HIDDEN)
        Wq = jax.random.normal(ks[4], (HIDDEN, HIDDEN), dtype=jnp.float32) * scale
        Wk = jax.random.normal(ks[5], (HIDDEN, HIDDEN), dtype=jnp.float32) * scale
        Wv = jax.random.normal(ks[6], (HIDDEN, HIDDEN), dtype=jnp.float32) * scale
        return {'x': x, 'w_ij': w_ij, 'edge_index': edge_index, 'cutoff': cutoff, 'Wq': Wq, 'Wk': Wk, 'Wv': Wv}
    _L1_gnn_all = _L1_gnn_setup()
    _L1_gnn_in = {k: v for k, v in _L1_gnn_all.items() if k in ('Wq', 'Wk', 'Wv')}
    del _L1_gnn_all
    return {'x': x, 'src': src, 'dst': dst, 'edge_attr_128': edge_attr_128, 'edge_attr_16': edge_attr_16, 'edge_weight1': edge_weight1, 'L0_gnn_W_lin': _L0_gnn_in['W_lin'], 'L0_gnn_W_edge': _L0_gnn_in['W_edge'], 'L0_gnn_att_src': _L0_gnn_in['att_src'], 'L0_gnn_att_dst': _L0_gnn_in['att_dst'], 'L0_gnn_att_edge': _L0_gnn_in['att_edge'], 'L0_gnn_bias': _L0_gnn_in['bias'], 'L0_gnn_ln_gamma': _L0_gnn_in['ln_gamma'], 'L0_gnn_ln_beta': _L0_gnn_in['ln_beta'], 'L1_gnn_Wq': _L1_gnn_in['Wq'], 'L1_gnn_Wk': _L1_gnn_in['Wk'], 'L1_gnn_Wv': _L1_gnn_in['Wv']}

def reference(x, src, dst, edge_attr_128, edge_attr_16, edge_weight1, L0_gnn_W_lin, L0_gnn_W_edge, L0_gnn_att_src, L0_gnn_att_dst, L0_gnn_att_edge, L0_gnn_bias, L0_gnn_ln_gamma, L0_gnn_ln_beta, L1_gnn_Wq, L1_gnn_Wk, L1_gnn_Wv):
    import jax
    import jax.numpy as jnp

    def _L0_gnn_ref(x, edge_index, edge_attr, W_lin, W_edge, att_src, att_dst, att_edge, bias, ln_gamma, ln_beta):
        import jax, jax.numpy as jnp
        import numpy as np
        H, C = (4, 32)
        NEG_SLOPE = 0.2
        LN_EPS = 1e-05
        N_NODES = 6250
        N_EDGES = 200000
        IN_CH = 128
        EDGE_DIM = 16
        N = x.shape[0]
        src, dst = (edge_index[0], edge_index[1])
        xl = (x @ W_lin.T).reshape(N, H, C)
        ef = (edge_attr @ W_edge.T).reshape(-1, H, C)
        x_j = xl[src]
        x_i = xl[dst]
        alpha = (x_i * att_src).sum(-1) + (x_j * att_dst).sum(-1) + (ef * att_edge).sum(-1)
        alpha = jax.nn.leaky_relu(alpha, NEG_SLOPE)
        amax = jax.ops.segment_max(alpha, dst, num_segments=N)
        e = jnp.exp(alpha - amax[dst])
        denom = jax.ops.segment_sum(e, dst, num_segments=N)
        alpha = e / (denom[dst] + 1e-16)
        msg = x_j * alpha[..., None]
        out = jax.ops.segment_sum(msg, dst, num_segments=N)
        out = out.reshape(N, H * C) + bias
        out = out + x
        mu = out.mean(-1, keepdims=True)
        var = ((out - mu) ** 2).mean(-1, keepdims=True)
        out = (out - mu) / jnp.sqrt(var + LN_EPS) * ln_gamma + ln_beta
        return jax.nn.elu(out)

    def _L1_gnn_ref(x, w_ij, edge_index, cutoff, Wq, Wk, Wv):
        import jax, jax.numpy as jnp
        import numpy as np
        N_NODES = 6250
        N_EDGES = 75000
        HIDDEN = 128
        N_HEADS = 8
        HEAD_DIM = HIDDEN // N_HEADS
        n = x.shape[0]
        q = (x @ Wq.T).reshape(n, N_HEADS, HEAD_DIM)
        k = (x @ Wk.T).reshape(n, N_HEADS, HEAD_DIM)
        v = (x @ Wv.T).reshape(n, N_HEADS, HEAD_DIM)
        src = edge_index[0]
        dst = edge_index[1]
        q_i = q[dst]
        k_j = k[src]
        v_j = v[src]
        w = w_ij.reshape(-1, N_HEADS, HEAD_DIM)
        alpha = jnp.sum(q_i * w * k_j, axis=-1) / jnp.sqrt(jnp.float32(HEAD_DIM))
        alpha = alpha * cutoff
        msgs = alpha[..., None] * v_j
        out = jax.ops.segment_sum(msgs, dst, num_segments=n)
        return out.reshape(n, HIDDEN)
    edge_index = jnp.stack([src, dst])
    x = _layernorm(x + _L0_gnn_ref(x, edge_index, edge_attr_16, L0_gnn_W_lin, L0_gnn_W_edge, L0_gnn_att_src, L0_gnn_att_dst, L0_gnn_att_edge, L0_gnn_bias, L0_gnn_ln_gamma, L0_gnn_ln_beta), axis=-1)
    x = _layernorm(x + _L1_gnn_ref(x, edge_attr_128, edge_index, edge_weight1, L1_gnn_Wq, L1_gnn_Wk, L1_gnn_Wv), axis=-1)
    return x

_drawn_inputs = setup_inputs


def setup_inputs(seed=0):
    import zlib

    import numpy as np

    out = dict(_drawn_inputs(seed))
    spreads = {'L0_gnn_bias': (0.0, 0.1), 'L0_gnn_ln_gamma': (1.0, 0.2), 'L0_gnn_ln_beta': (0.0, 0.1)}
    factors = {}
    for name, (base, spread) in spreads.items():
        noise = np.random.default_rng([zlib.crc32(name.encode()), seed]).standard_normal(out[name].shape)
        drawn = base * np.exp(spread * noise) if base else spread * noise
        out[name] = jnp.asarray(drawn.astype(out[name].dtype))
    for name, factor in factors.items():
        out[name] = (out[name] * factor).astype(out[name].dtype)
    return out
```

```python
import numpy as np
import concourse.bass as bass
from concourse import mybir

F32 = mybir.dt.float32
BF16 = mybir.dt.bfloat16
I32 = mybir.dt.int32
ALU = mybir.AluOpType
ACT = mybir.ActivationFunctionType
AX = mybir.AxisListType

P = 128
NODES, FEAT = 6250, 128
EDGES = 206250
HEADS0, HEADS1 = 4, 8
EDGE_DIM = 16
GROUP = 8
CHUNK_GROUPS = 12
CHUNK_TILES = GROUP * CHUNK_GROUPS
RUNS = P // HEADS0
RUN = CHUNK_TILES * P // RUNS
RUN_TILES = RUN // P
TILES = -(-EDGES // P)
CHUNKS = -(-TILES // CHUNK_TILES)
TILES0 = CHUNKS * CHUNK_TILES
GROUPS0 = TILES0 // GROUP
GROUPS1 = GROUPS0
GATHERED1 = -(-TILES // GROUP)
LAST_TILES = TILES - (CHUNKS - 1) * CHUNK_TILES
NODE_BLOCKS = -(-(NODES + P) // P)
NODE_ROWS = NODE_BLOCKS * P
XROW = FEAT + HEADS0
BATCH = 5
BATCHES = NODE_BLOCKS // BATCH
LN_EPS = 1e-5
SLOPE = 0.2
NEG = -1e30
assert GROUP * EDGE_DIM == P and CHUNKS % 2 == 1 and GROUPS1 % 4 == 0 and GROUPS1 - 4 < GATHERED1 and BATCHES % 2 == 0 and RUN_TILES * RUNS == CHUNK_TILES


def counter(eng, name):
    reg = eng.alloc_register(name)
    eng.reg_mov(reg, 0)
    return reg


def window_starts(eng, regs, base_row, first_group, pass_no):
    eng.reg_load(regs, base_row[0:1, bass.DynSlice(first_group, len(regs))])
    out = []
    for reg in regs:
        eng.reg_add(reg, reg, pass_no * P)
        eng.reg_alu(reg, reg, NODES, op=ALU.min)
        out.append(eng.snap(reg, min_val=0, max_val=NODES))
    return out


def wait_here(eng, sem, value, gate):
    eng.wait_ge(sem, value)
    eng.sem_inc(gate, 1)


def capped(eng, reg, value, most):
    eng.reg_mov(reg, value)
    eng.reg_alu(reg, reg, most, op=ALU.min)
    return reg


def program(nc, xT, xpad, src_idx0, src_idx1, dst_tile, dst_row, dst_runs, base_rep, last_rep, base_row,
            ea_turned, ea, ew, w_linT, w_lin, att, w_edge, att_edge, wqkvT, rows, ident, iota, node_of, own_tile, sel, sel4,
            out):
    S = nc.alloc_semaphore

    def sb(name, shape, dt=F32):
        return nc.alloc_sbuf_tensor(name, shape, dt).ap()

    x_table = nc.dram_tensor("x_table", [NODE_ROWS, XROW], F32, kind="Internal").ap()
    ai_table = nc.dram_tensor("ai_table", [NODE_ROWS, 3 * HEADS0], BF16, kind="Internal").ap()
    q_table = nc.dram_tensor("q_table", [NODE_ROWS, FEAT], F32, kind="Internal").ap()
    kv_table = nc.dram_tensor("kv_table", [NODE_ROWS, 2 * FEAT], F32, kind="Internal").ap()

    ident_sb = sb("ident_sb", [P, P])
    iota_sb = sb("iota_sb", [P, P])
    iota_pass = sb("iota_pass", [P, P])
    sel_sb = sb("sel_sb", [P, P])
    sel4_sb = sb("sel4_sb", [P, HEADS0])
    drel = sb("drel", [P, TILES0])
    base_sb = sb("base_sb", [1, GROUPS0], I32)
    passes_sb = sb("passes_sb", [P, 1], I32)
    sumT = sb("sumT", [P, NODE_ROWS])
    denT = sb("denT", [HEADS0, NODE_ROWS])
    rhs0 = sb("rhs0", [P, FEAT + 2 * HEADS0])
    we_att = sb("we_att", [P, GROUP * HEADS0])
    base_f = sb("base_f", [P, GROUPS0])
    node_col = sb("node_col", [P, 1])
    node_pass = sb("node_pass", [P, 1])
    ring = sb("ring", [P, 2 * CHUNK_TILES * XROW])
    work = sb("work", [P, 5 * GROUP * P])

    psum = nc.alloc_psum_tensor("psum", [P, 8 * 512], F32).ap()
    bank = [psum[:, i * 512:(i + 1) * 512] for i in range(4)]
    wide = [psum[:, (4 + 2 * i) * 512:(6 + 2 * i) * 512] for i in range(2)]

    dst_i = ring[:, 0:TILES0].bitcast(I32)
    base_i = ring[:, TILES0:TILES0 + GROUPS0].bitcast(I32)
    last_i = ring[:, TILES0 + GROUPS0:TILES0 + 2 * GROUPS0].bitcast(I32)
    span_i = ring[:, TILES0 + 2 * GROUPS0:TILES0 + 3 * GROUPS0].bitcast(I32)
    at = TILES0 + 3 * GROUPS0
    att_sb = ring[:, at:at + 2 * HEADS0]
    w_lin_sb = ring[:, at + 16:at + 16 + FEAT]
    w_edge_sb = ring[:, at + 160:at + 160 + P]
    att_edge_sb = ring[:, at + 288:at + 288 + HEADS0]
    own_tile_sb = ring[:, at + 292:at + 292 + GROUP * HEADS0]
    at += 384
    xT_slot = [ring[:, at + i * 2 * P:at + (i + 1) * 2 * P] for i in range(2)]
    at += 4 * P
    W0 = FEAT + 2 * HEADS0
    row_slot = [ring[:, at + i * 2 * W0:at + (i + 1) * 2 * W0].rearrange("p (b w) -> p b w", b=2)
                for i in range(2)]
    at += 4 * W0
    AI = NODE_BLOCKS * HEADS0
    ai_all = ring[:, at:at + AI]
    ai_rest = ring[:, at + AI:at + 2 * AI]
    ai_parts = ring[:, at + 2 * AI:at + 4 * AI].bitcast(BF16)[:, 0:3 * AI].rearrange("p (b s h) -> p b s h", s=3, h=HEADS0)
    ai_made = S("ai_made")
    ai_split = S("ai_split")
    ai_out = S("ai_out")
    consts_in = S("consts_in")
    ints_in = S("ints_in")
    weights_in = S("weights_in")
    folded = S("folded")
    folded_sb = S("folded_sb")
    xT_in = [S(f"xT_in{i}") for i in range(2)]
    rows_made = S("rows_made")
    rows_copied = S("rows_copied")
    rows_out = [S(f"rows_out{i}") for i in range(2)]
    PAIRS = NODE_BLOCKS // 2

    with nc.Block() as block:
        @block.sync
        def _(sp):
            for to, of in ((w_lin_sb, w_lin), (att_sb, att), (w_edge_sb, w_edge), (att_edge_sb, att_edge), (own_tile_sb, own_tile),
                           (rhs0[:, 0:FEAT], w_linT)):
                sp.dma_start(to, of).then_inc(weights_in, 16)
            with sp.Fori(0, PAIRS // 2) as i:
                for u in range(2):
                    sp.wait_ge(rows_made, 2 * i + u + 1)
                    sp.dma_start(xT_slot[u], xT[:, bass.DynSlice((2 * i + u) * 2 * P, 2 * P)]).then_inc(xT_in[u], 16)
            sp.wait_ge(rows_made, PAIRS)
            sp.dma_start(xT_slot[0], xT[:, (PAIRS - 1) * 2 * P:]).then_inc(xT_in[0], 16)
            sp.wait_ge(ai_split, 1)
            sp.dma_start(ai_table.rearrange("(b p) w -> p b w", p=P), ai_parts.rearrange("p b s h -> p b (s h)"))\
              .then_inc(ai_out, 16)
            sp.wait_ge(ai_out, 16)

        @block.gpsimd
        def _(pool):
            for to, of in ((ident_sb, ident), (iota_sb, iota), (sel_sb, sel), (sel4_sb, sel4), (node_col, node_of)):
                pool.dma_start(to, of).then_inc(consts_in, 16)
            for to, of in ((dst_i, dst_tile), (base_i, base_rep), (last_i, last_rep), (base_sb, base_row)):
                pool.dma_start(to, of).then_inc(ints_in, 16)
            pool.wait_ge(consts_in, 80)

        @block.tensor
        def _(pe):
            pe.wait_ge(weights_in, 96)
            pe.sem_inc(rows_made, 2)
            pe.matmul(bank[0][:, 0:2 * HEADS0], w_lin_sb, att_sb, start=True, stop=True)
            pe.matmul(bank[1][:, 0:HEADS0], w_edge_sb, att_edge_sb, start=True, stop=True).then_inc(folded, 1)
            pe.wait_ge(folded_sb, 2)

            def pair(u, n):
                for b in range(2):
                    last = pe.matmul(bank[2 + u][:, b * W0:(b + 1) * W0], xT_slot[u][:, b * P:(b + 1) * P],
                                     rhs0, start=True, stop=True)
                last.then_inc(rows_made, 1)

            with pe.Fori(0, PAIRS // 2) as i:
                for u in range(2):
                    pe.wait_ge(xT_in[u], 16 * (i + 1))
                    pe.wait_ge(rows_copied, 2 * i + u + 1)
                    pair(u, 2 * i + u)
            pe.wait_ge(xT_in[0], 16 * (PAIRS // 2 + 1))
            pe.wait_ge(rows_copied, PAIRS)
            pair(0, PAIRS - 1)

        @block.vector
        def _(dve):
            dve.sem_inc(rows_copied, 2)
            dve.wait_ge(weights_in, 96)
            dve.wait_ge(folded, 1)
            dve.tensor_copy(rhs0[:, FEAT:W0], bank[0][:, 0:2 * HEADS0]).then_inc(folded_sb, 1)
            dve.tensor_tensor(out=we_att.rearrange("p (t h) -> p t h", h=HEADS0),
                              in0=bank[1][:, 0:HEADS0].unsqueeze(1).to_broadcast([P, GROUP, HEADS0]),
                              in1=own_tile_sb.rearrange("p (t h) -> p t h", h=HEADS0), op=ALU.mult)\
               .then_inc(folded_sb, 1)
            dve.memset(sumT, 0.0)
            dve.memset(denT, 0.0)
            dve.wait_ge(ints_in, 64)
            dve.tensor_copy(base_f, base_i)
            dve.tensor_tensor(out=drel.rearrange("p (g t) -> p g t", t=GROUP),
                              in0=dst_i.rearrange("p (g t) -> p g t", t=GROUP),
                              in1=base_i.unsqueeze(2).to_broadcast([P, GROUPS0, GROUP]), op=ALU.subtract)
            dve.tensor_tensor(out=span_i, in0=last_i, in1=base_i, op=ALU.subtract)
            dve.drain()
            dve.tensor_reduce(out=passes_sb, in_=span_i, axis=AX.X, op=ALU.max)
            dve.drain()
            dve.tensor_scalar(passes_sb, passes_sb, 7, None, ALU.arith_shift_right)
            dve.drain()
            dve.tensor_scalar(passes_sb, passes_sb, 1, None, ALU.add)
            dve.wait_ge(ai_made, PAIRS)
            per_block = lambda t: t.rearrange("p (b h) -> p b h", h=HEADS0)
            dve.tensor_copy(ai_parts[:, :, 0, :], per_block(ai_all))
            for part in range(1, 3):
                dve.drain()
                dve.tensor_tensor(out=per_block(ai_rest if part == 1 else ai_all),
                                  in0=per_block(ai_all if part == 1 else ai_rest),
                                  in1=ai_parts[:, :, part - 1, :], op=ALU.subtract)
                dve.drain()
                last = dve.tensor_copy(ai_parts[:, :, part, :], per_block(ai_rest if part == 1 else ai_all))
            last.then_inc(ai_split, 1)

        @block.scalar
        def _(act):
            def copy_out(u, b0, pair_cols):
                made = bank[2 + u][:, 0:2 * W0].rearrange("p (b w) -> p b w", b=2)
                act.activation(ai_all[:, pair_cols].rearrange("p (b h) -> p b h", b=2), made[:, :, XROW:W0], ACT.Copy)\
                   .then_inc(ai_made, 1)
                act.activation(row_slot[u][:, :, 0:XROW], made[:, :, 0:XROW], ACT.Copy).then_inc(rows_copied, 1)
                act.drain()
                act.dma_start(x_table[b0, :].rearrange("(b p) w -> p b w", p=P), row_slot[u][:, :, 0:XROW])\
                   .then_inc(rows_out[u], 16)

            def pair_of(u, n, k2):
                act.wait_ge(rows_made, n + 3)
                if k2 is not None:
                    act.wait_ge(rows_out[u], 16 * k2)
                copy_out(u, bass.DynSlice(n * 2 * P, 2 * P), bass.DynSlice(n * 2 * HEADS0, 2 * HEADS0))

            for u in range(2):
                pair_of(u, u, None)
            with act.Fori(1, PAIRS // 2) as i:
                for u in range(2):
                    pair_of(u, 2 * i + u, i)
            pair_of(0, PAIRS - 1, PAIRS // 2)
            act.wait_ge(rows_out[0], 16 * (PAIRS // 2 + 1))
            act.wait_ge(rows_out[1], 16 * (PAIRS // 2))

    shared = dict(
        x_table=x_table, ai_table=ai_table, q_table=q_table, kv_table=kv_table, xpad=xpad,
        src_idx0=src_idx0, src_idx1=src_idx1, dst_row=dst_row, dst_runs=dst_runs, ea_turned=ea_turned,
        ea=ea, ew=ew, wqkvT=wqkvT, rows=rows, out=out, ident_sb=ident_sb, iota_sb=iota_sb,
        iota_pass=iota_pass, node_col=node_col, node_pass=node_pass, sel_sb=sel_sb, sel4_sb=sel4_sb,
        drel=drel, base_f=base_f, base_sb=base_sb, passes_sb=passes_sb, sumT=sumT, denT=denT,
        we_att=we_att, ring=ring, work=work, psum=psum, bank=bank, wide=wide)
    layer0(nc, S, sb, shared)
    between(nc, S, sb, shared)
    layer1(nc, S, sb, shared)
    final(nc, S, sb, shared)


def layer0(nc, S, sb, shared):
    k = shared
    GP = GROUP * P
    onehot = [k["work"][:, u * GP:(u + 1) * GP].rearrange("p (t n) -> p t n", t=GROUP) for u in range(2)]
    message = [k["work"][:, (2 + u) * GP:(3 + u) * GP].rearrange("p (t f) -> p t f", t=GROUP) for u in range(2)]
    onehotT = [k["work"][:, 4 * GP + u * GP // 2:4 * GP + (u + 1) * GP // 2].bitcast(BF16) for u in range(2)]
    dst_all = [sb(f"dst_all{i}", [P, GP], I32) for i in range(2)]
    ea_pair = [sb(f"ea_pair{i}", [P, 2, P]) for i in range(2)]
    idx = [sb(f"idx{i}", [P, CHUNK_TILES], I32) for i in range(2)]
    runs_dst = sb("runs_dst", [P, RUN + 2], I32)
    ai_win = [sb(f"ai_win{i}", [P, 3 * HEADS0], BF16) for i in range(2)]
    zeros = sb("zeros", [P, CHUNK_TILES * HEADS0], BF16)
    score = sb("score", [P, HEADS0, CHUNK_TILES])
    ex = sb("ex", [P, HEADS0, CHUNK_TILES])
    ex_group = [sb(f"ex_group{i}", [P, GROUP, HEADS0]) for i in range(2)]
    edge_change = sb("edge_change", [P, RUN + 1])
    ahead = sb("ahead", [P, RUN])
    back = sb("back", [P, RUN])
    cols = sb("cols", [P, 8])
    rowbuf = sb("rowbuf", [1, 5 * P])
    carry = sb("carry", [1, HEADS0])

    x_rows = k["ring"].rearrange("p (t w) -> p t w", w=XROW)
    scores_ps = k["bank"][0][:, 0:CHUNK_TILES * HEADS0]
    runs_ps = k["bank"][1][:, 0:RUN]
    small_ps = k["bank"][2]
    den_ps = [k["bank"][3 - u][0:HEADS0, 0:P] for u in range(2)]
    sum_ps = [k["wide"][1][:, u * 512:u * 512 + P] for u in range(2)]

    idx_in = [S(f"idx_in{i}") for i in range(2)]
    gathered = [S(f"gathered{i}") for i in range(2)]
    chunk_ready = S("chunk_ready")
    rows_released = S("rows_released")
    ea_in = [S(f"ea_in{i}") for i in range(2)]
    ea_used = S("ea_used")
    ai_in = [S(f"ai_in{i}") for i in range(2)]
    dst_in = [S(f"dst_in{i}") for i in range(2)]
    dst_used = S("dst_used")
    onehotT_made = S("onehotT_made")
    scores_added = S("scores_added")
    runs_in = S("runs_in")
    runs_used = S("runs_used")
    msg_made = S("msg_made")
    summed = S("summed")
    scores_summed = S("scores_summed")
    zeros_set = S("zeros_set")
    dve_to_pe = S("dve_to_pe")
    pe_to_dve = S("pe_to_dve")
    shifted = S("shifted")
    exp_done = S("exp_done")
    exT_done = S("exT_done")
    ex_copied = S("ex_copied")
    ex_free = S("ex_free")
    pe_gate = S("pe_gate")
    pool_gate = S("pool_gate")
    dve_gate = S("dve_gate")
    HALF = CHUNK_GROUPS // 2
    STEPS = 5
    run_ends = [ahead[:, RUN - 1:RUN], cols[:, 0:1], cols[:, 1:2]]

    with nc.Block() as block:
        @block.sync
        def _(sp):
            passes = sp.value_load(k["passes_sb"][0:1, 0:1], min_val=1, max_val=NODE_BLOCKS)
            visit = counter(sp, "sp_visit0")
            regs = [sp.alloc_register(f"sp_base0{u}") for u in range(2)]
            with sp.Fori(0, CHUNKS) as s:
                sp.wait_ge(runs_used, s + 1)
                sp.dma_start(runs_dst, k["dst_runs"][bass.DynSlice(s, 1), :, :].rearrange("o p n -> (o p) n"))\
                  .then_inc(runs_in, 16)
                with sp.Fori(0, HALF // 2) as g:
                    for u in range(2):
                        n = s * HALF + 2 * g + u
                        sp.wait_ge(ea_used, n + 1)
                        sp.dma_start(ea_pair[u], k["ea_turned"][bass.DynSlice(2 * n, 2), :, :].rearrange("g p e -> p g e"))\
                          .then_inc(ea_in[u], 16)
                with sp.Fori(0, passes) as r:
                    with sp.Fori(0, HALF) as g:
                        v = sp.snap(visit)
                        first_group = s * CHUNK_GROUPS + 2 * g
                        starts = window_starts(sp, regs, k["base_sb"], first_group, r)
                        for u in range(2):
                            sp.wait_ge(dst_used, 2 * v + u + 1)
                            sp.dma_start(dst_all[u], k["dst_row"][0:1, bass.DynSlice((first_group + u) * GP, GP)]
                                         .to_broadcast([P, GP])).then_inc(dst_in[u], 16)
                            sp.wait_ge(scores_added, 2 * v + u + 1)
                            sp.dma_start(ai_win[u], k["ai_table"][bass.DynSlice(starts[u], P), :]).then_inc(ai_in[u], 16)
                        sp.reg_add(visit, visit, 1)

        @block.gpsimd
        def _(pool):
            ALL = 16 * CHUNK_TILES

            def chunk(h, nth, s, tiles, before, following):
                wait_here(pool, idx_in[h], 16 * (nth + 1), pool_gate)
                wait_here(pool, rows_released, s + 1, pool_gate)
                for t in range(tiles):
                    pool.indirect_dma_start(x_rows[:, h * CHUNK_TILES + t, :], None, k["x_table"],
                                            bass.IndirectOffsetOnAxis(idx[h][:, t:t + 1], 0))\
                        .then_inc(gathered[h], 16)
                    if t == 4:
                        if before is not None:
                            pool.wait_ge(gathered[1 - h], before)
                            pool.sem_inc(chunk_ready, 1)
                        if following is not None:
                            pool.dma_start(idx[1 - h], k["src_idx0"][bass.DynSlice(following, 1), :, :]
                                           .rearrange("o p n -> (o p) n")).then_inc(idx_in[1 - h], 16)

            pool.dma_start(idx[0], k["src_idx0"][0, :, :]).then_inc(idx_in[0], 16)
            chunk(0, 0, 0, CHUNK_TILES, None, 1)
            PAIRS = CHUNKS // 2 - 1
            with pool.Fori(0, PAIRS) as i:
                chunk(1, i, 2 * i + 1, CHUNK_TILES, ALL * (i + 1), 2 * i + 2)
                chunk(0, i + 1, 2 * i + 2, CHUNK_TILES, ALL * (i + 1), 2 * i + 3)
            chunk(1, PAIRS, CHUNKS - 2, CHUNK_TILES, ALL * (PAIRS + 1), CHUNKS - 1)
            chunk(0, PAIRS + 1, CHUNKS - 1, LAST_TILES, ALL * (PAIRS + 1), None)
            pool.wait_ge(gathered[0], ALL * (PAIRS + 1) + 16 * LAST_TILES)
            pool.sem_inc(chunk_ready, 1)

        @block.tensor
        def _(pe):
            passes = pe.value_load(k["passes_sb"][0:1, 0:1], min_val=1, max_val=NODE_BLOCKS)
            d_visit = counter(pe, "pe_d_visit0")
            c_visit = counter(pe, "pe_c_visit0")
            pe.wait_ge(zeros_set, 1)
            with pe.Fori(0, CHUNKS) as s:
                pe.wait_ge(dve_to_pe, STEPS * s + 1)
                pe.matmul(scores_ps, zeros[:, 0:P], zeros, start=True, stop=False)
                for g in range(CHUNK_GROUPS):
                    if g % 2 == 0:
                        pe.wait_ge(ea_in[g // 2 % 2], 16 * (s * (HALF // 2) + g // 4 + 1))
                    last = pe.matmul(scores_ps[:, g * GROUP * HEADS0:(g + 1) * GROUP * HEADS0],
                                     ea_pair[g // 2 % 2][:, g % 2, :], k["we_att"], start=False, stop=False)
                    if g % 2 == 1:
                        last.then_inc(ea_used, 1)
                with pe.Fori(0, passes) as r:
                    d = pe.snap(d_visit)
                    for g in range(CHUNK_GROUPS):
                        pe.wait_ge(onehotT_made, d * CHUNK_GROUPS + g + 1)
                        pe.wait_ge(ai_in[g % 2], 16 * (d * HALF + g // 2 + 1))
                        for t in range(GROUP):
                            at = (g * GROUP + t) * HEADS0
                            for part in range(3):
                                last = pe.matmul(scores_ps[:, at:at + HEADS0], onehotT[g % 2][:, t * P:(t + 1) * P],
                                                 ai_win[g % 2][:, part * HEADS0:(part + 1) * HEADS0],
                                                 start=False, stop=False)
                        last.then_inc(scores_added, 1)
                    pe.reg_add(d_visit, d_visit, 1)
                pe.matmul(scores_ps, zeros[:, 0:P], zeros, start=False, stop=True).then_inc(scores_summed, 1)

                pe.wait_ge(dve_to_pe, STEPS * s + 2)
                for t in range(RUN_TILES):
                    last = pe.transpose(runs_ps[:, t * P:(t + 1) * P],
                                        score.rearrange("p h (c t) -> p (h c) t", t=RUN_TILES)[:, :, t], k["ident_sb"])
                last.then_inc(pe_to_dve, 1)
                pe.wait_ge(dve_to_pe, STEPS * s + 3)
                for c in range(3):
                    last = pe.transpose(small_ps[0:1, c * P:(c + 1) * P], run_ends[c], k["ident_sb"])
                last.then_inc(pe_to_dve, 1)
                wait_here(pe, dve_to_pe, STEPS * s + 4, pe_gate)
                pe.transpose(small_ps[:, 400:401], rowbuf[0:1, 3 * P:4 * P], k["ident_sb"][0:1, 0:1]).then_inc(pe_to_dve, 1)
                pe.wait_ge(dve_to_pe, STEPS * s + 5)
                pe.transpose(small_ps[0:1, 0:P], back[:, 0:1], k["ident_sb"]).then_inc(pe_to_dve, 1)
                wait_here(pe, dve_to_pe, STEPS * s + 6, pe_gate)
                pe.transpose(small_ps[:, 402:403], rowbuf[0:1, 3 * P:4 * P], k["ident_sb"][0:1, 0:1]).then_inc(pe_to_dve, 1)
                pe.wait_ge(exp_done, s + 1)
                for t in range(RUN_TILES):
                    pe.transpose(runs_ps[:, t * P:(t + 1) * P], ahead[:, t * P:(t + 1) * P], k["ident_sb"])
                pe.matmul(small_ps[:, 404:405], k["sel_sb"], cols[:, 5:6], start=True, stop=True)
                pe.matmul(small_ps[0:HEADS0, 406:407], k["sel4_sb"], cols[:, 5:6], start=True, stop=True)\
                  .then_inc(exT_done, 1)

                with pe.Fori(0, passes) as r:
                    with pe.Fori(0, HALF) as g:
                        c = pe.snap(c_visit)
                        for u in range(2):
                            pe.wait_ge(msg_made, 2 * c + u + 1)
                            for t in range(GROUP):
                                pe.matmul(sum_ps[u], message[u][:, t, :], onehot[u][:, t, :],
                                          start=t == 0, stop=t == GROUP - 1)
                            for t in range(GROUP):
                                last = pe.matmul(den_ps[u], ex_group[u][:, t, :], onehot[u][:, t, :],
                                                 start=t == 0, stop=t == GROUP - 1)
                            last.then_inc(summed, 1)
                        pe.reg_add(c_visit, c_visit, 1)

        @block.scalar
        def _(act):
            with act.Fori(0, CHUNKS) as s:
                act.wait_ge(shifted, s + 1)
                act.activation(ahead, back, ACT.Exp)
                act.activation(cols[:, 5:6], cols[:, 4:5], ACT.Exp).then_inc(exp_done, 1)
                act.wait_ge(exT_done, s + 1)
                act.wait_ge(ex_free, s + 1)
                act.activation(ex.rearrange("p h (c t) -> p (h c) t", t=RUN_TILES),
                               runs_ps.rearrange("p (t q) -> p q t", t=RUN_TILES), ACT.Copy).then_inc(ex_copied, 1)

        @block.vector
        def _(dve):
            passes = dve.value_load(k["passes_sb"][0:1, 0:1], min_val=1, max_val=NODE_BLOCKS)
            d_visit = counter(dve, "dve_d_visit0")
            c_visit = counter(dve, "dve_c_visit0")
            regs = [dve.alloc_register(f"dve_base0{u}") for u in range(2)]
            before = dve.alloc_register("dve_base_before0")
            dve.memset(zeros, 0.0).then_inc(zeros_set, 1)
            dve.memset(carry, NEG)
            dve.memset(cols, 0.0)
            for credit, n in ((rows_released, 2), (ea_used, 2), (dst_used, 2), (scores_added, 2), (runs_used, 1),
                              (summed, 1), (dve_to_pe, 1), (ex_free, 1)):
                dve.sem_inc(credit, n)

            def next_pass(numbers):
                dve.drain()
                dve.tensor_scalar(numbers, numbers, float(P), None, ALU.add)
                dve.drain()

            with dve.Fori(0, CHUNKS) as s:
                dve.drain()
                dve.tensor_copy(k["node_pass"], k["node_col"])
                dve.drain()
                with dve.Fori(0, passes) as r:
                    with dve.Fori(0, HALF) as g:
                        v = dve.snap(d_visit)
                        for u in range(2):
                            dve.wait_ge(dst_in[u], 16 * (v + 1))
                            dve.wait_ge(scores_added, 2 * v + u + 1)
                            dve.tensor_scalar(onehotT[u], dst_all[u],
                                              k["base_f"][:, bass.DynSlice(s * CHUNK_GROUPS + 2 * g + u, 1)],
                                              k["node_pass"], ALU.subtract, ALU.is_equal).then_inc(onehotT_made, 1)
                            dve.drain().then_inc(dst_used, 1)
                        dve.reg_add(d_visit, d_visit, 1)
                    next_pass(k["node_pass"])

                dve.wait_ge(runs_in, 16 * (s + 1))
                dve.tensor_tensor(out=edge_change, in0=runs_dst[:, 0:RUN + 1], in1=runs_dst[:, 1:RUN + 2],
                                  op=ALU.not_equal).then_inc(runs_used, 1)
                dve.tensor_copy(k["iota_pass"], k["iota_sb"])
                dve.drain()
                dve.tensor_scalar(edge_change, edge_change, NEG, None, ALU.mult)
                dve.drain()
                dve.tensor_reduce(out=cols[:, 0:1], in_=edge_change[:, 0:RUN], axis=AX.X, op=ALU.min)
                dve.tensor_reduce(out=cols[:, 1:2], in_=edge_change[:, 1:RUN + 1], axis=AX.X, op=ALU.min)

                dve.wait_ge(scores_summed, s + 1)
                dve.wait_ge(chunk_ready, s + 1)
                dve.tensor_tensor(out=score.rearrange("p h t -> p t h"),
                                  in0=scores_ps.rearrange("p (t h) -> p t h", h=HEADS0),
                                  in1=x_rows[:, bass.DynSlice((s % 2) * CHUNK_TILES, CHUNK_TILES), FEAT:XROW],
                                  op=ALU.add)
                dve.drain()
                flat = score.rearrange("p h t -> p (h t)")
                dve.scalar_tensor_tensor(out=flat, in0=flat, scalar=SLOPE, in1=flat, op0=ALU.mult, op1=ALU.max)\
                   .then_inc(dve_to_pe, 1)

                dve.wait_ge(pe_to_dve, 5 * s + 1)
                dve.tensor_tensor_scan(ahead, edge_change[:, 0:RUN], runs_ps, NEG, ALU.add, ALU.max).then_inc(dve_to_pe, 1)
                ends, pen, pen_back, into, over = (rowbuf[0:1, c * P:(c + 1) * P] for c in range(5))
                by_head = lambda row: row.rearrange("p (h c) -> p h c", h=HEADS0)
                carry3 = carry.unsqueeze(2)
                dve.wait_ge(pe_to_dve, 5 * s + 2)
                dve.tensor_copy(rowbuf[0:1, 0:3 * P], small_ps[0:1, 0:3 * P])
                dve.drain()
                dve.tensor_tensor(out=by_head(over)[:, :, 0:1], in0=by_head(pen)[:, :, 0:1], in1=carry3, op=ALU.add)
                dve.drain()
                dve.tensor_tensor(out=by_head(ends)[:, :, 0:1], in0=by_head(ends)[:, :, 0:1],
                                  in1=by_head(over)[:, :, 0:1], op=ALU.max)
                dve.memset(by_head(pen)[:, :, 0:1], 2 * NEG)
                dve.memset(by_head(pen_back)[:, :, RUNS - 1:RUNS], 2 * NEG)
                dve.drain()
                dve.tensor_tensor_scan(over, pen, ends, 0.0, ALU.add, ALU.max)
                dve.drain()
                dve.tensor_copy(by_head(into)[:, :, 1:RUNS], by_head(over)[:, :, 0:RUNS - 1])
                dve.tensor_copy(by_head(into)[:, :, 0:1], carry3).then_inc(dve_to_pe, 1)
                dve.drain()
                dve.tensor_copy(carry3, by_head(over)[:, :, RUNS - 1:RUNS])
                dve.wait_ge(pe_to_dve, 5 * s + 3)
                dve.tensor_copy(cols[:, 2:3], small_ps[:, 400:401])
                dve.drain()
                dve.tensor_tensor_scan(ahead, edge_change[:, 0:RUN], runs_ps, cols[:, 2:3], ALU.add, ALU.max)
                dve.drain()
                scan_back = (back[:, ::-1], edge_change[:, RUN:0:-1], ahead[:, ::-1])
                dve.tensor_tensor_scan(*scan_back, NEG, ALU.add, ALU.max).then_inc(dve_to_pe, 1)
                dve.wait_ge(pe_to_dve, 5 * s + 4)
                dve.tensor_copy(ends, small_ps[0:1, 0:P])
                dve.drain()
                dve.tensor_tensor_scan(over[:, ::-1], pen_back[:, ::-1], ends[:, ::-1], 0.0, ALU.add, ALU.max)
                dve.drain()
                dve.tensor_copy(by_head(into)[:, :, 0:RUNS - 1], by_head(over)[:, :, 1:RUNS])
                dve.memset(by_head(into)[:, :, RUNS - 1:RUNS], 2 * NEG).then_inc(dve_to_pe, 1)
                dve.wait_ge(pe_to_dve, 5 * s + 5)
                dve.tensor_copy(cols[:, 3:4], small_ps[:, 402:403])
                dve.drain()
                dve.tensor_tensor_scan(*scan_back, cols[:, 3:4], ALU.add, ALU.max)
                dve.drain()
                dve.tensor_tensor(out=cols[:, 4:5], in0=cols[:, 2:3], in1=back[:, 0:1], op=ALU.subtract)
                dve.drain()
                dve.tensor_scalar(cols[:, 4:5], cols[:, 4:5], 0.0, None, ALU.min)
                dve.tensor_tensor(out=back, in0=runs_ps, in1=back, op=ALU.subtract).then_inc(shifted, 1)

                dve.reg_load(regs[0], k["base_sb"][0:1, bass.DynSlice(s * CHUNK_GROUPS, 1)])
                first = dve.snap(regs[0], min_val=0, max_val=NODES)
                dve.wait_ge(exT_done, s + 1)
                column = k["sumT"][:, bass.DynSlice(first, 1)]
                dve.tensor_tensor(out=column, in0=column, in1=small_ps[:, 404:405], op=ALU.mult)
                column = k["denT"][:, bass.DynSlice(first, 1)]
                dve.tensor_tensor(out=column, in0=column, in1=small_ps[0:HEADS0, 406:407], op=ALU.mult)

                def make(u, first_tile, tile):
                    dve.tensor_tensor(out=onehot[u], in0=k["iota_pass"].unsqueeze(1).to_broadcast([P, GROUP, P]),
                                      in1=k["drel"][:, bass.DynSlice(first_tile, GROUP)].unsqueeze(2)
                                      .to_broadcast([P, GROUP, P]), op=ALU.is_equal)
                    dve.tensor_copy(ex_group[u], ex[:, :, bass.DynSlice(tile, GROUP)].rearrange("p h t -> p t h"))
                    dve.drain()
                    dve.tensor_tensor(
                        out=message[u].rearrange("p t (h f) -> p t h f", h=HEADS0),
                        in0=x_rows[:, bass.DynSlice((s % 2) * CHUNK_TILES + tile, GROUP), 0:FEAT]
                        .rearrange("p t (h f) -> p t h f", h=HEADS0),
                        in1=ex_group[u].unsqueeze(3).to_broadcast([P, GROUP, HEADS0, FEAT // HEADS0]),
                        op=ALU.mult).then_inc(msg_made, 1)

                def add(u, start, group):
                    dve.wait_ge(summed, group + 2)
                    for sums, part in ((k["sumT"], sum_ps[u]), (k["denT"], den_ps[u])):
                        window = sums[:, bass.DynSlice(start, P)]
                        dve.tensor_tensor(out=window, in0=window, in1=part, op=ALU.add)

                wait_here(dve, ex_copied, s + 1, dve_gate)
                with dve.Fori(0, passes) as r:
                    def pair(g, first):
                        v = dve.snap(c_visit)
                        tile = 2 * g * GROUP
                        starts = window_starts(dve, regs, k["base_sb"], s * CHUNK_GROUPS + 2 * g, r)
                        make(0, s * CHUNK_TILES + tile, tile)
                        if not first:
                            add(1, dve.snap(before, min_val=0, max_val=NODES), 2 * v - 1)
                        make(1, s * CHUNK_TILES + tile + GROUP, tile + GROUP)
                        dve.reg_mov(before, starts[1])
                        add(0, starts[0], 2 * v)
                        dve.reg_add(c_visit, c_visit, 1)

                    pair(0, True)
                    with dve.Fori(1, HALF) as g:
                        pair(g, False)
                    dve.drain()
                    add(1, dve.snap(before, min_val=0, max_val=NODES), 2 * dve.snap(c_visit) - 1)
                    next_pass(k["iota_pass"])
                dve.drain().then_inc(rows_released, 1)
                dve.drain().then_inc(ex_free, 1)


def between(nc, S, sb, shared):
    k = shared
    B = BATCH * FEAT
    cut = [0]

    def part(cols):
        cut[0] += cols
        return k["ring"][:, cut[0] - cols:cut[0]]

    rows_sb = part(3 * FEAT)
    bias, gamma, beta = (rows_sb[:, i * FEAT:(i + 1) * FEAT].unsqueeze(1).to_broadcast([P, BATCH, FEAT])
                         for i in range(3))
    w_sb = part(3 * FEAT)
    x_in = [part(B) for _ in range(2)]
    sT, y, low, x1s, x1T = (part(B) for _ in range(5))
    dT = part(B)[0:HEADS0, :]
    qkv = [part(3 * B).rearrange("p (b w) -> p b w", b=BATCH) for _ in range(2)]
    rden = part(BATCH * HEADS0)
    stats = part(6 * BATCH).rearrange("p (b w) -> p b w", b=BATCH)
    mv = part(2 * BATCH).rearrange("p (b w) -> p b w", b=BATCH)
    rstd = part(BATCH)
    half_neg = part(BATCH)
    assert cut[0] <= 2 * CHUNK_TILES * XROW - NODE_ROWS
    x1 = k["ring"][:, 2 * CHUNK_TILES * XROW - NODE_ROWS:]

    y3, low3, x1s3 = (t.rearrange("p (b f) -> p b f", b=BATCH) for t in (y, low, x1s))
    y_ps, dn_ps, x1T_ps = k["wide"][0][:, 0:B], k["bank"][2][:, 0:BATCH * HEADS0], k["wide"][1][:, 0:B]

    w_in = S("w_in")
    xb_in = [S(f"xb_in{i}") for i in range(2)]
    x_used = S("x_used")
    sums_copied = S("sums_copied")
    sums_turned = S("sums_turned")
    low_made = S("low_made")
    var_made = S("var_made")
    rstd_made = S("rstd_made")
    low_exp = S("low_exp")
    x1_made = S("x1_made")
    x1_turned = S("x1_turned")
    x1T_copied = S("x1T_copied")
    qkv_made = S("qkv_made")
    qkv_copied = S("qkv_copied")
    qkv_out = [S(f"qkv_out{i}") for i in range(2)]

    with nc.Block() as block:
        @block.sync
        def _(sp):
            regx = sp.alloc_register("sp_batch_ahead")
            sp.dma_start(rows_sb, k["rows"]).then_inc(w_in, 16)
            sp.dma_start(w_sb, k["wqkvT"]).then_inc(w_in, 16)
            for u in range(2):
                sp.dma_start(x_in[u].rearrange("p (b f) -> p b f", b=BATCH),
                             k["xpad"][u * BATCH * P:(u + 1) * BATCH * P, :].rearrange("(b p) f -> p b f", p=P))\
                  .then_inc(xb_in[u], 16)
            with sp.Fori(0, BATCHES // 2) as i:
                for u in range(2):
                    n = 2 * i + u
                    nodes = bass.DynSlice(n * BATCH * P, BATCH * P)
                    sp.wait_ge(qkv_copied, BATCH * (n + 1) + 1)
                    sp.dma_start(k["q_table"][nodes, :].rearrange("(b p) f -> p b f", p=P), qkv[u][:, :, 0:FEAT])\
                      .then_inc(qkv_out[u], 16)
                    sp.dma_start(k["kv_table"][nodes, :].rearrange("(b p) f -> p b f", p=P), qkv[u][:, :, FEAT:])\
                      .then_inc(qkv_out[u], 16)
                    ahead = sp.snap(capped(sp, regx, n + 2, BATCHES - 1), min_val=0, max_val=BATCHES - 1)
                    sp.wait_ge(x_used, n + 1)
                    sp.dma_start(x_in[u].rearrange("p (b f) -> p b f", b=BATCH),
                                 k["xpad"][bass.DynSlice(ahead * (BATCH * P), BATCH * P), :]
                                 .rearrange("(b p) f -> p b f", p=P)).then_inc(xb_in[u], 16)
            for u in range(2):
                sp.wait_ge(xb_in[u], 16 * (BATCHES // 2 + 1))
                sp.wait_ge(qkv_out[u], 32 * (BATCHES // 2))

        @block.gpsimd
        def _(pool):
            pool.memset(half_neg, -0.5)
            pool.drain()
            with pool.Fori(0, 2 * BATCHES) as i:
                pool.wait_ge(var_made, i + 1)
                pool.tensor_tensor(out=rstd, in0=rstd, in1=half_neg, op=ALU.pow).then_inc(rstd_made, 1)

        @block.tensor
        def _(pe):
            pe.wait_ge(w_in, 32)
            with pe.Fori(0, BATCHES) as n:
                pe.wait_ge(sums_copied, n + 1)
                for b in range(BATCH):
                    pe.transpose(y_ps[:, b * P:(b + 1) * P], sT[:, b * P:(b + 1) * P], k["ident_sb"])
                for b in range(BATCH):
                    last = pe.transpose(dn_ps[:, b * HEADS0:(b + 1) * HEADS0], dT[:, b * P:(b + 1) * P],
                                        k["ident_sb"][0:HEADS0, 0:HEADS0])
                last.then_inc(sums_turned, 1)
                pe.wait_ge(x1_made, n + 1)
                for b in range(BATCH):
                    last = pe.transpose(x1T_ps[:, b * P:(b + 1) * P], x1s[:, b * P:(b + 1) * P], k["ident_sb"])
                last.then_inc(x1_turned, 1)
                pe.wait_ge(x1T_copied, n + 1)
                for b in range(BATCH):
                    pe.wait_ge(qkv_copied, BATCH * n + max(b - 1, 0) + 1)
                    pe.matmul(k["bank"][b % 2][:, 0:3 * FEAT], x1T[:, b * P:(b + 1) * P], w_sb,
                              start=True, stop=True).then_inc(qkv_made, 1)

        @block.scalar
        def _(act):
            def batch(u, n, times_written):
                nodes = bass.DynSlice(n * B, B)
                act.activation(sT, k["sumT"][:, nodes], ACT.Copy)
                act.activation(dT, k["denT"][:, nodes], ACT.Copy).then_inc(sums_copied, 1)
                act.wait_ge(low_made, n + 1)
                act.activation(low, low, ACT.Exp).then_inc(low_exp, 1)
                act.wait_ge(x1_turned, n + 1)
                act.activation(x1T, x1T_ps, ACT.Copy).then_inc(x1T_copied, 1)
                act.activation(x1[:, nodes], x1s, ACT.Copy)
                if times_written is not None:
                    act.wait_ge(qkv_out[u], 32 * times_written)
                for b in range(BATCH):
                    act.wait_ge(qkv_made, BATCH * n + b + 1)
                    act.activation(qkv[u][:, b, :], k["bank"][b % 2][:, 0:3 * FEAT], ACT.Copy).then_inc(qkv_copied, 1)

            for u in range(2):
                batch(u, u, None)
            with act.Fori(1, BATCHES // 2) as i:
                for u in range(2):
                    batch(u, 2 * i + u, i)

        @block.vector
        def _(dve):
            dve.sem_inc(qkv_copied, 1)
            dve.wait_ge(w_in, 32)

            with dve.Fori(0, BATCHES // 2) as i:
                for u in range(2):
                    n = 2 * i + u
                    x3 = x_in[u].rearrange("p (b f) -> p b f", b=BATCH)
                    dve.wait_ge(sums_turned, n + 1)
                    dve.tensor_scalar(rden, dn_ps, 1e-16, None, ALU.add)
                    dve.drain()
                    dve.reciprocal(rden, rden)
                    dve.drain()
                    dve.tensor_tensor(out=y.rearrange("p (q f) -> p q f", f=FEAT // HEADS0),
                                      in0=y_ps.rearrange("p (q f) -> p q f", f=FEAT // HEADS0),
                                      in1=rden.unsqueeze(2).to_broadcast([P, BATCH * HEADS0, FEAT // HEADS0]),
                                      op=ALU.mult)
                    dve.drain()
                    dve.tensor_tensor(out=y3, in0=y3, in1=bias, op=ALU.add)
                    dve.drain()
                    dve.wait_ge(xb_in[u], 16 * (i + 1))
                    dve.tensor_tensor(out=y, in0=y, in1=x_in[u], op=ALU.add)
                    norm(dve, y3, y3, stats, mv, rstd, var_made, rstd_made, 2 * n)
                    dve.drain()
                    dve.tensor_tensor(out=y3, in0=y3, in1=gamma, op=ALU.mult)
                    dve.drain()
                    dve.tensor_tensor(out=y3, in0=y3, in1=beta, op=ALU.add)
                    dve.drain()
                    dve.tensor_scalar(low, y, 0.0, None, ALU.min).then_inc(low_made, 1)
                    dve.wait_ge(low_exp, n + 1)
                    dve.scalar_tensor_tensor(out=y, in0=y, scalar=0.0, in1=low, op0=ALU.max, op1=ALU.add)
                    dve.drain()
                    dve.scalar_tensor_tensor(out=y, in0=y, scalar=-1.0, in1=x_in[u], op0=ALU.add, op1=ALU.add)\
                       .then_inc(x_used, 1)
                    norm(dve, x1s3, y3, stats, mv, rstd, var_made, rstd_made, 2 * n + 1).then_inc(x1_made, 1)


def norm(dve, out, y, stats, mv, rstd, var_made, rstd_made, nth, out_free=None):
    dve.drain()
    for b in range(BATCH):
        dve.bn_stats(stats[:, b, :], y[:, b, :])
    dve.drain()
    for b in range(BATCH):
        dve.bn_aggr(mv[:, b, :], stats[:, b, :])
    dve.drain()
    dve.tensor_scalar(rstd, mv[:, :, 1], LN_EPS, None, ALU.add).then_inc(var_made, 1)
    dve.wait_ge(rstd_made, nth + 1)
    if out_free is not None:
        dve.wait_ge(*out_free)
    for b in range(BATCH):
        last = dve.tensor_scalar(out[:, b, :], y[:, b, :], mv[:, b, 0:1], rstd[:, b:b + 1], ALU.subtract, ALU.mult)
    return last


def layer1(nc, S, sb, shared):
    k = shared
    GP = GROUP * P
    SLOTS = 4
    cut = [0]

    def part(cols):
        cut[0] += cols
        return k["ring"][:, cut[0] - cols:cut[0]]

    tiles3 = lambda t: t.rearrange("p (t n) -> p t n", t=GROUP)
    kv = [tiles3(part(2 * GP)) for _ in range(SLOTS)]
    w = [tiles3(part(GP)) for _ in range(SLOTS)]
    q_win = [part(FEAT) for _ in range(SLOTS)]
    prod = tiles3(part(GP))
    message = [tiles3(part(GP)) for _ in range(2)]
    idx = [part(GROUP).bitcast(I32) for _ in range(SLOTS)]
    alpha = part(GROUP * HEADS1)
    edge_w = part(GROUPS1 * GROUP)
    assert cut[0] <= 2 * CHUNK_TILES * XROW - NODE_ROWS
    onehot = [tiles3(k["work"][:, u * GP:(u + 1) * GP]) for u in range(SLOTS)]
    onehotT = k["work"][:, 4 * GP:5 * GP]
    sum_ps = [k["bank"][u][:, 0:P] for u in range(2)]
    T_ps = k["wide"][0]
    q_ps = [k["psum"][:, 2 * 512:4 * 512], k["wide"][1]]

    edge_w_in = S("edge_w_in")
    idx_in = [S(f"idx1_in{i}") for i in range(SLOTS)]
    kv_in = [S(f"kv_in{i}") for i in range(SLOTS)]
    w_in = [S(f"w1_in{i}") for i in range(SLOTS)]
    q_in = [S(f"q_in{i}") for i in range(SLOTS)]
    kv_ready = S("kv_ready")
    onehot_made = S("onehot1_made")
    onehot_turned = S("onehot1_turned")
    onehotT_made = S("onehot1T_made")
    q_spread = S("q_spread")
    q_used = S("q_used")
    msg_made = S("msg1_made")
    summed = S("summed1")
    pool_gate = S("pool1_gate")
    ROUNDS = GROUPS1 // SLOTS

    def absolute(eng, round_reg):
        return eng.snap(round_reg) * SLOTS

    with nc.Block() as block:
        @block.sync
        def _(sp):
            passes = sp.value_load(k["passes_sb"][0:1, 0:1], min_val=1, max_val=NODE_BLOCKS)
            rounds = counter(sp, "sp_rounds1")
            regs = [sp.alloc_register(f"sp_base1{u}") for u in range(SLOTS)]
            sp.dma_start(edge_w, k["ew"]).then_inc(edge_w_in, 16)
            with sp.Fori(0, passes) as r:
                with sp.Fori(0, ROUNDS) as i:
                    n0 = absolute(sp, rounds)
                    starts = window_starts(sp, regs, k["base_sb"], SLOTS * i, r)
                    for j in range(SLOTS):
                        sp.wait_ge(msg_made, n0 + j + 1)
                        sp.dma_start(idx[j], k["src_idx1"][bass.DynSlice(SLOTS * i + j, 1), :, :]
                                     .rearrange("o p n -> (o p) n")).then_inc(idx_in[j], 16)
                        sp.dma_start(q_win[j], k["q_table"][bass.DynSlice(starts[j], P), :]).then_inc(q_in[j], 16)
                        sp.dma_start(w[j], k["ea"][bass.DynSlice((SLOTS * i + j) * GP, GP), :]
                                     .rearrange("(t p) f -> p t f", p=P)).then_inc(w_in[j], 16)
                    sp.reg_add(rounds, rounds, 1)

        @block.gpsimd
        def _(pool):
            passes = pool.value_load(k["passes_sb"][0:1, 0:1], min_val=1, max_val=NODE_BLOCKS)
            rounds = counter(pool, "pool_rounds1")
            full_rounds = counter(pool, "pool_full_rounds1")
            LAST_ROUND = GATHERED1 - (GROUPS1 - SLOTS)
            LAG = 3

            def one_round(groups, first):
                nth, nth_full = pool.snap(rounds), pool.snap(full_rounds)
                for j in range(groups):
                    wait_here(pool, msg_made, nth * SLOTS + j + 1, pool_gate)
                    wait_here(pool, idx_in[j], 16 * (nth + 1), pool_gate)
                    for t in range(GROUP):
                        pool.indirect_dma_start(kv[j][:, t, :], None, k["kv_table"],
                                                bass.IndirectOffsetOnAxis(idx[j][:, t:t + 1], 0))\
                            .then_inc(kv_in[j], 16)
                        if t == LAG and (j or not first):
                            arrived((j - 1) % SLOTS, nth_full if j == 0 else (nth if j <= LAST_ROUND else nth_full) + 1)
                pool.reg_add(rounds, rounds, 1)

            def arrived(j, times):
                wait_here(pool, kv_in[j], times * (16 * GROUP), pool_gate)
                pool.sem_inc(kv_ready, 1)

            with pool.Fori(0, passes) as r:
                one_round(SLOTS, True)
                pool.reg_add(full_rounds, full_rounds, 1)
                with pool.Fori(1, ROUNDS - 1) as i:
                    one_round(SLOTS, False)
                    pool.reg_add(full_rounds, full_rounds, 1)
                one_round(LAST_ROUND, False)
                arrived(LAST_ROUND - 1, pool.snap(rounds))
                pool.sem_inc(kv_ready, GROUPS1 - GATHERED1)

        @block.tensor
        def _(pe):
            passes = pe.value_load(k["passes_sb"][0:1, 0:1], min_val=1, max_val=NODE_BLOCKS)
            rounds = counter(pe, "pe_rounds1")

            def turn(n, j):
                pe.wait_ge(onehot_made, n + 1)
                for t in range(GROUP):
                    last = pe.transpose(T_ps[:, t * P:(t + 1) * P], onehot[j][:, t, :], k["ident_sb"])
                last.then_inc(onehot_turned, 1)

            def spread(n, j, nth):
                pe.wait_ge(onehotT_made, n + 1)
                pe.wait_ge(q_in[j], 16 * (nth + 1))
                pe.wait_ge(q_used, n + 1)
                for t in range(GROUP):
                    last = pe.matmul(q_ps[j % 2][:, t * P:(t + 1) * P], onehotT[:, t * P:(t + 1) * P], q_win[j],
                                     start=True, stop=True)
                last.then_inc(q_spread, 1)

            def sums(n, j):
                pe.wait_ge(msg_made, n + SLOTS + 1)
                for t in range(GROUP):
                    last = pe.matmul(sum_ps[j % 2], message[j % 2][:, t, :], onehot[j][:, t, :],
                                     start=t == 0, stop=t == GROUP - 1)
                last.then_inc(summed, 1)

            def one_round(last_round):
                nth = pe.snap(rounds)
                n0 = nth * SLOTS
                for j in range(SLOTS):
                    more = not last_round or j + 2 < SLOTS
                    if more:
                        turn(n0 + j + 2, (j + 2) % SLOTS)
                        spread(n0 + j + 2, (j + 2) % SLOTS, nth if j < 2 else nth + 1)
                    sums(n0 + j, j)
                pe.reg_add(rounds, rounds, 1)

            with pe.Fori(0, passes) as r:
                nth = pe.snap(rounds)
                for j in range(2):
                    turn(nth * SLOTS + j, j)
                    spread(nth * SLOTS + j, j, nth)
                with pe.Fori(0, ROUNDS - 1) as i:
                    one_round(False)
                one_round(True)

        @block.scalar
        def _(act):
            passes = act.value_load(k["passes_sb"][0:1, 0:1], min_val=1, max_val=NODE_BLOCKS)
            group = counter(act, "act_group1")
            with act.Fori(0, passes) as r:
                with act.Fori(0, GROUPS1) as i:
                    n = act.snap(group)
                    act.wait_ge(onehot_turned, n + 1)
                    act.wait_ge(q_spread, n + 1)
                    act.activation(onehotT, T_ps, ACT.Copy).then_inc(onehotT_made, 1)
                    act.reg_add(group, group, 1)

        @block.vector
        def _(dve):
            passes = dve.value_load(k["passes_sb"][0:1, 0:1], min_val=1, max_val=NODE_BLOCKS)
            rounds = counter(dve, "dve_rounds1")
            regs = [dve.alloc_register(f"dve_base1{u}") for u in range(SLOTS)]
            before = dve.alloc_register("dve_base_before1")
            for credit, n in ((q_spread, 1), (q_used, 2), (msg_made, SLOTS)):
                dve.sem_inc(credit, n)
            dve.memset(k["sumT"], 0.0)
            dve.tensor_copy(k["iota_pass"], k["iota_sb"])
            dve.drain()
            dve.wait_ge(edge_w_in, 16)

            def make_onehot(i, j):
                dve.tensor_tensor(out=onehot[j], in0=k["iota_pass"].unsqueeze(1).to_broadcast([P, GROUP, P]),
                                  in1=k["drel"][:, bass.DynSlice(i * GROUP, GROUP)].unsqueeze(2)
                                  .to_broadcast([P, GROUP, P]), op=ALU.is_equal).then_inc(onehot_made, 1)

            def messages(i, n, j, nth):
                dve.wait_ge(w_in[j], 16 * (nth + 1))
                dve.wait_ge(kv_ready, n + 1)
                dve.tensor_tensor(out=prod, in0=kv[j][:, :, 0:FEAT], in1=w[j], op=ALU.mult)
                dve.drain()
                dve.wait_ge(q_spread, n + 2)
                dve.tensor_tensor(out=prod, in0=prod, in1=tiles3(q_ps[j % 2]), op=ALU.mult).then_inc(q_used, 1)
                dve.drain()
                dve.tensor_reduce(out=alpha, in_=prod.rearrange("p t (h d) -> p (t h) d", h=HEADS1),
                                  axis=AX.X, op=ALU.add)
                dve.drain()
                by_tile = alpha.rearrange("p (t h) -> p t h", h=HEADS1)
                dve.scalar_tensor_tensor(
                    out=by_tile, in0=by_tile, scalar=(FEAT // HEADS1) ** -0.5,
                    in1=edge_w[:, bass.DynSlice(i * GROUP, GROUP)].unsqueeze(2).to_broadcast([P, GROUP, HEADS1]),
                    op0=ALU.mult, op1=ALU.mult)
                dve.drain()
                dve.tensor_tensor(
                    out=message[j % 2].rearrange("p t (h d) -> p t h d", h=HEADS1),
                    in0=kv[j][:, :, FEAT:].rearrange("p t (h d) -> p t h d", h=HEADS1),
                    in1=by_tile.unsqueeze(3).to_broadcast([P, GROUP, HEADS1, FEAT // HEADS1]),
                    op=ALU.mult).then_inc(msg_made, 1)

            def add(n, j, start):
                dve.wait_ge(summed, n + 1)
                window = k["sumT"][:, bass.DynSlice(start, P)]
                dve.tensor_tensor(out=window, in0=window, in1=sum_ps[j % 2], op=ALU.add)

            def one_round(i, first, last_round, r):
                nth = dve.snap(rounds)
                n0 = nth * SLOTS
                starts = window_starts(dve, regs, k["base_sb"], SLOTS * i, r)
                for j in range(SLOTS):
                    if not last_round or j + 2 < SLOTS:
                        make_onehot(SLOTS * i + j + 2, (j + 2) % SLOTS)
                    messages(SLOTS * i + j, n0 + j, j, nth)
                    if j:
                        add(n0 + j - 1, j - 1, starts[j - 1])
                    elif not first:
                        add(n0 - 1, SLOTS - 1, dve.snap(before, min_val=0, max_val=NODES))
                dve.reg_mov(before, starts[-1])
                dve.reg_add(rounds, rounds, 1)

            with dve.Fori(0, passes) as r:
                for j in range(2):
                    make_onehot(j, j)
                one_round(0, True, False, r)
                with dve.Fori(1, ROUNDS - 1) as i:
                    one_round(i, False, False, r)
                one_round(ROUNDS - 1, False, True, r)
                dve.drain()
                add(dve.snap(rounds) * SLOTS - 1, SLOTS - 1, dve.snap(before, min_val=0, max_val=NODES))
                dve.drain()
                dve.tensor_scalar(k["iota_pass"], k["iota_pass"], float(P), None, ALU.add)
                dve.drain()


def final(nc, S, sb, shared):
    k = shared
    B = BATCH * FEAT
    sT = [k["ring"][:, u * B:(u + 1) * B] for u in range(2)]
    y = [k["ring"][:, (2 + u) * B:(3 + u) * B] for u in range(2)]
    o = [k["ring"][:, (4 + u) * B:(5 + u) * B].rearrange("p (b f) -> p b f", b=BATCH) for u in range(2)]
    at = 6 * B
    stats = k["ring"][:, at:at + 6 * BATCH].rearrange("p (b w) -> p b w", b=BATCH)
    mv = k["ring"][:, at + 32:at + 32 + 2 * BATCH].rearrange("p (b w) -> p b w", b=BATCH)
    rstd = k["ring"][:, at + 48:at + 48 + BATCH]
    half_neg = k["ring"][:, at + 56:at + 56 + BATCH]
    x1 = k["ring"][:, 2 * CHUNK_TILES * XROW - NODE_ROWS:]
    copied = S("copied2")
    turned = S("turned2")
    added = S("added2")
    made = S("made2")
    var_made = S("var2_made")
    rstd_made = S("rstd2_made")
    written = [S(f"written{i}") for i in range(2)]

    with nc.Block() as block:
        @block.scalar
        def _(act):
            with act.Fori(0, BATCHES // 2) as i:
                for u in range(2):
                    n = 2 * i + u
                    act.wait_ge(added, n + 1)
                    act.activation(sT[u], k["sumT"][:, bass.DynSlice(n * B, B)], ACT.Copy).then_inc(copied, 1)

        @block.gpsimd
        def _(pool):
            pool.memset(half_neg, -0.5)
            pool.drain()
            with pool.Fori(0, BATCHES) as i:
                pool.wait_ge(var_made, i + 1)
                pool.tensor_tensor(out=rstd, in0=rstd, in1=half_neg, op=ALU.pow).then_inc(rstd_made, 1)

        @block.tensor
        def _(pe):
            with pe.Fori(0, BATCHES // 2) as i:
                for u in range(2):
                    pe.wait_ge(copied, 2 * i + u + 1)
                    for b in range(BATCH):
                        last = pe.transpose(k["wide"][u][:, b * P:(b + 1) * P], sT[u][:, b * P:(b + 1) * P], k["ident_sb"])
                    last.then_inc(turned, 1)

        @block.vector
        def _(dve):
            dve.sem_inc(added, 2)

            def batch(u, n, times_written):
                dve.wait_ge(turned, n + 1)
                dve.tensor_tensor(out=y[u], in0=k["wide"][u][:, 0:B], in1=x1[:, bass.DynSlice(n * B, B)], op=ALU.add)\
                   .then_inc(added, 1)
                free = None if times_written is None else (written[u], 16 * times_written)
                norm(dve, o[u], y[u].rearrange("p (b f) -> p b f", b=BATCH), stats, mv, rstd,
                     var_made, rstd_made, n, free).then_inc(made, 1)

            for u in range(2):
                batch(u, u, None)
            with dve.Fori(1, BATCHES // 2) as i:
                for u in range(2):
                    batch(u, 2 * i + u, i)

        @block.sync
        def _(sp):
            with sp.Fori(0, BATCHES // 2) as i:
                for u in range(2):
                    n = 2 * i + u
                    sp.wait_ge(made, n + 1)
                    sp.dma_start(k["out"][bass.DynSlice(n * BATCH * P, BATCH * P), :].rearrange("(b p) f -> p b f", p=P),
                                 o[u]).then_inc(written[u], 16)
            for u in range(2):
                sp.wait_ge(written[u], 16 * (BATCHES // 2))


def kernel(x, src, dst, edge_attr_128, edge_attr_16, edge_weight1, L0_gnn_W_lin, L0_gnn_W_edge,
           L0_gnn_att_src, L0_gnn_att_dst, L0_gnn_att_edge, L0_gnn_bias, L0_gnn_ln_gamma, L0_gnn_ln_beta,
           L1_gnn_Wq, L1_gnn_Wk, L1_gnn_Wv):
    import concourse.bacc as bacc
    from concourse.bass_utils import run_bass_kernel_spmd

    f32, i32 = np.float32, np.int32
    x = np.asarray(x)
    src, dst = np.asarray(src).astype(i32), np.asarray(dst).astype(i32)
    slots = TILES0 * P
    src_p = np.concatenate([src, np.zeros(slots - EDGES, i32)])
    dst_p = np.concatenate([dst, np.full(slots - EDGES, NODES, i32)])
    slots1 = slots
    ea = np.concatenate([np.asarray(edge_attr_128), np.zeros((slots1 - EDGES, FEAT), f32)])
    ea16 = np.concatenate([np.asarray(edge_attr_16), np.zeros((slots - EDGES, EDGE_DIM), f32)])
    ew = np.concatenate([np.asarray(edge_weight1)[:, 0], np.zeros(slots1 - EDGES, f32)])
    xpad = np.concatenate([x, np.zeros((NODE_ROWS - NODES, FEAT), f32)])

    per_chunk = dst_p.reshape(CHUNKS, RUNS, RUN)
    around = np.concatenate([np.array([-1], i32), dst_p, np.array([-1], i32)])
    runs = np.stack([around[n * RUN:n * RUN + RUN + 2] for n in range(CHUNKS * RUNS)])
    dst_runs = np.tile(runs.reshape(CHUNKS, 1, RUNS, RUN + 2), (1, HEADS0, 1, 1)).reshape(CHUNKS, P, RUN + 2)
    group_ends = dst_p.reshape(GROUPS0, GROUP * P)

    def by_head(vector):
        v = np.asarray(vector).reshape(HEADS0, -1)
        m = np.zeros((HEADS0, v.shape[1], HEADS0), f32)
        for h in range(HEADS0):
            m[h, :, h] = v[h]
        return m.reshape(-1, HEADS0)

    sel4 = np.zeros((P, HEADS0), f32)
    sel4[np.arange(HEADS0) * RUNS, np.arange(HEADS0)] = 1
    arrays = {
        "xT": xpad.T, "xpad": xpad,
        "src_idx0": src_p.reshape(CHUNKS, CHUNK_TILES, P).transpose(0, 2, 1),
        "src_idx1": src_p[:slots1].reshape(GROUPS1, GROUP, P).transpose(0, 2, 1),
        "dst_tile": dst_p.reshape(TILES0, P).T,
        "dst_runs": dst_runs,
        "base_rep": np.broadcast_to(group_ends[:, 0], (P, GROUPS0)),
        "last_rep": np.broadcast_to(group_ends[:, -1], (P, GROUPS0)),
        "base_row": group_ends[:, 0].reshape(1, GROUPS0),
        "dst_row": dst_p.reshape(1, -1),
        "ea_turned": ea16.reshape(GROUPS0, GROUP, P, EDGE_DIM).transpose(0, 1, 3, 2).reshape(GROUPS0, P, P),
        "ea": ea, "ew": ew.reshape(GROUPS1 * GROUP, P).T,
        "w_linT": np.asarray(L0_gnn_W_lin).T, "w_lin": np.asarray(L0_gnn_W_lin),
        "att": np.concatenate([by_head(L0_gnn_att_dst), by_head(L0_gnn_att_src)], axis=1),
        "w_edge": np.tile(np.asarray(L0_gnn_W_edge), (1, GROUP)), "att_edge": by_head(L0_gnn_att_edge),
        "wqkvT": np.concatenate([np.asarray(m).T for m in (L1_gnn_Wq, L1_gnn_Wk, L1_gnn_Wv)], axis=1),
        "rows": np.broadcast_to(np.concatenate([np.asarray(v) for v in (L0_gnn_bias, L0_gnn_ln_gamma, L0_gnn_ln_beta)]),
                                (P, 3 * FEAT)),
        "ident": np.eye(P, dtype=f32),
        "node_of": np.arange(P, dtype=f32).reshape(P, 1),
        "own_tile": np.kron(np.eye(GROUP, dtype=f32), np.ones((EDGE_DIM, HEADS0), f32)),
        "iota": np.broadcast_to(np.arange(P, dtype=f32), (P, P)),
        "sel": np.repeat(sel4, FEAT // HEADS0, axis=1),
        "sel4": sel4,
    }
    arrays = {name: np.ascontiguousarray(a) for name, a in arrays.items()}
    nc = bacc.Bacc("TRN2", target_bir_lowering=False, num_devices=1)
    args = {name: nc.dram_tensor(f"{name}_dram", list(a.shape), mybir.dt.from_np(a.dtype), kind="ExternalInput").ap()
            for name, a in arrays.items()}
    args["out"] = nc.dram_tensor("out_dram", [NODE_ROWS, FEAT], F32, kind="ExternalOutput").ap()
    program(nc, **args)
    r = run_bass_kernel_spmd(nc, [{f"{name}_dram": a for name, a in arrays.items()}], core_ids=[0])
    return r.results[0]["out_dram"][:NODES]
```

```python
import numpy as np
import concourse.bass as bass
from concourse import mybir

F32 = mybir.dt.float32
BF16 = mybir.dt.bfloat16
I32 = mybir.dt.int32
ALU = mybir.AluOpType
ACT = mybir.ActivationFunctionType
AX = mybir.AxisListType

P = 128
NODES, FEAT = 6250, 128
EDGES = 206250
HEADS0, HEADS1 = 4, 8
EDGE_DIM = 16
GROUP = 8
CHUNK_GROUPS = 12
CHUNK_TILES = GROUP * CHUNK_GROUPS
RUNS = P // HEADS0
RUN = CHUNK_TILES * P // RUNS
RUN_TILES = RUN // P
TILES = -(-EDGES // P)
CHUNKS = -(-TILES // CHUNK_TILES)
TILES0 = CHUNKS * CHUNK_TILES
GROUPS0 = TILES0 // GROUP
GROUPS1 = GROUPS0
GATHERED1 = -(-TILES // GROUP)
LAST_TILES = TILES - (CHUNKS - 1) * CHUNK_TILES
LAST_GROUPS = -(-LAST_TILES // GROUP)
NODE_BLOCKS = -(-(NODES + P) // P)
NODE_ROWS = NODE_BLOCKS * P
XROW = FEAT + HEADS0
PARTS = 3
BATCH = 5
BATCHES = NODE_BLOCKS // BATCH
LN_EPS = 1e-5
SLOPE = 0.2
NEG = -1e30
assert GROUP * EDGE_DIM == P and CHUNKS % 2 == 1 and GROUPS1 % 4 == 0 and GROUPS1 - 4 < GATHERED1 and BATCHES % 2 == 0
assert RUN_TILES * RUNS == CHUNK_TILES and LAST_GROUPS % 2 == 0


def counter(eng, name):
    reg = eng.alloc_register(name)
    eng.reg_mov(reg, 0)
    return reg


def window_starts(eng, regs, base_row, first_group, pass_no):
    eng.reg_load(regs, base_row[0:1, bass.DynSlice(first_group, len(regs))])
    out = []
    for reg in regs:
        eng.reg_add(reg, reg, pass_no * P)
        eng.reg_alu(reg, reg, NODES, op=ALU.min)
        out.append(eng.snap(reg, min_val=0, max_val=NODES))
    return out


def wait_here(eng, sem, value, gate):
    eng.wait_ge(sem, value)
    eng.sem_inc(gate, 1)


def program(nc, xT, xpad, src_idx0, src_idx1, dst_tile, dst_row, dst_runs, base_rep, last_rep, base_row,
            ea_turned, ea, ew, w_linT, w_lin, att, w_edge, att_edge, wqkvT, rows, ident, iota, node_of, own_tile, sel, sel_parts,
            out):
    S = nc.alloc_semaphore

    def sb(name, shape, dt=F32):
        return nc.alloc_sbuf_tensor(name, shape, dt).ap()

    x_table = nc.dram_tensor("x_table", [NODE_ROWS, XROW], F32, kind="Internal").ap()
    ai_table = nc.dram_tensor("ai_table", [NODE_ROWS, 3 * HEADS0], BF16, kind="Internal").ap()
    q_table = nc.dram_tensor("q_table", [NODE_ROWS, FEAT], F32, kind="Internal").ap()
    kv_table = nc.dram_tensor("kv_table", [NODE_ROWS, 2 * FEAT], F32, kind="Internal").ap()

    ident_sb = sb("ident_sb", [P, P])
    iota_sb = sb("iota_sb", [P, P])
    iota_pass = sb("iota_pass", [P, P])
    sel_sb = sb("sel_sb", [P, P])
    sel_parts_sb = sb("sel_parts_sb", [P, PARTS * HEADS0])
    drel = sb("drel", [P, TILES0])
    base_sb = sb("base_sb", [1, GROUPS0], I32)
    passes_sb = sb("passes_sb", [P, 1], I32)
    sumT = sb("sumT", [P, NODE_ROWS])
    denT = sb("denT", [PARTS * HEADS0, NODE_ROWS])
    we_att = sb("we_att", [P, GROUP * HEADS0])
    base_f = sb("base_f", [P, GROUPS0])
    node_col = sb("node_col", [P, 1])
    node_pass = sb("node_pass", [P, 1])
    ring = sb("ring", [P, 2 * CHUNK_TILES * XROW])
    work = sb("work", [P, 5 * GROUP * P])

    psum = nc.alloc_psum_tensor("psum", [P, 8 * 512], F32).ap()
    bank = [psum[:, i * 512:(i + 1) * 512] for i in range(4)]
    wide = [psum[:, (4 + 2 * i) * 512:(6 + 2 * i) * 512] for i in range(2)]

    dst_i = ring[:, 0:TILES0].bitcast(I32)
    base_i = ring[:, TILES0:TILES0 + GROUPS0].bitcast(I32)
    last_i = ring[:, TILES0 + GROUPS0:TILES0 + 2 * GROUPS0].bitcast(I32)
    span_i = ring[:, TILES0 + 2 * GROUPS0:TILES0 + 3 * GROUPS0].bitcast(I32)
    at = TILES0 + 3 * GROUPS0
    att_sb = ring[:, at:at + 2 * HEADS0]
    w_lin_sb = ring[:, at + 16:at + 16 + FEAT]
    w_edge_sb = ring[:, at + 160:at + 160 + P]
    att_edge_sb = ring[:, at + 288:at + 288 + HEADS0]
    own_tile_sb = ring[:, at + 292:at + 292 + GROUP * HEADS0]
    at += 384
    xT_slot = [ring[:, at + i * 2 * P:at + (i + 1) * 2 * P] for i in range(2)]
    at += 4 * P
    W0 = FEAT + 2 * HEADS0
    row_slot = [ring[:, at + i * 2 * W0:at + (i + 1) * 2 * W0].rearrange("p (b w) -> p b w", b=2)
                for i in range(2)]
    at += 4 * W0
    rhs0 = ring[:, at:at + W0]
    at += W0
    AI = NODE_BLOCKS * HEADS0
    ai_all = ring[:, at:at + AI]
    ai_rest = ring[:, at + AI:at + 2 * AI]
    ai_parts = ring[:, at + 2 * AI:at + 4 * AI].bitcast(BF16)[:, 0:3 * AI].rearrange("p (b s h) -> p b s h", s=3, h=HEADS0)
    ai_made = S("ai_made")
    ai_split = S("ai_split")
    ai_out = S("ai_out")
    consts_in = S("consts_in")
    ints_in = S("ints_in")
    weights_in = S("weights_in")
    folded = S("folded")
    folded_sb = S("folded_sb")
    xT_in = [S(f"xT_in{i}") for i in range(2)]
    rows_made = S("rows_made")
    rows_copied = S("rows_copied")
    rows_out = [S(f"rows_out{i}") for i in range(2)]
    PAIRS = NODE_BLOCKS // 2

    with nc.Block() as block:
        @block.sync
        def _(sp):
            for to, of in ((w_lin_sb, w_lin), (att_sb, att), (w_edge_sb, w_edge), (att_edge_sb, att_edge), (own_tile_sb, own_tile),
                           (rhs0[:, 0:FEAT], w_linT)):
                sp.dma_start(to, of).then_inc(weights_in, 16)
            with sp.Fori(0, PAIRS // 2) as i:
                for u in range(2):
                    sp.wait_ge(rows_made, 2 * i + u + 1)
                    sp.dma_start(xT_slot[u], xT[:, bass.DynSlice((2 * i + u) * 2 * P, 2 * P)]).then_inc(xT_in[u], 16)
            sp.wait_ge(rows_made, PAIRS)
            sp.dma_start(xT_slot[0], xT[:, (PAIRS - 1) * 2 * P:]).then_inc(xT_in[0], 16)
            sp.wait_ge(ai_split, 1)
            sp.dma_start(ai_table.rearrange("(b p) w -> p b w", p=P), ai_parts.rearrange("p b s h -> p b (s h)"))\
              .then_inc(ai_out, 16)
            sp.wait_ge(ai_out, 16)

        @block.gpsimd
        def _(pool):
            for to, of in ((ident_sb, ident), (iota_sb, iota), (sel_sb, sel), (sel_parts_sb, sel_parts), (node_col, node_of)):
                pool.dma_start(to, of).then_inc(consts_in, 16)
            for to, of in ((dst_i, dst_tile), (base_i, base_rep), (last_i, last_rep), (base_sb, base_row)):
                pool.dma_start(to, of).then_inc(ints_in, 16)
            pool.wait_ge(consts_in, 80)

        @block.tensor
        def _(pe):
            pe.wait_ge(weights_in, 96)
            pe.sem_inc(rows_made, 2)
            pe.matmul(bank[0][:, 0:2 * HEADS0], w_lin_sb, att_sb, start=True, stop=True)
            pe.matmul(bank[1][:, 0:HEADS0], w_edge_sb, att_edge_sb, start=True, stop=True).then_inc(folded, 1)
            pe.wait_ge(folded_sb, 2)

            def pair(u, n):
                for b in range(2):
                    last = pe.matmul(bank[2 + u][:, b * W0:(b + 1) * W0], xT_slot[u][:, b * P:(b + 1) * P],
                                     rhs0, start=True, stop=True)
                last.then_inc(rows_made, 1)

            with pe.Fori(0, PAIRS // 2) as i:
                for u in range(2):
                    pe.wait_ge(xT_in[u], 16 * (i + 1))
                    pe.wait_ge(rows_copied, 2 * i + u + 1)
                    pair(u, 2 * i + u)
            pe.wait_ge(xT_in[0], 16 * (PAIRS // 2 + 1))
            pe.wait_ge(rows_copied, PAIRS)
            pair(0, PAIRS - 1)

        @block.vector
        def _(dve):
            dve.sem_inc(rows_copied, 2)
            dve.wait_ge(weights_in, 96)
            dve.wait_ge(folded, 1)
            dve.tensor_copy(rhs0[:, FEAT:W0], bank[0][:, 0:2 * HEADS0]).then_inc(folded_sb, 1)
            dve.tensor_tensor(out=we_att.rearrange("p (t h) -> p t h", h=HEADS0),
                              in0=bank[1][:, 0:HEADS0].unsqueeze(1).to_broadcast([P, GROUP, HEADS0]),
                              in1=own_tile_sb.rearrange("p (t h) -> p t h", h=HEADS0), op=ALU.mult)\
               .then_inc(folded_sb, 1)
            dve.memset(sumT, 0.0)
            dve.memset(denT, 0.0)
            dve.wait_ge(ints_in, 64)
            dve.tensor_copy(base_f, base_i)
            dve.tensor_tensor(out=drel.rearrange("p (g t) -> p g t", t=GROUP),
                              in0=dst_i.rearrange("p (g t) -> p g t", t=GROUP),
                              in1=base_i.unsqueeze(2).to_broadcast([P, GROUPS0, GROUP]), op=ALU.subtract)
            dve.tensor_tensor(out=span_i, in0=last_i, in1=base_i, op=ALU.subtract)
            dve.drain()
            dve.tensor_reduce(out=passes_sb, in_=span_i, axis=AX.X, op=ALU.max)
            dve.drain()
            dve.tensor_scalar(passes_sb, passes_sb, 7, None, ALU.arith_shift_right)
            dve.drain()
            dve.tensor_scalar(passes_sb, passes_sb, 1, None, ALU.add)
            dve.wait_ge(ai_made, PAIRS)
            per_block = lambda t: t.rearrange("p (b h) -> p b h", h=HEADS0)
            dve.tensor_copy(ai_parts[:, :, 0, :], per_block(ai_all))
            for part in range(1, 3):
                dve.drain()
                dve.tensor_tensor(out=per_block(ai_rest if part == 1 else ai_all),
                                  in0=per_block(ai_all if part == 1 else ai_rest),
                                  in1=ai_parts[:, :, part - 1, :], op=ALU.subtract)
                dve.drain()
                last = dve.tensor_copy(ai_parts[:, :, part, :], per_block(ai_rest if part == 1 else ai_all))
            last.then_inc(ai_split, 1)

        @block.scalar
        def _(act):
            def copy_out(u, b0, pair_cols):
                made = bank[2 + u][:, 0:2 * W0].rearrange("p (b w) -> p b w", b=2)
                act.activation(ai_all[:, pair_cols].rearrange("p (b h) -> p b h", b=2), made[:, :, XROW:W0], ACT.Copy)\
                   .then_inc(ai_made, 1)
                act.activation(row_slot[u][:, :, 0:XROW], made[:, :, 0:XROW], ACT.Copy).then_inc(rows_copied, 1)
                act.drain()
                act.dma_start(x_table[b0, :].rearrange("(b p) w -> p b w", p=P), row_slot[u][:, :, 0:XROW])\
                   .then_inc(rows_out[u], 16)

            def pair_of(u, n, k2):
                act.wait_ge(rows_made, n + 3)
                if k2 is not None:
                    act.wait_ge(rows_out[u], 16 * k2)
                copy_out(u, bass.DynSlice(n * 2 * P, 2 * P), bass.DynSlice(n * 2 * HEADS0, 2 * HEADS0))

            for u in range(2):
                pair_of(u, u, None)
            with act.Fori(1, PAIRS // 2) as i:
                for u in range(2):
                    pair_of(u, 2 * i + u, i)
            pair_of(0, PAIRS - 1, PAIRS // 2)
            act.wait_ge(rows_out[0], 16 * (PAIRS // 2 + 1))
            act.wait_ge(rows_out[1], 16 * (PAIRS // 2))

    shared = dict(
        x_table=x_table, ai_table=ai_table, q_table=q_table, kv_table=kv_table, xpad=xpad,
        src_idx0=src_idx0, src_idx1=src_idx1, dst_row=dst_row, dst_runs=dst_runs, ea_turned=ea_turned,
        ea=ea, ew=ew, wqkvT=wqkvT, rows=rows, out=out, ident_sb=ident_sb, iota_sb=iota_sb,
        iota_pass=iota_pass, node_col=node_col, node_pass=node_pass, sel_sb=sel_sb, sel_parts_sb=sel_parts_sb,
        drel=drel, base_f=base_f, base_sb=base_sb, passes_sb=passes_sb, sumT=sumT, denT=denT,
        we_att=we_att, ring=ring, work=work, psum=psum, bank=bank, wide=wide)
    layer0(nc, S, sb, shared)
    between(nc, S, sb, shared)
    layer1(nc, S, sb, shared)
    final(nc, S, sb, shared)


def layer0(nc, S, sb, shared):
    k = shared
    GP = GROUP * P
    onehot = [k["work"][:, u * GP:(u + 1) * GP].rearrange("p (t n) -> p t n", t=GROUP) for u in range(2)]
    message = [k["work"][:, (2 + u) * GP:(3 + u) * GP].rearrange("p (t f) -> p t f", t=GROUP) for u in range(2)]
    onehotT = [k["work"][:, 4 * GP + u * GP // 2:4 * GP + (u + 1) * GP // 2].bitcast(BF16) for u in range(2)]
    dst_all = [sb(f"dst_all{i}", [P, GP], I32) for i in range(2)]
    ea_pair = [sb(f"ea_pair{i}", [P, 2, P]) for i in range(2)]
    idx = [sb(f"idx{i}", [P, CHUNK_TILES], I32) for i in range(2)]
    runs_dst = sb("runs_dst", [P, RUN + 2], I32)
    ai_win = [sb(f"ai_win{i}", [P, 3 * HEADS0], BF16) for i in range(2)]
    zeros = sb("zeros", [P, CHUNK_TILES * HEADS0], BF16)
    score = sb("score", [P, HEADS0, CHUNK_TILES])
    ex = score
    ex_parts = sb("ex_parts", [P, CHUNK_TILES, PARTS, HEADS0], BF16)
    ex_group = [sb(f"ex_group{i}", [P, GROUP, PARTS, HEADS0], BF16) for i in range(2)]
    onehot_bf = [sb(f"onehot_bf{i}", [P, GROUP, P], BF16) for i in range(2)]
    edge_change = sb("edge_change", [P, RUN + 1])
    ahead = sb("ahead", [P, RUN])
    back = sb("back", [P, RUN])
    cols = sb("cols", [P, 8])
    rowbuf = sb("rowbuf", [1, 5 * P])
    carry = sb("carry", [1, HEADS0])

    x_rows = k["ring"].rearrange("p (t w) -> p t w", w=XROW)
    scores_ps = k["bank"][0][:, 0:CHUNK_TILES * HEADS0]
    runs_ps = k["bank"][1][:, 0:RUN]
    small_ps = k["bank"][2]
    den_ps = [k["bank"][3 - u][0:PARTS * HEADS0, 0:P] for u in range(2)]
    sum_ps = [k["wide"][1][:, u * 512:u * 512 + P] for u in range(2)]

    idx_in = [S(f"idx_in{i}") for i in range(2)]
    gathered = [S(f"gathered{i}") for i in range(2)]
    chunk_ready = S("chunk_ready")
    rows_released = S("rows_released")
    ea_in = [S(f"ea_in{i}") for i in range(2)]
    ea_used = S("ea_used")
    ai_in = [S(f"ai_in{i}") for i in range(2)]
    dst_in = [S(f"dst_in{i}") for i in range(2)]
    dst_used = S("dst_used")
    onehotT_made = S("onehotT_made")
    scores_added = S("scores_added")
    runs_in = S("runs_in")
    runs_used = S("runs_used")
    onehot_made = S("onehot_made")
    onehot_bf_made = S("onehot_bf_made")
    msg_made = S("msg_made")
    summed = S("summed")
    scores_summed = S("scores_summed")
    zeros_set = S("zeros_set")
    dve_to_pe = S("dve_to_pe")
    pe_to_dve = S("pe_to_dve")
    shifted = S("shifted")
    exp_done = S("exp_done")
    exT_done = S("exT_done")
    ex_copied = S("ex_copied")
    pe_gate = S("pe_gate")
    pool_gate = S("pool_gate")
    dve_gate = S("dve_gate")
    HALF = CHUNK_GROUPS // 2
    STEPS = 5
    run_ends = [ahead[:, RUN - 1:RUN], cols[:, 0:1], cols[:, 1:2]]

    with nc.Block() as block:
        @block.sync
        def _(sp):
            passes = sp.value_load(k["passes_sb"][0:1, 0:1], min_val=1, max_val=NODE_BLOCKS)
            visit = counter(sp, "sp_visit0")
            regs = [sp.alloc_register(f"sp_base0{u}") for u in range(2)]
            with sp.Fori(0, CHUNKS) as s:
                sp.wait_ge(runs_used, s + 1)
                sp.dma_start(runs_dst, k["dst_runs"][bass.DynSlice(s, 1), :, :].rearrange("o p n -> (o p) n"))\
                  .then_inc(runs_in, 16)
                with sp.Fori(0, HALF // 2) as g:
                    for u in range(2):
                        n = s * HALF + 2 * g + u
                        sp.wait_ge(ea_used, n + 1)
                        sp.dma_start(ea_pair[u], k["ea_turned"][bass.DynSlice(2 * n, 2), :, :].rearrange("g p e -> p g e"))\
                          .then_inc(ea_in[u], 16)
                with sp.Fori(0, passes) as r:
                    with sp.Fori(0, HALF) as g:
                        v = sp.snap(visit)
                        first_group = s * CHUNK_GROUPS + 2 * g
                        starts = window_starts(sp, regs, k["base_sb"], first_group, r)
                        for u in range(2):
                            sp.wait_ge(dst_used, 2 * v + u + 1)
                            sp.dma_start(dst_all[u], k["dst_row"][0:1, bass.DynSlice((first_group + u) * GP, GP)]
                                         .to_broadcast([P, GP])).then_inc(dst_in[u], 16)
                            sp.wait_ge(scores_added, 2 * v + u + 1)
                            sp.dma_start(ai_win[u], k["ai_table"][bass.DynSlice(starts[u], P), :]).then_inc(ai_in[u], 16)
                        sp.reg_add(visit, visit, 1)

        @block.gpsimd
        def _(pool):
            ALL = 16 * CHUNK_TILES

            def chunk(h, nth, s, tiles, before, following):
                wait_here(pool, idx_in[h], 16 * (nth + 1), pool_gate)
                wait_here(pool, rows_released, s + 1, pool_gate)
                for t in range(tiles):
                    pool.indirect_dma_start(x_rows[:, h * CHUNK_TILES + t, :], None, k["x_table"],
                                            bass.IndirectOffsetOnAxis(idx[h][:, t:t + 1], 0))\
                        .then_inc(gathered[h], 16)
                    if t == 4:
                        if before is not None:
                            pool.wait_ge(gathered[1 - h], before)
                            pool.sem_inc(chunk_ready, 1)
                        if following is not None:
                            pool.dma_start(idx[1 - h], k["src_idx0"][bass.DynSlice(following, 1), :, :]
                                           .rearrange("o p n -> (o p) n")).then_inc(idx_in[1 - h], 16)

            pool.dma_start(idx[0], k["src_idx0"][0, :, :]).then_inc(idx_in[0], 16)
            chunk(0, 0, 0, CHUNK_TILES, None, 1)
            PAIRS = CHUNKS // 2 - 1
            with pool.Fori(0, PAIRS) as i:
                chunk(1, i, 2 * i + 1, CHUNK_TILES, ALL * (i + 1), 2 * i + 2)
                chunk(0, i + 1, 2 * i + 2, CHUNK_TILES, ALL * (i + 1), 2 * i + 3)
            chunk(1, PAIRS, CHUNKS - 2, CHUNK_TILES, ALL * (PAIRS + 1), CHUNKS - 1)
            chunk(0, PAIRS + 1, CHUNKS - 1, LAST_TILES, ALL * (PAIRS + 1), None)
            pool.wait_ge(gathered[0], ALL * (PAIRS + 1) + 16 * LAST_TILES)
            pool.sem_inc(chunk_ready, 1)

        @block.tensor
        def _(pe):
            passes = pe.value_load(k["passes_sb"][0:1, 0:1], min_val=1, max_val=NODE_BLOCKS)
            d_visit = counter(pe, "pe_d_visit0")
            c_visit = counter(pe, "pe_c_visit0")

            def open_scores(s):
                pe.matmul(scores_ps, zeros[:, 0:P], zeros, start=True, stop=False)
                for g in range(CHUNK_GROUPS):
                    if g % 2 == 0:
                        pe.wait_ge(ea_in[g // 2 % 2], 16 * (s * (HALF // 2) + g // 4 + 1))
                    last = pe.matmul(scores_ps[:, g * GROUP * HEADS0:(g + 1) * GROUP * HEADS0],
                                     ea_pair[g // 2 % 2][:, g % 2, :], k["we_att"], start=False, stop=False)
                    if g % 2 == 1:
                        last.then_inc(ea_used, 1)

            def scores_group(d, g):
                pe.wait_ge(onehotT_made, d * CHUNK_GROUPS + g + 1)
                pe.wait_ge(ai_in[g % 2], 16 * (d * HALF + g // 2 + 1))
                for t in range(GROUP):
                    at = (g * GROUP + t) * HEADS0
                    for part in range(PARTS):
                        last = pe.matmul(scores_ps[:, at:at + HEADS0], onehotT[g % 2][:, t * P:(t + 1) * P],
                                         ai_win[g % 2][:, part * HEADS0:(part + 1) * HEADS0],
                                         start=False, stop=False)
                last.then_inc(scores_added, 1)

            def close_scores():
                pe.matmul(scores_ps, zeros[:, 0:P], zeros, start=False, stop=True).then_inc(scores_summed, 1)

            def maxima(s):
                pe.wait_ge(dve_to_pe, STEPS * s + 1)
                for t in range(RUN_TILES):
                    last = pe.transpose(runs_ps[:, t * P:(t + 1) * P],
                                        score.rearrange("p h (c t) -> p (h c) t", t=RUN_TILES)[:, :, t], k["ident_sb"])
                last.then_inc(pe_to_dve, 1)
                pe.wait_ge(dve_to_pe, STEPS * s + 2)
                for c in range(3):
                    last = pe.transpose(small_ps[0:1, c * P:(c + 1) * P], run_ends[c], k["ident_sb"])
                last.then_inc(pe_to_dve, 1)
                wait_here(pe, dve_to_pe, STEPS * s + 3, pe_gate)
                pe.transpose(small_ps[:, 400:401], rowbuf[0:1, 3 * P:4 * P], k["ident_sb"][0:1, 0:1]).then_inc(pe_to_dve, 1)
                pe.wait_ge(dve_to_pe, STEPS * s + 4)
                pe.transpose(small_ps[0:1, 0:P], back[:, 0:1], k["ident_sb"]).then_inc(pe_to_dve, 1)
                wait_here(pe, dve_to_pe, STEPS * s + 5, pe_gate)
                pe.transpose(small_ps[:, 402:403], rowbuf[0:1, 3 * P:4 * P], k["ident_sb"][0:1, 0:1]).then_inc(pe_to_dve, 1)
                pe.wait_ge(exp_done, s + 1)
                for t in range(RUN_TILES):
                    pe.transpose(runs_ps[:, t * P:(t + 1) * P], ahead[:, t * P:(t + 1) * P], k["ident_sb"])
                pe.matmul(small_ps[:, 404:405], k["sel_sb"], cols[:, 5:6], start=True, stop=True)
                pe.matmul(small_ps[0:PARTS * HEADS0, 406:407], k["sel_parts_sb"], cols[:, 5:6], start=True, stop=True)\
                  .then_inc(exT_done, 1)

            def sums_group(c, g):
                u = g % 2
                pe.wait_ge(msg_made, c + g + 1)
                for t in range(GROUP):
                    pe.matmul(sum_ps[u], message[u][:, t, :], onehot[u][:, t, :], start=t == 0, stop=t == GROUP - 1)
                pe.wait_ge(onehot_bf_made, c + g + 1)
                for t in range(GROUP):
                    last = pe.matmul(den_ps[u], ex_group[u][:, t, :, :].rearrange("p s h -> p (s h)"),
                                     onehot_bf[u][:, t, :], start=t == 0, stop=t == GROUP - 1)
                last.then_inc(summed, 1)

            pe.wait_ge(zeros_set, 1)
            open_scores(0)
            with pe.Fori(0, passes) as r:
                d = pe.snap(d_visit)
                for g in range(CHUNK_GROUPS):
                    scores_group(d, g)
                pe.reg_add(d_visit, d_visit, 1)
            close_scores()
            with pe.Fori(0, CHUNKS - 1) as s:
                maxima(s)
                open_scores(s + 1)
                with pe.Fori(0, passes) as r:
                    c, d = pe.snap(c_visit), pe.snap(d_visit)
                    for g in range(CHUNK_GROUPS):
                        scores_group(d, g)
                        sums_group(c, g)
                    pe.reg_add(c_visit, c_visit, CHUNK_GROUPS)
                    pe.reg_add(d_visit, d_visit, 1)
                close_scores()
            maxima(CHUNKS - 1)
            with pe.Fori(0, passes) as r:
                c = pe.snap(c_visit)
                for g in range(LAST_GROUPS):
                    sums_group(c, g)
                pe.reg_add(c_visit, c_visit, LAST_GROUPS)

        @block.scalar
        def _(act):
            passes = act.value_load(k["passes_sb"][0:1, 0:1], min_val=1, max_val=NODE_BLOCKS)
            group = counter(act, "act_group0")

            def chunk(s, groups):
                act.wait_ge(shifted, s + 1)
                act.activation(ahead, back, ACT.Exp)
                act.activation(cols[:, 5:6], cols[:, 4:5], ACT.Exp).then_inc(exp_done, 1)
                act.wait_ge(exT_done, s + 1)
                act.activation(ex.rearrange("p h (c t) -> p (h c) t", t=RUN_TILES),
                               runs_ps.rearrange("p (t q) -> p q t", t=RUN_TILES), ACT.Copy).then_inc(ex_copied, 1)
                with act.Fori(0, passes) as r:
                    with act.Fori(0, groups // 2) as g:
                        n = act.snap(group)
                        for u in range(2):
                            act.wait_ge(onehot_made, n + u + 1)
                            act.wait_ge(summed, n + u + 1)
                            act.activation(onehot_bf[u], onehot[u], ACT.Copy)
                            act.activation(ex_group[u].rearrange("p t s h -> p t (s h)"),
                                           ex_parts[:, bass.DynSlice((2 * g + u) * GROUP, GROUP), :, :]
                                           .rearrange("p t s h -> p t (s h)"), ACT.Copy).then_inc(onehot_bf_made, 1)
                        act.reg_add(group, group, 2)

            with act.Fori(0, CHUNKS - 1) as s:
                chunk(s, CHUNK_GROUPS)
            chunk(CHUNKS - 1, LAST_GROUPS)

        @block.vector
        def _(dve):
            passes = dve.value_load(k["passes_sb"][0:1, 0:1], min_val=1, max_val=NODE_BLOCKS)
            d_visit = counter(dve, "dve_d_visit0")
            c_visit = counter(dve, "dve_c_visit0")
            regs = [dve.alloc_register(f"dve_base0{u}") for u in range(2)]
            before = dve.alloc_register("dve_base_before0")
            dve.memset(zeros, 0.0).then_inc(zeros_set, 1)
            dve.memset(carry, NEG)
            dve.memset(cols, 0.0)
            for credit, n in ((rows_released, 2), (ea_used, 2), (dst_used, 2), (scores_added, 2), (runs_used, 1),
                              (summed, 2)):
                dve.sem_inc(credit, n)

            def first_pass():
                dve.drain()
                dve.tensor_copy(k["node_pass"], k["node_col"])
                dve.tensor_copy(k["iota_pass"], k["iota_sb"])
                dve.drain()

            def next_pass():
                dve.drain()
                for numbers in (k["node_pass"], k["iota_pass"]):
                    dve.tensor_scalar(numbers, numbers, float(P), None, ALU.add)
                dve.drain()

            def scores_onehot(u, v, group):
                dve.wait_ge(dst_in[u], 16 * (v + 1))
                dve.wait_ge(scores_added, 2 * v + u + 1)
                dve.tensor_scalar(onehotT[u], dst_all[u], k["base_f"][:, bass.DynSlice(group, 1)],
                                  k["node_pass"], ALU.subtract, ALU.is_equal).then_inc(onehotT_made, 1)
                dve.drain().then_inc(dst_used, 1)

            def maxima(s):
                dve.wait_ge(runs_in, 16 * (s + 1))
                dve.tensor_tensor(out=edge_change, in0=runs_dst[:, 0:RUN + 1], in1=runs_dst[:, 1:RUN + 2],
                                  op=ALU.not_equal).then_inc(runs_used, 1)
                dve.drain()
                dve.tensor_scalar(edge_change, edge_change, NEG, None, ALU.mult)
                dve.drain()
                dve.tensor_reduce(out=cols[:, 0:1], in_=edge_change[:, 0:RUN], axis=AX.X, op=ALU.min)
                dve.tensor_reduce(out=cols[:, 1:2], in_=edge_change[:, 1:RUN + 1], axis=AX.X, op=ALU.min)

                dve.wait_ge(scores_summed, s + 1)
                dve.wait_ge(chunk_ready, s + 1)
                dve.tensor_tensor(out=score.rearrange("p h t -> p t h"),
                                  in0=scores_ps.rearrange("p (t h) -> p t h", h=HEADS0),
                                  in1=x_rows[:, bass.DynSlice((s % 2) * CHUNK_TILES, CHUNK_TILES), FEAT:XROW],
                                  op=ALU.add)
                dve.drain()
                flat = score.rearrange("p h t -> p (h t)")
                dve.scalar_tensor_tensor(out=flat, in0=flat, scalar=SLOPE, in1=flat, op0=ALU.mult, op1=ALU.max)\
                   .then_inc(dve_to_pe, 1)

                dve.wait_ge(pe_to_dve, 5 * s + 1)
                dve.tensor_tensor_scan(ahead, edge_change[:, 0:RUN], runs_ps, NEG, ALU.add, ALU.max).then_inc(dve_to_pe, 1)
                ends, pen, pen_back, into, over = (rowbuf[0:1, c * P:(c + 1) * P] for c in range(5))
                by_head = lambda row: row.rearrange("p (h c) -> p h c", h=HEADS0)
                carry3 = carry.unsqueeze(2)
                dve.wait_ge(pe_to_dve, 5 * s + 2)
                dve.tensor_copy(rowbuf[0:1, 0:3 * P], small_ps[0:1, 0:3 * P])
                dve.drain()
                dve.tensor_tensor(out=by_head(over)[:, :, 0:1], in0=by_head(pen)[:, :, 0:1], in1=carry3, op=ALU.add)
                dve.drain()
                dve.tensor_tensor(out=by_head(ends)[:, :, 0:1], in0=by_head(ends)[:, :, 0:1],
                                  in1=by_head(over)[:, :, 0:1], op=ALU.max)
                dve.memset(by_head(pen)[:, :, 0:1], 2 * NEG)
                dve.memset(by_head(pen_back)[:, :, RUNS - 1:RUNS], 2 * NEG)
                dve.drain()
                dve.tensor_tensor_scan(over, pen, ends, 0.0, ALU.add, ALU.max)
                dve.drain()
                dve.tensor_copy(by_head(into)[:, :, 1:RUNS], by_head(over)[:, :, 0:RUNS - 1])
                dve.tensor_copy(by_head(into)[:, :, 0:1], carry3).then_inc(dve_to_pe, 1)
                dve.drain()
                dve.tensor_copy(carry3, by_head(over)[:, :, RUNS - 1:RUNS])
                dve.wait_ge(pe_to_dve, 5 * s + 3)
                dve.tensor_copy(cols[:, 2:3], small_ps[:, 400:401])
                dve.drain()
                dve.tensor_tensor_scan(ahead, edge_change[:, 0:RUN], runs_ps, cols[:, 2:3], ALU.add, ALU.max)
                dve.drain()
                scan_back = (back[:, ::-1], edge_change[:, RUN:0:-1], ahead[:, ::-1])
                dve.tensor_tensor_scan(*scan_back, NEG, ALU.add, ALU.max).then_inc(dve_to_pe, 1)
                dve.wait_ge(pe_to_dve, 5 * s + 4)
                dve.tensor_copy(ends, small_ps[0:1, 0:P])
                dve.drain()
                dve.tensor_tensor_scan(over[:, ::-1], pen_back[:, ::-1], ends[:, ::-1], 0.0, ALU.add, ALU.max)
                dve.drain()
                dve.tensor_copy(by_head(into)[:, :, 0:RUNS - 1], by_head(over)[:, :, 1:RUNS])
                dve.memset(by_head(into)[:, :, RUNS - 1:RUNS], 2 * NEG).then_inc(dve_to_pe, 1)
                dve.wait_ge(pe_to_dve, 5 * s + 5)
                dve.tensor_copy(cols[:, 3:4], small_ps[:, 402:403])
                dve.drain()
                dve.tensor_tensor_scan(*scan_back, cols[:, 3:4], ALU.add, ALU.max)
                dve.drain()
                dve.tensor_tensor(out=cols[:, 4:5], in0=cols[:, 2:3], in1=back[:, 0:1], op=ALU.subtract)
                dve.drain()
                dve.tensor_scalar(cols[:, 4:5], cols[:, 4:5], 0.0, None, ALU.min)
                dve.tensor_tensor(out=back, in0=runs_ps, in1=back, op=ALU.subtract).then_inc(shifted, 1)

                dve.reg_load(regs[0], k["base_sb"][0:1, bass.DynSlice(s * CHUNK_GROUPS, 1)])
                first = dve.snap(regs[0], min_val=0, max_val=NODES)
                dve.wait_ge(exT_done, s + 1)
                column = k["sumT"][:, bass.DynSlice(first, 1)]
                dve.tensor_tensor(out=column, in0=column, in1=small_ps[:, 404:405], op=ALU.mult)
                column = k["denT"][:, bass.DynSlice(first, 1)]
                dve.tensor_tensor(out=column, in0=column, in1=small_ps[0:PARTS * HEADS0, 406:407], op=ALU.mult)

                wait_here(dve, ex_copied, s + 1, dve_gate)
                rest = ahead.rearrange("p (t h) -> p t h", h=HEADS0)
                of = ex.rearrange("p h t -> p t h")
                for part in range(PARTS):
                    if part:
                        dve.drain()
                        dve.tensor_tensor(out=rest, in0=of, in1=ex_parts[:, :, part - 1, :], op=ALU.subtract)
                        dve.drain()
                        of = rest
                    dve.tensor_copy(ex_parts[:, :, part, :], of)

            def make(u, s, tile):
                dve.tensor_tensor(out=onehot[u], in0=k["iota_pass"].unsqueeze(1).to_broadcast([P, GROUP, P]),
                                  in1=k["drel"][:, bass.DynSlice(s * CHUNK_TILES + tile, GROUP)].unsqueeze(2)
                                  .to_broadcast([P, GROUP, P]), op=ALU.is_equal).then_inc(onehot_made, 1)
                dve.tensor_tensor(
                    out=message[u].rearrange("p t (h f) -> p t h f", h=HEADS0),
                    in0=x_rows[:, bass.DynSlice((s % 2) * CHUNK_TILES + tile, GROUP), 0:FEAT]
                    .rearrange("p t (h f) -> p t h f", h=HEADS0),
                    in1=ex[:, :, bass.DynSlice(tile, GROUP)].rearrange("p h t -> p t h").unsqueeze(3)
                    .to_broadcast([P, GROUP, HEADS0, FEAT // HEADS0]),
                    op=ALU.mult).then_inc(msg_made, 1)

            def add(u, start, group):
                dve.wait_ge(summed, group + 3)
                for sums, part in ((k["sumT"], sum_ps[u]), (k["denT"], den_ps[u])):
                    window = sums[:, bass.DynSlice(start, P)]
                    dve.tensor_tensor(out=window, in0=window, in1=part, op=ALU.add)

            def messages(s, groups, more):
                first_pass()
                with dve.Fori(0, passes) as r:
                    def pair(g, first):
                        v = dve.snap(c_visit)
                        d = dve.snap(d_visit)
                        tile = 2 * g * GROUP
                        starts = window_starts(dve, regs, k["base_sb"], s * CHUNK_GROUPS + 2 * g, r)
                        make(0, s, tile)
                        if more:
                            scores_onehot(0, d, (s + 1) * CHUNK_GROUPS + 2 * g)
                        else:
                            dve.drain()
                        if not first:
                            add(1, dve.snap(before, min_val=0, max_val=NODES), 2 * v - 1)
                        make(1, s, tile + GROUP)
                        if more:
                            scores_onehot(1, d, (s + 1) * CHUNK_GROUPS + 2 * g + 1)
                        else:
                            dve.drain()
                        dve.reg_mov(before, starts[1])
                        add(0, starts[0], 2 * v)
                        dve.reg_add(c_visit, c_visit, 1)
                        if more:
                            dve.reg_add(d_visit, d_visit, 1)

                    pair(0, True)
                    with dve.Fori(1, groups // 2) as g:
                        pair(g, False)
                    dve.drain()
                    add(1, dve.snap(before, min_val=0, max_val=NODES), 2 * dve.snap(c_visit) - 1)
                    next_pass()
                dve.drain().then_inc(rows_released, 1)

            first_pass()
            with dve.Fori(0, passes) as r:
                with dve.Fori(0, HALF) as g:
                    v = dve.snap(d_visit)
                    for u in range(2):
                        scores_onehot(u, v, 2 * g + u)
                    dve.reg_add(d_visit, d_visit, 1)
                next_pass()
            with dve.Fori(0, CHUNKS - 1) as s:
                maxima(s)
                messages(s, CHUNK_GROUPS, True)
            maxima(CHUNKS - 1)
            messages(CHUNKS - 1, LAST_GROUPS, False)


def between(nc, S, sb, shared):
    k = shared
    B = BATCH * FEAT
    DEN = PARTS * HEADS0
    cut = [0]

    def part(cols):
        cut[0] += cols
        return k["ring"][:, cut[0] - cols:cut[0]]

    rows_sb = part(3 * FEAT)
    bias, gamma, beta = (rows_sb[:, i * FEAT:(i + 1) * FEAT].unsqueeze(1).to_broadcast([P, BATCH, FEAT])
                         for i in range(3))
    w_sb = part(3 * FEAT)
    x_in, x_bias, sT, y, x1s, x1T = ([part(B) for _ in range(2)] for _ in range(6))
    dT = [part(B)[0:DEN, :] for _ in range(2)]
    low = part(B)
    qkv = [part(3 * B).rearrange("p (b w) -> p b w", b=BATCH) for _ in range(2)]
    rden = part(BATCH * HEADS0)
    blocks = lambda t: t.rearrange("p (b w) -> p b w", b=BATCH)
    stats = [blocks(part(6 * BATCH)) for _ in range(2)]
    mv = [blocks(part(2 * BATCH)) for _ in range(2)]
    rstd = [part(BATCH) for _ in range(2)]
    half_neg = part(BATCH)
    assert cut[0] <= 2 * CHUNK_TILES * XROW - NODE_ROWS
    x1 = k["ring"][:, 2 * CHUNK_TILES * XROW - NODE_ROWS:]

    turned_ps = [k["psum"][:, 2 * 512:4 * 512], k["wide"][0]]
    y_ps = [t[:, 0:B] for t in turned_ps]
    dn_ps = [t[:, B:B + BATCH * DEN] for t in turned_ps]
    x1T_ps = k["wide"][1][:, 0:B]

    w_in = S("w_in")
    xb_in = [S(f"xb_in{i}") for i in range(2)]
    bias_added = S("bias_added")
    x_used = S("x_used")
    sums_copied = S("sums_copied")
    sums_turned = S("sums_turned")
    sums_used = S("sums_used")
    low_made = S("low_made")
    var_made = S("var_made")
    rstd_made = S("rstd_made")
    low_exp = S("low_exp")
    x1_made = S("x1_made")
    x1_turned = S("x1_turned")
    x1_kept = S("x1_kept")
    x1T_copied = S("x1T_copied")
    qkv_made = S("qkv_made")
    qkv_copied = S("qkv_copied")
    qkv_out = [S(f"qkv_out{i}") for i in range(2)]

    with nc.Block() as block:
        @block.sync
        def _(sp):
            sp.dma_start(rows_sb, k["rows"]).then_inc(w_in, 16)
            for u in range(2):
                sp.dma_start(blocks(x_in[u]), k["xpad"][u * BATCH * P:(u + 1) * BATCH * P, :]
                             .rearrange("(b p) f -> p b f", p=P)).then_inc(xb_in[u], 16)
            sp.dma_start(w_sb, k["wqkvT"]).then_inc(w_in, 16)

            def batch(u, n, more):
                nodes = bass.DynSlice(n * BATCH * P, BATCH * P)
                if more:
                    sp.wait_ge(x_used, n + 1)
                    sp.dma_start(blocks(x_in[u]), k["xpad"][bass.DynSlice((n + 2) * (BATCH * P), BATCH * P), :]
                                 .rearrange("(b p) f -> p b f", p=P)).then_inc(xb_in[u], 16)
                sp.wait_ge(qkv_copied, BATCH * (n + 1) + 2)
                sp.dma_start(k["q_table"][nodes, :].rearrange("(b p) f -> p b f", p=P), qkv[u][:, :, 0:FEAT])\
                  .then_inc(qkv_out[u], 16)
                sp.dma_start(k["kv_table"][nodes, :].rearrange("(b p) f -> p b f", p=P), qkv[u][:, :, FEAT:])\
                  .then_inc(qkv_out[u], 16)

            with sp.Fori(0, BATCHES // 2 - 1) as i:
                for u in range(2):
                    batch(u, 2 * i + u, True)
            for u in range(2):
                batch(u, BATCHES - 2 + u, False)
            for u in range(2):
                sp.wait_ge(qkv_out[u], 32 * (BATCHES // 2))

        @block.gpsimd
        def _(pool):
            pool.memset(half_neg, -0.5)
            pool.drain()
            pool.wait_ge(w_in, 32)

            def add_bias(u, nth):
                pool.wait_ge(xb_in[u], 16 * (nth + 1))
                pool.tensor_tensor(out=blocks(x_bias[u]), in0=blocks(x_in[u]), in1=bias, op=ALU.add)\
                    .then_inc(bias_added, 1)

            def power(which, nth):
                pool.wait_ge(var_made, nth)
                pool.tensor_tensor(out=rstd[which], in0=rstd[which], in1=half_neg, op=ALU.pow).then_inc(rstd_made, 1)

            for u in range(2):
                add_bias(u, 0)
            power(0, 1)
            with pool.Fori(0, BATCHES // 2 - 1) as i:
                for u in range(2):
                    n = 2 * i + u
                    power(0, 2 * n + 2)
                    power(1, 2 * n + 3)
                    add_bias(u, i + 1)
            power(0, 2 * BATCHES - 2)
            power(1, 2 * BATCHES - 1)
            power(1, 2 * BATCHES)

        @block.tensor
        def _(pe):
            def turn_sums(u, n):
                pe.wait_ge(sums_copied, n + 1)
                pe.wait_ge(sums_used, n + 1)
                for b in range(BATCH):
                    pe.transpose(y_ps[u][:, b * P:(b + 1) * P], sT[u][:, b * P:(b + 1) * P], k["ident_sb"])
                for b in range(BATCH):
                    last = pe.transpose(dn_ps[u][:, b * DEN:(b + 1) * DEN], dT[u][:, b * P:(b + 1) * P],
                                        k["ident_sb"][0:DEN, 0:DEN])
                last.then_inc(sums_turned, 1)

            def products(u, n):
                pe.wait_ge(x1_made, n + 1)
                for b in range(BATCH):
                    last = pe.transpose(x1T_ps[:, b * P:(b + 1) * P], x1s[u][:, b * P:(b + 1) * P], k["ident_sb"])
                last.then_inc(x1_turned, 1)
                pe.wait_ge(x1T_copied, n + 1)
                for b in range(BATCH):
                    pe.wait_ge(qkv_copied, BATCH * n + b + 1)
                    pe.matmul(k["bank"][b % 2 if u == 0 else (b + 1) % 2][:, 0:3 * FEAT], x1T[u][:, b * P:(b + 1) * P],
                              w_sb, start=True, stop=True).then_inc(qkv_made, 1)

            for u in range(2):
                turn_sums(u, u)
            pe.wait_ge(w_in, 32)
            with pe.Fori(0, BATCHES // 2 - 1) as i:
                for u in range(2):
                    turn_sums(u, 2 * i + u + 2)
                    products(u, 2 * i + u)
            for u in range(2):
                products(u, BATCHES - 2 + u)

        @block.scalar
        def _(act):
            def copy_sums(u, n):
                nodes = bass.DynSlice(n * B, B)
                act.activation(sT[u], k["sumT"][:, nodes], ACT.Copy)
                act.activation(dT[u], k["denT"][:, nodes], ACT.Copy).then_inc(sums_copied, 1)

            def exponentials(n):
                act.wait_ge(low_made, n + 1)
                act.activation(low, low, ACT.Exp).then_inc(low_exp, 1)

            def batch(u, n, times_written, ahead):
                if ahead >= 1:
                    exponentials(n + 1)
                if ahead >= 3:
                    act.wait_ge(sums_turned, n + 2)
                    copy_sums(1 - u, n + 3)
                act.wait_ge(x1_turned, n + 1)
                act.activation(x1T[u], x1T_ps, ACT.Copy).then_inc(x1T_copied, 1)
                if times_written is not None:
                    act.wait_ge(qkv_out[u], 32 * times_written)
                for b in range(BATCH):
                    act.wait_ge(qkv_made, BATCH * n + b + 1)
                    act.activation(qkv[u][:, b, :], k["bank"][b % 2 if u == 0 else (b + 1) % 2][:, 0:3 * FEAT],
                                   ACT.Copy).then_inc(qkv_copied, 1)
                act.activation(x1[:, bass.DynSlice(n * B, B)], x1s[u], ACT.Copy).then_inc(x1_kept, 1)

            for u in range(2):
                copy_sums(u, u)
            act.wait_ge(sums_turned, 1)
            copy_sums(0, 2)
            exponentials(0)
            for u in range(2):
                batch(u, u, None, 3)
            with act.Fori(1, BATCHES // 2 - 2) as i:
                for u in range(2):
                    batch(u, 2 * i + u, i, 3)
            for n in range(BATCHES - 4, BATCHES):
                batch(n % 2, n, n // 2, min(3, BATCHES - 1 - n))

        @block.vector
        def _(dve):
            dve.sem_inc(sums_used, 2)
            dve.sem_inc(x1_kept, 2)
            dve.sem_inc(qkv_copied, 2)

            def first_sums(u, n):
                dve.wait_ge(sums_turned, n + 1)
                dve.tensor_reduce(out=rden.rearrange("p (b h) -> p b h", h=HEADS0),
                                  in_=dn_ps[u].rearrange("p (b s h) -> p b h s", s=PARTS, h=HEADS0),
                                  axis=AX.X, op=ALU.add)
                dve.drain()
                dve.tensor_scalar(rden, rden, 1e-16, None, ALU.add)
                dve.drain()
                dve.reciprocal(rden, rden)
                dve.drain()
                dve.tensor_tensor(out=y[u].rearrange("p (q f) -> p q f", f=FEAT // HEADS0),
                                  in0=y_ps[u].rearrange("p (q f) -> p q f", f=FEAT // HEADS0),
                                  in1=rden.unsqueeze(2).to_broadcast([P, BATCH * HEADS0, FEAT // HEADS0]),
                                  op=ALU.mult).then_inc(sums_used, 1)
                dve.drain()
                dve.wait_ge(bias_added, n + 1)
                dve.tensor_tensor(out=y[u], in0=y[u], in1=x_bias[u], op=ALU.add)
                spread(dve, blocks(y[u]), stats[0], mv[0], rstd[0], var_made)

            def first_norm(u, n, nth):
                dve.wait_ge(rstd_made, nth)
                scale(dve, blocks(y[u]), blocks(y[u]), mv[0], rstd[0])
                dve.drain()
                dve.tensor_tensor(out=blocks(y[u]), in0=blocks(y[u]), in1=gamma, op=ALU.mult)
                dve.drain()
                dve.tensor_tensor(out=blocks(y[u]), in0=blocks(y[u]), in1=beta, op=ALU.add)
                dve.drain()
                dve.tensor_scalar(low, y[u], 0.0, None, ALU.min).then_inc(low_made, 1)

            def second_sums(u, n):
                dve.wait_ge(low_exp, n + 1)
                dve.scalar_tensor_tensor(out=y[u], in0=y[u], scalar=0.0, in1=low, op0=ALU.max, op1=ALU.add)
                dve.drain()
                dve.scalar_tensor_tensor(out=y[u], in0=y[u], scalar=-1.0, in1=x_in[u], op0=ALU.add, op1=ALU.add)\
                   .then_inc(x_used, 1)
                spread(dve, blocks(y[u]), stats[1], mv[1], rstd[1], var_made)

            def second_norm(u, n, nth):
                dve.wait_ge(rstd_made, nth)
                dve.wait_ge(x1_kept, n + 1)
                scale(dve, blocks(x1s[u]), blocks(y[u]), mv[1], rstd[1]).then_inc(x1_made, 1)

            def step(u, n):
                first_sums(1 - u, n + 1)
                second_sums(u, n)
                first_norm(1 - u, n + 1, 2 * n + 2)
                second_norm(u, n, 2 * n + 3)

            first_sums(0, 0)
            first_norm(0, 0, 1)
            with dve.Fori(0, BATCHES // 2 - 1) as i:
                for u in range(2):
                    step(u, 2 * i + u)
            step(0, BATCHES - 2)
            second_sums(1, BATCHES - 1)
            second_norm(1, BATCHES - 1, 2 * BATCHES)


def spread(dve, y, stats, mv, rstd, var_made):
    dve.drain()
    for b in range(BATCH):
        dve.bn_stats(stats[:, b, :], y[:, b, :])
    dve.drain()
    for b in range(BATCH):
        dve.bn_aggr(mv[:, b, :], stats[:, b, :])
    dve.drain()
    dve.tensor_scalar(rstd, mv[:, :, 1], LN_EPS, None, ALU.add).then_inc(var_made, 1)


def scale(dve, out, y, mv, rstd):
    for b in range(BATCH):
        last = dve.tensor_scalar(out[:, b, :], y[:, b, :], mv[:, b, 0:1], rstd[:, b:b + 1], ALU.subtract, ALU.mult)
    return last


def norm(dve, out, y, stats, mv, rstd, var_made, rstd_made, nth, out_free=None):
    dve.drain()
    for b in range(BATCH):
        dve.bn_stats(stats[:, b, :], y[:, b, :])
    dve.drain()
    for b in range(BATCH):
        dve.bn_aggr(mv[:, b, :], stats[:, b, :])
    dve.drain()
    dve.tensor_scalar(rstd, mv[:, :, 1], LN_EPS, None, ALU.add).then_inc(var_made, 1)
    dve.wait_ge(rstd_made, nth + 1)
    if out_free is not None:
        dve.wait_ge(*out_free)
    for b in range(BATCH):
        last = dve.tensor_scalar(out[:, b, :], y[:, b, :], mv[:, b, 0:1], rstd[:, b:b + 1], ALU.subtract, ALU.mult)
    return last


def layer1(nc, S, sb, shared):
    k = shared
    GP = GROUP * P
    SLOTS = 4
    cut = [0]

    def part(cols):
        cut[0] += cols
        return k["ring"][:, cut[0] - cols:cut[0]]

    tiles3 = lambda t: t.rearrange("p (t n) -> p t n", t=GROUP)
    kv = [tiles3(part(2 * GP)) for _ in range(SLOTS)]
    w = [tiles3(part(GP)) for _ in range(SLOTS)]
    q_win = [part(FEAT) for _ in range(SLOTS)]
    prod = tiles3(part(GP))
    message = [tiles3(part(GP)) for _ in range(2)]
    idx = [part(GROUP).bitcast(I32) for _ in range(SLOTS)]
    alpha = part(GROUP * HEADS1)
    edge_w = part(GROUPS1 * GROUP)
    assert cut[0] <= 2 * CHUNK_TILES * XROW - NODE_ROWS
    onehot = [tiles3(k["work"][:, u * GP:(u + 1) * GP]) for u in range(SLOTS)]
    onehotT = k["work"][:, 4 * GP:5 * GP]
    sum_ps = [k["bank"][u][:, 0:P] for u in range(2)]
    T_ps = k["wide"][0]
    q_ps = [k["psum"][:, 2 * 512:4 * 512], k["wide"][1]]

    edge_w_in = S("edge_w_in")
    idx_in = [S(f"idx1_in{i}") for i in range(SLOTS)]
    kv_in = [S(f"kv_in{i}") for i in range(SLOTS)]
    w_in = [S(f"w1_in{i}") for i in range(SLOTS)]
    q_in = [S(f"q_in{i}") for i in range(SLOTS)]
    kv_ready = S("kv_ready")
    onehot_made = S("onehot1_made")
    onehot_turned = S("onehot1_turned")
    onehotT_made = S("onehot1T_made")
    q_spread = S("q_spread")
    q_used = S("q_used")
    msg_made = S("msg1_made")
    summed = S("summed1")
    pool_gate = S("pool1_gate")
    ROUNDS = GROUPS1 // SLOTS

    def absolute(eng, round_reg):
        return eng.snap(round_reg) * SLOTS

    with nc.Block() as block:
        @block.sync
        def _(sp):
            passes = sp.value_load(k["passes_sb"][0:1, 0:1], min_val=1, max_val=NODE_BLOCKS)
            rounds = counter(sp, "sp_rounds1")
            regs = [sp.alloc_register(f"sp_base1{u}") for u in range(SLOTS)]
            sp.dma_start(edge_w, k["ew"]).then_inc(edge_w_in, 16)
            with sp.Fori(0, passes) as r:
                with sp.Fori(0, ROUNDS) as i:
                    n0 = absolute(sp, rounds)
                    starts = window_starts(sp, regs, k["base_sb"], SLOTS * i, r)
                    for j in range(SLOTS):
                        sp.wait_ge(msg_made, n0 + j + 1)
                        sp.dma_start(idx[j], k["src_idx1"][bass.DynSlice(SLOTS * i + j, 1), :, :]
                                     .rearrange("o p n -> (o p) n")).then_inc(idx_in[j], 16)
                        sp.dma_start(q_win[j], k["q_table"][bass.DynSlice(starts[j], P), :]).then_inc(q_in[j], 16)
                        sp.dma_start(w[j], k["ea"][bass.DynSlice((SLOTS * i + j) * GP, GP), :]
                                     .rearrange("(t p) f -> p t f", p=P)).then_inc(w_in[j], 16)
                    sp.reg_add(rounds, rounds, 1)

        @block.gpsimd
        def _(pool):
            passes = pool.value_load(k["passes_sb"][0:1, 0:1], min_val=1, max_val=NODE_BLOCKS)
            rounds = counter(pool, "pool_rounds1")
            full_rounds = counter(pool, "pool_full_rounds1")
            LAST_ROUND = GATHERED1 - (GROUPS1 - SLOTS)
            LAG = 3

            def one_round(groups, first):
                nth, nth_full = pool.snap(rounds), pool.snap(full_rounds)
                for j in range(groups):
                    wait_here(pool, msg_made, nth * SLOTS + j + 1, pool_gate)
                    wait_here(pool, idx_in[j], 16 * (nth + 1), pool_gate)
                    for t in range(GROUP):
                        pool.indirect_dma_start(kv[j][:, t, :], None, k["kv_table"],
                                                bass.IndirectOffsetOnAxis(idx[j][:, t:t + 1], 0))\
                            .then_inc(kv_in[j], 16)
                        if t == LAG and (j or not first):
                            arrived((j - 1) % SLOTS, nth_full if j == 0 else (nth if j <= LAST_ROUND else nth_full) + 1)
                pool.reg_add(rounds, rounds, 1)

            def arrived(j, times):
                wait_here(pool, kv_in[j], times * (16 * GROUP), pool_gate)
                pool.sem_inc(kv_ready, 1)

            with pool.Fori(0, passes) as r:
                one_round(SLOTS, True)
                pool.reg_add(full_rounds, full_rounds, 1)
                with pool.Fori(1, ROUNDS - 1) as i:
                    one_round(SLOTS, False)
                    pool.reg_add(full_rounds, full_rounds, 1)
                one_round(LAST_ROUND, False)
                arrived(LAST_ROUND - 1, pool.snap(rounds))
                pool.sem_inc(kv_ready, GROUPS1 - GATHERED1)

        @block.tensor
        def _(pe):
            passes = pe.value_load(k["passes_sb"][0:1, 0:1], min_val=1, max_val=NODE_BLOCKS)
            rounds = counter(pe, "pe_rounds1")

            def turn(n, j):
                pe.wait_ge(onehot_made, n + 1)
                for t in range(GROUP):
                    last = pe.transpose(T_ps[:, t * P:(t + 1) * P], onehot[j][:, t, :], k["ident_sb"])
                last.then_inc(onehot_turned, 1)

            def spread(n, j, nth):
                pe.wait_ge(onehotT_made, n + 1)
                pe.wait_ge(q_in[j], 16 * (nth + 1))
                pe.wait_ge(q_used, n + 1)
                for t in range(GROUP):
                    last = pe.matmul(q_ps[j % 2][:, t * P:(t + 1) * P], onehotT[:, t * P:(t + 1) * P], q_win[j],
                                     start=True, stop=True)
                last.then_inc(q_spread, 1)

            def sums(n, j):
                pe.wait_ge(msg_made, n + SLOTS + 1)
                for t in range(GROUP):
                    last = pe.matmul(sum_ps[j % 2], message[j % 2][:, t, :], onehot[j][:, t, :],
                                     start=t == 0, stop=t == GROUP - 1)
                last.then_inc(summed, 1)

            def one_round(last_round):
                nth = pe.snap(rounds)
                n0 = nth * SLOTS
                for j in range(SLOTS):
                    more = not last_round or j + 2 < SLOTS
                    if more:
                        turn(n0 + j + 2, (j + 2) % SLOTS)
                        spread(n0 + j + 2, (j + 2) % SLOTS, nth if j < 2 else nth + 1)
                    sums(n0 + j, j)
                pe.reg_add(rounds, rounds, 1)

            with pe.Fori(0, passes) as r:
                nth = pe.snap(rounds)
                for j in range(2):
                    turn(nth * SLOTS + j, j)
                    spread(nth * SLOTS + j, j, nth)
                with pe.Fori(0, ROUNDS - 1) as i:
                    one_round(False)
                one_round(True)

        @block.scalar
        def _(act):
            passes = act.value_load(k["passes_sb"][0:1, 0:1], min_val=1, max_val=NODE_BLOCKS)
            group = counter(act, "act_group1")
            with act.Fori(0, passes) as r:
                with act.Fori(0, GROUPS1) as i:
                    n = act.snap(group)
                    act.wait_ge(onehot_turned, n + 1)
                    act.wait_ge(q_spread, n + 1)
                    act.activation(onehotT, T_ps, ACT.Copy).then_inc(onehotT_made, 1)
                    act.reg_add(group, group, 1)

        @block.vector
        def _(dve):
            passes = dve.value_load(k["passes_sb"][0:1, 0:1], min_val=1, max_val=NODE_BLOCKS)
            rounds = counter(dve, "dve_rounds1")
            regs = [dve.alloc_register(f"dve_base1{u}") for u in range(SLOTS)]
            before = dve.alloc_register("dve_base_before1")
            for credit, n in ((q_spread, 1), (q_used, 2), (msg_made, SLOTS)):
                dve.sem_inc(credit, n)
            dve.memset(k["sumT"], 0.0)
            dve.tensor_copy(k["iota_pass"], k["iota_sb"])
            dve.drain()
            dve.wait_ge(edge_w_in, 16)

            def make_onehot(i, j):
                dve.tensor_tensor(out=onehot[j], in0=k["iota_pass"].unsqueeze(1).to_broadcast([P, GROUP, P]),
                                  in1=k["drel"][:, bass.DynSlice(i * GROUP, GROUP)].unsqueeze(2)
                                  .to_broadcast([P, GROUP, P]), op=ALU.is_equal).then_inc(onehot_made, 1)

            def messages(i, n, j, nth):
                dve.wait_ge(w_in[j], 16 * (nth + 1))
                dve.wait_ge(kv_ready, n + 1)
                dve.tensor_tensor(out=prod, in0=kv[j][:, :, 0:FEAT], in1=w[j], op=ALU.mult)
                dve.drain()
                dve.wait_ge(q_spread, n + 2)
                dve.tensor_tensor(out=prod, in0=prod, in1=tiles3(q_ps[j % 2]), op=ALU.mult).then_inc(q_used, 1)
                dve.drain()
                dve.tensor_reduce(out=alpha, in_=prod.rearrange("p t (h d) -> p (t h) d", h=HEADS1),
                                  axis=AX.X, op=ALU.add)
                dve.drain()
                by_tile = alpha.rearrange("p (t h) -> p t h", h=HEADS1)
                dve.scalar_tensor_tensor(
                    out=by_tile, in0=by_tile, scalar=(FEAT // HEADS1) ** -0.5,
                    in1=edge_w[:, bass.DynSlice(i * GROUP, GROUP)].unsqueeze(2).to_broadcast([P, GROUP, HEADS1]),
                    op0=ALU.mult, op1=ALU.mult)
                dve.drain()
                dve.tensor_tensor(
                    out=message[j % 2].rearrange("p t (h d) -> p t h d", h=HEADS1),
                    in0=kv[j][:, :, FEAT:].rearrange("p t (h d) -> p t h d", h=HEADS1),
                    in1=by_tile.unsqueeze(3).to_broadcast([P, GROUP, HEADS1, FEAT // HEADS1]),
                    op=ALU.mult).then_inc(msg_made, 1)

            def add(n, j, start):
                dve.wait_ge(summed, n + 1)
                window = k["sumT"][:, bass.DynSlice(start, P)]
                dve.tensor_tensor(out=window, in0=window, in1=sum_ps[j % 2], op=ALU.add)

            def one_round(i, first, last_round, r):
                nth = dve.snap(rounds)
                n0 = nth * SLOTS
                starts = window_starts(dve, regs, k["base_sb"], SLOTS * i, r)
                for j in range(SLOTS):
                    if not last_round or j + 2 < SLOTS:
                        make_onehot(SLOTS * i + j + 2, (j + 2) % SLOTS)
                    messages(SLOTS * i + j, n0 + j, j, nth)
                    if j:
                        add(n0 + j - 1, j - 1, starts[j - 1])
                    elif not first:
                        add(n0 - 1, SLOTS - 1, dve.snap(before, min_val=0, max_val=NODES))
                dve.reg_mov(before, starts[-1])
                dve.reg_add(rounds, rounds, 1)

            with dve.Fori(0, passes) as r:
                for j in range(2):
                    make_onehot(j, j)
                one_round(0, True, False, r)
                with dve.Fori(1, ROUNDS - 1) as i:
                    one_round(i, False, False, r)
                one_round(ROUNDS - 1, False, True, r)
                dve.drain()
                add(dve.snap(rounds) * SLOTS - 1, SLOTS - 1, dve.snap(before, min_val=0, max_val=NODES))
                dve.drain()
                dve.tensor_scalar(k["iota_pass"], k["iota_pass"], float(P), None, ALU.add)
                dve.drain()


def final(nc, S, sb, shared):
    k = shared
    B = BATCH * FEAT
    sT = [k["ring"][:, u * B:(u + 1) * B] for u in range(2)]
    y = [k["ring"][:, (2 + u) * B:(3 + u) * B] for u in range(2)]
    o = [k["ring"][:, (4 + u) * B:(5 + u) * B].rearrange("p (b f) -> p b f", b=BATCH) for u in range(2)]
    at = 6 * B
    stats = k["ring"][:, at:at + 6 * BATCH].rearrange("p (b w) -> p b w", b=BATCH)
    mv = k["ring"][:, at + 32:at + 32 + 2 * BATCH].rearrange("p (b w) -> p b w", b=BATCH)
    rstd = k["ring"][:, at + 48:at + 48 + BATCH]
    half_neg = k["ring"][:, at + 56:at + 56 + BATCH]
    x1 = k["ring"][:, 2 * CHUNK_TILES * XROW - NODE_ROWS:]
    copied = S("copied2")
    turned = S("turned2")
    added = S("added2")
    made = S("made2")
    var_made = S("var2_made")
    rstd_made = S("rstd2_made")
    written = [S(f"written{i}") for i in range(2)]

    with nc.Block() as block:
        @block.scalar
        def _(act):
            with act.Fori(0, BATCHES // 2) as i:
                for u in range(2):
                    n = 2 * i + u
                    act.wait_ge(added, n + 1)
                    act.activation(sT[u], k["sumT"][:, bass.DynSlice(n * B, B)], ACT.Copy).then_inc(copied, 1)

        @block.gpsimd
        def _(pool):
            pool.memset(half_neg, -0.5)
            pool.drain()
            with pool.Fori(0, BATCHES) as i:
                pool.wait_ge(var_made, i + 1)
                pool.tensor_tensor(out=rstd, in0=rstd, in1=half_neg, op=ALU.pow).then_inc(rstd_made, 1)

        @block.tensor
        def _(pe):
            with pe.Fori(0, BATCHES // 2) as i:
                for u in range(2):
                    pe.wait_ge(copied, 2 * i + u + 1)
                    for b in range(BATCH):
                        last = pe.transpose(k["wide"][u][:, b * P:(b + 1) * P], sT[u][:, b * P:(b + 1) * P], k["ident_sb"])
                    last.then_inc(turned, 1)

        @block.vector
        def _(dve):
            dve.sem_inc(added, 2)

            def batch(u, n, times_written):
                dve.wait_ge(turned, n + 1)
                dve.tensor_tensor(out=y[u], in0=k["wide"][u][:, 0:B], in1=x1[:, bass.DynSlice(n * B, B)], op=ALU.add)\
                   .then_inc(added, 1)
                free = None if times_written is None else (written[u], 16 * times_written)
                norm(dve, o[u], y[u].rearrange("p (b f) -> p b f", b=BATCH), stats, mv, rstd,
                     var_made, rstd_made, n, free).then_inc(made, 1)

            for u in range(2):
                batch(u, u, None)
            with dve.Fori(1, BATCHES // 2) as i:
                for u in range(2):
                    batch(u, 2 * i + u, i)

        @block.sync
        def _(sp):
            with sp.Fori(0, BATCHES // 2) as i:
                for u in range(2):
                    n = 2 * i + u
                    sp.wait_ge(made, n + 1)
                    sp.dma_start(k["out"][bass.DynSlice(n * BATCH * P, BATCH * P), :].rearrange("(b p) f -> p b f", p=P),
                                 o[u]).then_inc(written[u], 16)
            for u in range(2):
                sp.wait_ge(written[u], 16 * (BATCHES // 2))


def kernel(x, src, dst, edge_attr_128, edge_attr_16, edge_weight1, L0_gnn_W_lin, L0_gnn_W_edge,
           L0_gnn_att_src, L0_gnn_att_dst, L0_gnn_att_edge, L0_gnn_bias, L0_gnn_ln_gamma, L0_gnn_ln_beta,
           L1_gnn_Wq, L1_gnn_Wk, L1_gnn_Wv):
    import concourse.bacc as bacc
    from concourse.bass_utils import run_bass_kernel_spmd

    f32, i32 = np.float32, np.int32
    x = np.asarray(x)
    src, dst = np.asarray(src).astype(i32), np.asarray(dst).astype(i32)
    slots = TILES0 * P
    src_p = np.concatenate([src, np.zeros(slots - EDGES, i32)])
    dst_p = np.concatenate([dst, np.full(slots - EDGES, NODES, i32)])
    slots1 = slots
    ea = np.concatenate([np.asarray(edge_attr_128), np.zeros((slots1 - EDGES, FEAT), f32)])
    ea16 = np.concatenate([np.asarray(edge_attr_16), np.zeros((slots - EDGES, EDGE_DIM), f32)])
    ew = np.concatenate([np.asarray(edge_weight1)[:, 0], np.zeros(slots1 - EDGES, f32)])
    xpad = np.concatenate([x, np.zeros((NODE_ROWS - NODES, FEAT), f32)])

    per_chunk = dst_p.reshape(CHUNKS, RUNS, RUN)
    around = np.concatenate([np.array([-1], i32), dst_p, np.array([-1], i32)])
    runs = np.stack([around[n * RUN:n * RUN + RUN + 2] for n in range(CHUNKS * RUNS)])
    dst_runs = np.tile(runs.reshape(CHUNKS, 1, RUNS, RUN + 2), (1, HEADS0, 1, 1)).reshape(CHUNKS, P, RUN + 2)
    group_ends = dst_p.reshape(GROUPS0, GROUP * P)

    def by_head(vector):
        v = np.asarray(vector).reshape(HEADS0, -1)
        m = np.zeros((HEADS0, v.shape[1], HEADS0), f32)
        for h in range(HEADS0):
            m[h, :, h] = v[h]
        return m.reshape(-1, HEADS0)

    sel4 = np.zeros((P, HEADS0), f32)
    sel4[np.arange(HEADS0) * RUNS, np.arange(HEADS0)] = 1
    arrays = {
        "xT": xpad.T, "xpad": xpad,
        "src_idx0": src_p.reshape(CHUNKS, CHUNK_TILES, P).transpose(0, 2, 1),
        "src_idx1": src_p[:slots1].reshape(GROUPS1, GROUP, P).transpose(0, 2, 1),
        "dst_tile": dst_p.reshape(TILES0, P).T,
        "dst_runs": dst_runs,
        "base_rep": np.broadcast_to(group_ends[:, 0], (P, GROUPS0)),
        "last_rep": np.broadcast_to(group_ends[:, -1], (P, GROUPS0)),
        "base_row": group_ends[:, 0].reshape(1, GROUPS0),
        "dst_row": dst_p.reshape(1, -1),
        "ea_turned": ea16.reshape(GROUPS0, GROUP, P, EDGE_DIM).transpose(0, 1, 3, 2).reshape(GROUPS0, P, P),
        "ea": ea, "ew": ew.reshape(GROUPS1 * GROUP, P).T,
        "w_linT": np.asarray(L0_gnn_W_lin).T, "w_lin": np.asarray(L0_gnn_W_lin),
        "att": np.concatenate([by_head(L0_gnn_att_dst), by_head(L0_gnn_att_src)], axis=1),
        "w_edge": np.tile(np.asarray(L0_gnn_W_edge), (1, GROUP)), "att_edge": by_head(L0_gnn_att_edge),
        "wqkvT": np.concatenate([np.asarray(m).T for m in (L1_gnn_Wq, L1_gnn_Wk, L1_gnn_Wv)], axis=1),
        "rows": np.broadcast_to(np.concatenate([np.asarray(v) for v in (L0_gnn_bias, L0_gnn_ln_gamma, L0_gnn_ln_beta)]),
                                (P, 3 * FEAT)),
        "ident": np.eye(P, dtype=f32),
        "node_of": np.arange(P, dtype=f32).reshape(P, 1),
        "own_tile": np.kron(np.eye(GROUP, dtype=f32), np.ones((EDGE_DIM, HEADS0), f32)),
        "iota": np.broadcast_to(np.arange(P, dtype=f32), (P, P)),
        "sel": np.repeat(sel4, FEAT // HEADS0, axis=1),
        "sel_parts": np.tile(sel4, (1, PARTS)),
    }
    arrays = {name: np.ascontiguousarray(a) for name, a in arrays.items()}
    nc = bacc.Bacc("TRN2", target_bir_lowering=False, num_devices=1)
    args = {name: nc.dram_tensor(f"{name}_dram", list(a.shape), mybir.dt.from_np(a.dtype), kind="ExternalInput").ap()
            for name, a in arrays.items()}
    args["out"] = nc.dram_tensor("out_dram", [NODE_ROWS, FEAT], F32, kind="ExternalOutput").ap()
    program(nc, **args)
    r = run_bass_kernel_spmd(nc, [{f"{name}_dram": a for name, a in arrays.items()}], core_ids=[0])
    return r.results[0]["out_dram"][:NODES]
```

```python
import numpy as np
import concourse.bass as bass
from concourse import mybir

F32 = mybir.dt.float32
BF16 = mybir.dt.bfloat16
I32 = mybir.dt.int32
ALU = mybir.AluOpType
ACT = mybir.ActivationFunctionType
AX = mybir.AxisListType

P = 128
NODES, FEAT = 6250, 128
EDGES = 206250
HEADS0, HEADS1 = 4, 8
EDGE_DIM = 16
GROUP = 8
CHUNK_GROUPS = 12
CHUNK_TILES = GROUP * CHUNK_GROUPS
RUNS = P // HEADS0
RUN = CHUNK_TILES * P // RUNS
RUN_TILES = RUN // P
TILES = -(-EDGES // P)
CHUNKS = -(-TILES // CHUNK_TILES)
TILES0 = CHUNKS * CHUNK_TILES
GROUPS0 = TILES0 // GROUP
GROUPS1 = -(-TILES // GROUP)
LAST_TILES = TILES - (CHUNKS - 1) * CHUNK_TILES
LAST_GROUPS = -(-LAST_TILES // GROUP)
NODE_BLOCKS = -(-(NODES + P) // P)
NODE_ROWS = NODE_BLOCKS * P
XROW = FEAT + HEADS0
PARTS = 3
BATCH = 5
BATCHES = NODE_BLOCKS // BATCH
RING_COLS = 2 * CHUNK_TILES * XROW
LN_EPS = 1e-5
SLOPE = 0.2
NEG = -1e30
assert GROUP * EDGE_DIM == P and CHUNKS % 2 == 1 and BATCHES % 2 == 0
assert RUN_TILES * RUNS == CHUNK_TILES and LAST_GROUPS % 2 == 0


def counter(eng, name):
    reg = eng.alloc_register(name)
    eng.reg_mov(reg, 0)
    return reg


def window_starts(eng, regs, base_row, first_group, pass_no):
    eng.reg_load(regs, base_row[0:1, bass.DynSlice(first_group, len(regs))])
    out = []
    for reg in regs:
        eng.reg_add(reg, reg, pass_no * P)
        eng.reg_alu(reg, reg, NODES, op=ALU.min)
        out.append(eng.snap(reg, min_val=0, max_val=NODES))
    return out


def wait_here(eng, sem, value, gate):
    eng.wait_ge(sem, value)
    eng.sem_inc(gate, 1)


def program(nc, xT, xpad, src_idx0, src_idx1, dst_tile, dst_row, dst_runs, base_rep, last_rep, base_row,
            ea_turned, ea, ew, w_linT, w_lin, att, w_edge, att_edge, wqkvT, rows, ident, iota, node_of, own_tile,
            sel, sel_parts, fold, out):
    S = nc.alloc_semaphore

    def sb(name, shape, dt=F32):
        return nc.alloc_sbuf_tensor(name, shape, dt).ap()

    x_table = nc.dram_tensor("x_table", [NODE_ROWS, XROW], F32, kind="Internal").ap()
    ai_table = nc.dram_tensor("ai_table", [NODE_ROWS, PARTS * HEADS0], BF16, kind="Internal").ap()
    q_table = nc.dram_tensor("q_table", [NODE_ROWS, FEAT], F32, kind="Internal").ap()
    kv_table = nc.dram_tensor("kv_table", [NODE_ROWS, 2 * FEAT], F32, kind="Internal").ap()

    ident_sb = sb("ident_sb", [P, P])
    iota_sb = sb("iota_sb", [P, P])
    iota_pass = sb("iota_pass", [P, P])
    sel_sb = sb("sel_sb", [P, P])
    fold_sb = sb("fold_sb", [PARTS * HEADS0, HEADS0])
    sel_parts_sb = sb("sel_parts_sb", [P, PARTS * HEADS0])
    drel = sb("drel", [P, TILES0])
    base_sb = sb("base_sb", [1, GROUPS0], I32)
    passes_sb = sb("passes_sb", [P, 1], I32)
    sumT = sb("sumT", [P, NODE_ROWS])
    denT = sb("denT", [PARTS * HEADS0, NODE_ROWS])
    we_att = sb("we_att", [P, GROUP * HEADS0])
    base_f = sb("base_f", [P, GROUPS0])
    node_col = sb("node_col", [P, 1])
    node_pass = sb("node_pass", [P, 1])
    ring = sb("ring", [P, RING_COLS])
    x1_rows = ring[:, RING_COLS - NODE_ROWS:]
    work = sb("work", [P, 5 * GROUP * P])

    idx0 = [sb(f"idx{i}", [P, CHUNK_TILES], I32) for i in range(2)]
    idx0_in = [S(f"idx_in{i}") for i in range(2)]

    psum = nc.alloc_psum_tensor("psum", [P, 8 * 512], F32).ap()
    bank = [psum[:, i * 512:(i + 1) * 512] for i in range(4)]
    wide = [psum[:, (4 + 2 * i) * 512:(6 + 2 * i) * 512] for i in range(2)]

    dst_i = ring[:, 0:TILES0].bitcast(I32)
    base_i = ring[:, TILES0:TILES0 + GROUPS0].bitcast(I32)
    last_i = ring[:, TILES0 + GROUPS0:TILES0 + 2 * GROUPS0].bitcast(I32)
    span_i = ring[:, TILES0 + 2 * GROUPS0:TILES0 + 3 * GROUPS0].bitcast(I32)
    at = TILES0 + 3 * GROUPS0
    att_sb = ring[:, at:at + 2 * HEADS0]
    w_lin_sb = ring[:, at + 16:at + 16 + FEAT]
    w_edge_sb = ring[:, at + 160:at + 160 + P]
    att_edge_sb = ring[:, at + 288:at + 288 + HEADS0]
    own_tile_sb = ring[:, at + 292:at + 292 + GROUP * HEADS0]
    at += 384
    W0 = FEAT + 2 * HEADS0
    rhs0 = ring[:, at:at + W0]
    at += W0
    xT_sb = ring[:, at:at + NODE_ROWS]
    at += NODE_ROWS
    table_rows = ring[:, at:at + NODE_BLOCKS * XROW].rearrange("p (b w) -> p b w", w=XROW)
    at += NODE_BLOCKS * XROW
    AI = NODE_BLOCKS * HEADS0
    ai_all = ring[:, at:at + AI]
    ai_rest = ring[:, at + AI:at + 2 * AI]
    ai_parts = ring[:, at + 2 * AI:at + 4 * AI].bitcast(BF16)[:, 0:3 * AI].rearrange("p (b s h) -> p b s h", s=3, h=HEADS0)
    ai_made = S("ai_made")
    ai_split = S("ai_split")
    ai_out = S("ai_out")
    consts_in = S("consts_in")
    ints_in = S("ints_in")
    weights_in = S("weights_in")
    folded = S("folded")
    folded_sb = S("folded_sb")
    xT_in = [S(f"xT_in{i}") for i in range(3)]
    rows_made = S("rows_made")
    rows_copied = S("rows_copied")
    rows_out = S("rows_out")
    PIECE_PAIRS = 5
    PIECES = NODE_BLOCKS // (2 * PIECE_PAIRS)
    PIECE_NODES = 2 * PIECE_PAIRS * P
    LOADS = ((0, 1), (1, 3), (3, PIECES))
    assert PIECES * PIECE_NODES == NODE_ROWS and at + 4 * AI <= RING_COLS
    pair_ps = [psum[:, (2 + j) * 512:(2 + j) * 512 + 2 * W0] for j in range(PIECE_PAIRS)]

    with nc.Block() as block:
        @block.sync
        def _(sp):
            for to, of in ((w_lin_sb, w_lin), (att_sb, att), (rhs0[:, 0:FEAT], w_linT), (w_edge_sb, w_edge),
                           (att_edge_sb, att_edge), (own_tile_sb, own_tile)):
                sp.dma_start(to, of).then_inc(weights_in, 16)
            for i, (first, past) in enumerate(LOADS):
                pieces = slice(first * PIECE_NODES, past * PIECE_NODES)
                sp.dma_start(xT_sb[:, pieces], xT[:, pieces]).then_inc(xT_in[i], 16)
            with sp.Fori(0, PIECES) as i:
                sp.wait_ge(rows_copied, PIECE_PAIRS * (i + 2))
                sp.dma_start(x_table[bass.DynSlice(i * PIECE_NODES, PIECE_NODES), :].rearrange("(b p) w -> p b w", p=P),
                             table_rows[:, bass.DynSlice(i * 2 * PIECE_PAIRS, 2 * PIECE_PAIRS), :]).then_inc(rows_out, 16)
            sp.wait_ge(ai_split, 1)
            sp.dma_start(ai_table.rearrange("(b p) w -> p b w", p=P), ai_parts.rearrange("p b s h -> p b (s h)"))\
              .then_inc(ai_out, 16)
            sp.wait_ge(ai_out, 16)
            sp.wait_ge(rows_out, 16 * PIECES)

        @block.gpsimd
        def _(pool):
            for to, of in ((dst_i, dst_tile), (base_i, base_rep), (last_i, last_rep), (base_sb, base_row)):
                pool.dma_start(to, of).then_inc(ints_in, 16)
            for to, of in ((ident_sb, ident), (iota_sb, iota), (sel_sb, sel), (sel_parts_sb, sel_parts), (fold_sb, fold), (node_col, node_of)):
                pool.dma_start(to, of).then_inc(consts_in, 16)
            pool.dma_start(idx0[0], src_idx0[0, :, :]).then_inc(idx0_in[0], 16)
            pool.memset(denT, 0.0)
            pool.wait_ge(consts_in, 96)

        @block.tensor
        def _(pe):
            pe.wait_ge(weights_in, 96)
            pe.matmul(bank[0][:, 0:2 * HEADS0], w_lin_sb, att_sb, start=True, stop=True)
            pe.matmul(bank[1][:, 0:HEADS0], w_edge_sb, att_edge_sb, start=True, stop=True).then_inc(folded, 1)
            pe.wait_ge(folded_sb, 1)

            def piece(i):
                for j in range(PIECE_PAIRS):
                    pe.wait_ge(rows_copied, PIECE_PAIRS * i + j + 1)
                    pe.wait_ge(ai_made, PIECE_PAIRS * i + j + 1)
                    for b in range(2):
                        last = pe.matmul(pair_ps[j][:, b * W0:(b + 1) * W0],
                                         xT_sb[:, i * PIECE_NODES + (2 * j + b) * P:][:, 0:P], rhs0, start=True, stop=True)
                    last.then_inc(rows_made, 1)

            for load, (first, past) in enumerate(LOADS):
                pe.wait_ge(xT_in[load], 16)
                for i in range(first, past):
                    piece(i)

        @block.scalar
        def _(act):
            act.sem_inc(rows_copied, PIECE_PAIRS)
            for i in range(PIECES):
                for j in range(PIECE_PAIRS):
                    act.wait_ge(rows_made, PIECE_PAIRS * i + j + 1)
                    act.activation(table_rows[:, (i * PIECE_PAIRS + j) * 2:(i * PIECE_PAIRS + j) * 2 + 2, :],
                                   pair_ps[j].rearrange("p (b w) -> p b w", b=2)[:, :, 0:XROW], ACT.Copy)\
                        .then_inc(rows_copied, 1)

        @block.vector
        def _(dve):
            dve.sem_inc(ai_made, PIECE_PAIRS)
            dve.memset(sumT, 0.0)
            dve.wait_ge(weights_in, 96)
            dve.wait_ge(folded, 1)
            dve.tensor_copy(rhs0[:, FEAT:W0], bank[0][:, 0:2 * HEADS0]).then_inc(folded_sb, 1)
            dve.tensor_tensor(out=we_att.rearrange("p (t h) -> p t h", h=HEADS0),
                              in0=bank[1][:, 0:HEADS0].unsqueeze(1).to_broadcast([P, GROUP, HEADS0]),
                              in1=own_tile_sb.rearrange("p (t h) -> p t h", h=HEADS0), op=ALU.mult)
            with dve.Fori(0, PIECES) as i:
                for j in range(PIECE_PAIRS):
                    dve.wait_ge(rows_copied, PIECE_PAIRS * (i + 1) + j + 1)
                    dve.tensor_copy(ai_all[:, bass.DynSlice((i * PIECE_PAIRS + j) * 2 * HEADS0, 2 * HEADS0)]
                                    .rearrange("p (b h) -> p b h", b=2),
                                    pair_ps[j].rearrange("p (b w) -> p b w", b=2)[:, :, XROW:W0]).then_inc(ai_made, 1)
            per_block = lambda t: t.rearrange("p (b h) -> p b h", h=HEADS0)
            dve.drain()
            dve.tensor_copy(ai_parts[:, :, 0, :], per_block(ai_all))
            for part in range(1, PARTS):
                dve.drain()
                dve.tensor_tensor(out=per_block(ai_rest if part == 1 else ai_all),
                                  in0=per_block(ai_all if part == 1 else ai_rest),
                                  in1=ai_parts[:, :, part - 1, :], op=ALU.subtract)
                dve.drain()
                last = dve.tensor_copy(ai_parts[:, :, part, :], per_block(ai_rest if part == 1 else ai_all))
            last.then_inc(ai_split, 1)
            dve.wait_ge(ints_in, 64)
            dve.tensor_copy(base_f, base_i)
            dve.tensor_tensor(out=drel.rearrange("p (g t) -> p g t", t=GROUP),
                              in0=dst_i.rearrange("p (g t) -> p g t", t=GROUP),
                              in1=base_i.unsqueeze(2).to_broadcast([P, GROUPS0, GROUP]), op=ALU.subtract)
            dve.tensor_tensor(out=span_i, in0=last_i, in1=base_i, op=ALU.subtract)
            dve.drain()
            dve.tensor_reduce(out=passes_sb, in_=span_i, axis=AX.X, op=ALU.max)
            dve.drain()
            dve.tensor_scalar(passes_sb, passes_sb, 7, None, ALU.arith_shift_right)
            dve.drain()
            dve.tensor_scalar(passes_sb, passes_sb, 1, None, ALU.add)

    shared = dict(
        x_table=x_table, ai_table=ai_table, q_table=q_table, kv_table=kv_table, xpad=xpad,
        src_idx0=src_idx0, src_idx1=src_idx1, dst_row=dst_row, dst_runs=dst_runs, ea_turned=ea_turned,
        ea=ea, ew=ew, wqkvT=wqkvT, rows=rows, out=out, ident_sb=ident_sb, iota_sb=iota_sb,
        iota_pass=iota_pass, node_col=node_col, node_pass=node_pass, sel_sb=sel_sb, sel_parts_sb=sel_parts_sb, fold_sb=fold_sb,
        drel=drel, base_f=base_f, base_sb=base_sb, passes_sb=passes_sb, sumT=sumT, denT=denT,
        we_att=we_att, ring=ring, idx0=idx0, idx0_in=idx0_in, x1_rows=x1_rows, work=work, psum=psum, bank=bank, wide=wide)
    layer0(nc, S, sb, shared)
    between(nc, S, sb, shared)
    layer1(nc, S, sb, shared)
    final(nc, S, sb, shared)


def layer0(nc, S, sb, shared):
    k = shared
    GP = GROUP * P
    onehot = [k["work"][:, u * GP:(u + 1) * GP].rearrange("p (t n) -> p t n", t=GROUP) for u in range(2)]
    message = [k["work"][:, (2 + u) * GP:(3 + u) * GP].rearrange("p (t f) -> p t f", t=GROUP) for u in range(2)]
    onehotT = [k["work"][:, 4 * GP + u * GP // 2:4 * GP + (u + 1) * GP // 2].bitcast(BF16) for u in range(2)]
    dst_all = [sb(f"dst_all{i}", [P, GP], I32) for i in range(2)]
    ea_pair = [sb(f"ea_pair{i}", [P, 2, P]) for i in range(2)]
    idx = k["idx0"]
    runs_dst = sb("runs_dst", [P, RUN + 2], I32)
    ai_win = [sb(f"ai_win{i}", [P, PARTS * HEADS0], BF16) for i in range(2)]
    zeros = sb("zeros", [P, CHUNK_TILES * HEADS0], BF16)
    score = sb("score", [P, HEADS0, CHUNK_TILES])
    ex = score
    ex_parts = sb("ex_parts", [P, CHUNK_TILES, PARTS, HEADS0], BF16)
    ex_group = [sb(f"ex_group{i}", [P, GROUP, PARTS, HEADS0], BF16) for i in range(2)]
    onehot_bf = [sb(f"onehot_bf{i}", [P, GROUP, P], BF16) for i in range(2)]
    edge_change = sb("edge_change", [P, RUN + 1])
    ahead = sb("ahead", [P, RUN])
    back = sb("back", [P, RUN])
    cols = sb("cols", [P, 8])
    rowbuf = sb("rowbuf", [1, 5 * P])
    carry = sb("carry", [1, HEADS0])

    x_rows = k["ring"][:, 0:2 * CHUNK_TILES * XROW].rearrange("p (t w) -> p t w", w=XROW)
    scores_ps = k["bank"][0][:, 0:CHUNK_TILES * HEADS0]
    runs_ps = k["bank"][1][:, 0:RUN]
    small_ps = k["bank"][2]
    den_ps = [k["bank"][3 - u][0:PARTS * HEADS0, 0:P] for u in range(2)]
    sum_ps = [k["wide"][1][:, u * 512:u * 512 + P] for u in range(2)]

    idx_in = k["idx0_in"]
    gathered = [S(f"gathered{i}") for i in range(2)]
    chunk_ready = S("chunk_ready")
    rows_released = S("rows_released")
    ea_in = [S(f"ea_in{i}") for i in range(2)]
    ea_used = S("ea_used")
    ai_in = [S(f"ai_in{i}") for i in range(2)]
    dst_in = [S(f"dst_in{i}") for i in range(2)]
    dst_used = S("dst_used")
    onehotT_made = S("onehotT_made")
    scores_added = S("scores_added")
    runs_in = S("runs_in")
    runs_used = S("runs_used")
    onehot_made = S("onehot_made")
    onehot_bf_made = S("onehot_bf_made")
    msg_made = S("msg_made")
    summed = S("summed")
    scores_summed = S("scores_summed")
    zeros_set = S("zeros_set")
    dve_to_pe = S("dve_to_pe")
    pe_to_dve = S("pe_to_dve")
    shifted = S("shifted")
    exp_done = S("exp_done")
    exT_done = S("exT_done")
    ex_copied = S("ex_copied")
    pe_gate = S("pe_gate")
    pool_gate = S("pool_gate")
    dve_gate = S("dve_gate")
    HALF = CHUNK_GROUPS // 2
    STEPS = 5
    run_ends = [ahead[:, RUN - 1:RUN], cols[:, 0:1], cols[:, 1:2]]

    with nc.Block() as block:
        @block.sync
        def _(sp):
            passes = sp.value_load(k["passes_sb"][0:1, 0:1], min_val=1, max_val=NODE_BLOCKS)
            visit = counter(sp, "sp_visit0")
            regs = [sp.alloc_register(f"sp_base0{u}") for u in range(2)]
            with sp.Fori(0, CHUNKS) as s:
                sp.wait_ge(runs_used, s + 1)
                sp.dma_start(runs_dst, k["dst_runs"][bass.DynSlice(s, 1), :, :].rearrange("o p n -> (o p) n"))\
                  .then_inc(runs_in, 16)
                with sp.Fori(0, HALF // 2) as g:
                    for u in range(2):
                        n = s * HALF + 2 * g + u
                        sp.wait_ge(ea_used, n + 1)
                        sp.dma_start(ea_pair[u], k["ea_turned"][bass.DynSlice(2 * n, 2), :, :].rearrange("g p e -> p g e"))\
                          .then_inc(ea_in[u], 16)
                with sp.Fori(0, passes) as r:
                    with sp.Fori(0, HALF) as g:
                        v = sp.snap(visit)
                        first_group = s * CHUNK_GROUPS + 2 * g
                        starts = window_starts(sp, regs, k["base_sb"], first_group, r)
                        for u in range(2):
                            sp.wait_ge(dst_used, 2 * v + u + 1)
                            sp.dma_start(dst_all[u], k["dst_row"][0:1, bass.DynSlice((first_group + u) * GP, GP)]
                                         .to_broadcast([P, GP])).then_inc(dst_in[u], 16)
                            sp.wait_ge(scores_added, 2 * v + u + 1)
                            sp.dma_start(ai_win[u], k["ai_table"][bass.DynSlice(starts[u], P), :]).then_inc(ai_in[u], 16)
                        sp.reg_add(visit, visit, 1)

        @block.gpsimd
        def _(pool):
            ALL = 16 * CHUNK_TILES

            def chunk(h, nth, s, tiles, before, following):
                wait_here(pool, idx_in[h], 16 * (nth + 1), pool_gate)
                wait_here(pool, rows_released, s + 1, pool_gate)
                for t in range(tiles):
                    pool.indirect_dma_start(x_rows[:, h * CHUNK_TILES + t, :], None, k["x_table"],
                                            bass.IndirectOffsetOnAxis(idx[h][:, t:t + 1], 0))\
                        .then_inc(gathered[h], 16)
                    if t == 4:
                        if before is not None:
                            pool.wait_ge(gathered[1 - h], before)
                            pool.sem_inc(chunk_ready, 1)
                        if following is not None:
                            pool.dma_start(idx[1 - h], k["src_idx0"][bass.DynSlice(following, 1), :, :]
                                           .rearrange("o p n -> (o p) n")).then_inc(idx_in[1 - h], 16)

            chunk(0, 0, 0, CHUNK_TILES, None, 1)
            PAIRS = CHUNKS // 2 - 1
            with pool.Fori(0, PAIRS) as i:
                chunk(1, i, 2 * i + 1, CHUNK_TILES, ALL * (i + 1), 2 * i + 2)
                chunk(0, i + 1, 2 * i + 2, CHUNK_TILES, ALL * (i + 1), 2 * i + 3)
            chunk(1, PAIRS, CHUNKS - 2, CHUNK_TILES, ALL * (PAIRS + 1), CHUNKS - 1)
            chunk(0, PAIRS + 1, CHUNKS - 1, LAST_TILES, ALL * (PAIRS + 1), None)
            pool.wait_ge(gathered[0], ALL * (PAIRS + 1) + 16 * LAST_TILES)
            pool.sem_inc(chunk_ready, 1)

        @block.tensor
        def _(pe):
            passes = pe.value_load(k["passes_sb"][0:1, 0:1], min_val=1, max_val=NODE_BLOCKS)
            d_visit = counter(pe, "pe_d_visit0")
            c_visit = counter(pe, "pe_c_visit0")

            def open_scores(s):
                pe.matmul(scores_ps, zeros[:, 0:P], zeros, start=True, stop=False)
                for g in range(CHUNK_GROUPS):
                    if g % 2 == 0:
                        pe.wait_ge(ea_in[g // 2 % 2], 16 * (s * (HALF // 2) + g // 4 + 1))
                    last = pe.matmul(scores_ps[:, g * GROUP * HEADS0:(g + 1) * GROUP * HEADS0],
                                     ea_pair[g // 2 % 2][:, g % 2, :], k["we_att"], start=False, stop=False)
                    if g % 2 == 1:
                        last.then_inc(ea_used, 1)

            def scores_group(d, g):
                pe.wait_ge(onehotT_made, d * CHUNK_GROUPS + g + 1)
                pe.wait_ge(ai_in[g % 2], 16 * (d * HALF + g // 2 + 1))
                for t in range(GROUP):
                    at = (g * GROUP + t) * HEADS0
                    for part in range(PARTS):
                        last = pe.matmul(scores_ps[:, at:at + HEADS0], onehotT[g % 2][:, t * P:(t + 1) * P],
                                         ai_win[g % 2][:, part * HEADS0:(part + 1) * HEADS0],
                                         start=False, stop=False)
                last.then_inc(scores_added, 1)

            def close_scores():
                pe.matmul(scores_ps, zeros[:, 0:P], zeros, start=False, stop=True).then_inc(scores_summed, 1)

            def maxima(s):
                pe.wait_ge(dve_to_pe, STEPS * s + 1)
                for t in range(RUN_TILES):
                    last = pe.transpose(runs_ps[:, t * P:(t + 1) * P],
                                        score.rearrange("p h (c t) -> p (h c) t", t=RUN_TILES)[:, :, t], k["ident_sb"])
                last.then_inc(pe_to_dve, 1)
                pe.wait_ge(dve_to_pe, STEPS * s + 2)
                for c in range(3):
                    last = pe.transpose(small_ps[0:1, c * P:(c + 1) * P], run_ends[c], k["ident_sb"])
                last.then_inc(pe_to_dve, 1)
                wait_here(pe, dve_to_pe, STEPS * s + 3, pe_gate)
                pe.transpose(small_ps[:, 400:401], rowbuf[0:1, 3 * P:4 * P], k["ident_sb"][0:1, 0:1]).then_inc(pe_to_dve, 1)
                pe.wait_ge(dve_to_pe, STEPS * s + 4)
                pe.transpose(small_ps[0:1, 0:P], back[:, 0:1], k["ident_sb"]).then_inc(pe_to_dve, 1)
                wait_here(pe, dve_to_pe, STEPS * s + 5, pe_gate)
                pe.transpose(small_ps[:, 402:403], rowbuf[0:1, 3 * P:4 * P], k["ident_sb"][0:1, 0:1]).then_inc(pe_to_dve, 1)
                pe.wait_ge(exp_done, s + 1)
                for t in range(RUN_TILES):
                    pe.transpose(runs_ps[:, t * P:(t + 1) * P], ahead[:, t * P:(t + 1) * P], k["ident_sb"])
                pe.matmul(small_ps[:, 404:405], k["sel_sb"], cols[:, 5:6], start=True, stop=True)
                pe.matmul(small_ps[0:PARTS * HEADS0, 406:407], k["sel_parts_sb"], cols[:, 5:6], start=True, stop=True)\
                  .then_inc(exT_done, 1)

            def sums_group(c, g):
                u = g % 2
                pe.wait_ge(msg_made, c + g + 1)
                for t in range(GROUP):
                    pe.matmul(sum_ps[u], message[u][:, t, :], onehot[u][:, t, :], start=t == 0, stop=t == GROUP - 1)
                pe.wait_ge(onehot_bf_made, c + g + 1)
                for t in range(GROUP):
                    last = pe.matmul(den_ps[u], ex_group[u][:, t, :, :].rearrange("p s h -> p (s h)"),
                                     onehot_bf[u][:, t, :], start=t == 0, stop=t == GROUP - 1)
                last.then_inc(summed, 1)

            pe.wait_ge(zeros_set, 1)
            open_scores(0)
            with pe.Fori(0, passes) as r:
                d = pe.snap(d_visit)
                for g in range(CHUNK_GROUPS):
                    scores_group(d, g)
                pe.reg_add(d_visit, d_visit, 1)
            close_scores()
            with pe.Fori(0, CHUNKS - 1) as s:
                maxima(s)
                open_scores(s + 1)
                with pe.Fori(0, passes) as r:
                    c, d = pe.snap(c_visit), pe.snap(d_visit)
                    for g in range(CHUNK_GROUPS):
                        scores_group(d, g)
                        sums_group(c, g)
                    pe.reg_add(c_visit, c_visit, CHUNK_GROUPS)
                    pe.reg_add(d_visit, d_visit, 1)
                close_scores()
            maxima(CHUNKS - 1)
            with pe.Fori(0, passes) as r:
                c = pe.snap(c_visit)
                for g in range(LAST_GROUPS):
                    sums_group(c, g)
                pe.reg_add(c_visit, c_visit, LAST_GROUPS)

        @block.scalar
        def _(act):
            passes = act.value_load(k["passes_sb"][0:1, 0:1], min_val=1, max_val=NODE_BLOCKS)
            group = counter(act, "act_group0")

            def chunk(s, groups):
                act.wait_ge(shifted, s + 1)
                act.activation(ahead, back, ACT.Exp)
                act.activation(cols[:, 5:6], cols[:, 4:5], ACT.Exp).then_inc(exp_done, 1)
                act.wait_ge(exT_done, s + 1)
                act.activation(ex.rearrange("p h (c t) -> p (h c) t", t=RUN_TILES),
                               runs_ps.rearrange("p (t q) -> p q t", t=RUN_TILES), ACT.Copy).then_inc(ex_copied, 1)
                with act.Fori(0, passes) as r:
                    with act.Fori(0, groups // 2) as g:
                        n = act.snap(group)
                        for u in range(2):
                            act.wait_ge(onehot_made, n + u + 1)
                            act.wait_ge(summed, n + u + 1)
                            act.activation(onehot_bf[u], onehot[u], ACT.Copy)
                            act.activation(ex_group[u].rearrange("p t s h -> p t (s h)"),
                                           ex_parts[:, bass.DynSlice((2 * g + u) * GROUP, GROUP), :, :]
                                           .rearrange("p t s h -> p t (s h)"), ACT.Copy).then_inc(onehot_bf_made, 1)
                        act.reg_add(group, group, 2)

            with act.Fori(0, CHUNKS - 1) as s:
                chunk(s, CHUNK_GROUPS)
            chunk(CHUNKS - 1, LAST_GROUPS)

        @block.vector
        def _(dve):
            passes = dve.value_load(k["passes_sb"][0:1, 0:1], min_val=1, max_val=NODE_BLOCKS)
            d_visit = counter(dve, "dve_d_visit0")
            c_visit = counter(dve, "dve_c_visit0")
            regs = [dve.alloc_register(f"dve_base0{u}") for u in range(2)]
            before = dve.alloc_register("dve_base_before0")
            dve.memset(zeros, 0.0).then_inc(zeros_set, 1)
            dve.memset(carry, NEG)
            dve.memset(cols, 0.0)
            for credit, n in ((rows_released, 2), (ea_used, 2), (dst_used, 2), (scores_added, 2), (runs_used, 1),
                              (summed, 2)):
                dve.sem_inc(credit, n)

            def first_pass():
                dve.drain()
                dve.tensor_copy(k["node_pass"], k["node_col"])
                dve.tensor_copy(k["iota_pass"], k["iota_sb"])
                dve.drain()

            def next_pass():
                dve.drain()
                for numbers in (k["node_pass"], k["iota_pass"]):
                    dve.tensor_scalar(numbers, numbers, float(P), None, ALU.add)
                dve.drain()

            def scores_onehot(u, v, group):
                dve.wait_ge(dst_in[u], 16 * (v + 1))
                dve.wait_ge(scores_added, 2 * v + u + 1)
                dve.tensor_scalar(onehotT[u], dst_all[u], k["base_f"][:, bass.DynSlice(group, 1)],
                                  k["node_pass"], ALU.subtract, ALU.is_equal).then_inc(onehotT_made, 1)
                dve.drain().then_inc(dst_used, 1)

            def maxima(s):
                dve.wait_ge(runs_in, 16 * (s + 1))
                dve.tensor_tensor(out=edge_change, in0=runs_dst[:, 0:RUN + 1], in1=runs_dst[:, 1:RUN + 2],
                                  op=ALU.not_equal).then_inc(runs_used, 1)
                dve.drain()
                dve.tensor_scalar(edge_change, edge_change, NEG, None, ALU.mult)
                dve.drain()
                dve.tensor_reduce(out=cols[:, 0:1], in_=edge_change[:, 0:RUN], axis=AX.X, op=ALU.min)
                dve.tensor_reduce(out=cols[:, 1:2], in_=edge_change[:, 1:RUN + 1], axis=AX.X, op=ALU.min)

                dve.wait_ge(scores_summed, s + 1)
                dve.wait_ge(chunk_ready, s + 1)
                dve.tensor_tensor(out=score.rearrange("p h t -> p t h"),
                                  in0=scores_ps.rearrange("p (t h) -> p t h", h=HEADS0),
                                  in1=x_rows[:, bass.DynSlice((s % 2) * CHUNK_TILES, CHUNK_TILES), FEAT:XROW],
                                  op=ALU.add)
                dve.drain()
                flat = score.rearrange("p h t -> p (h t)")
                dve.scalar_tensor_tensor(out=flat, in0=flat, scalar=SLOPE, in1=flat, op0=ALU.mult, op1=ALU.max)\
                   .then_inc(dve_to_pe, 1)

                dve.wait_ge(pe_to_dve, 5 * s + 1)
                dve.tensor_tensor_scan(ahead, edge_change[:, 0:RUN], runs_ps, NEG, ALU.add, ALU.max).then_inc(dve_to_pe, 1)
                ends, pen, pen_back, into, over = (rowbuf[0:1, c * P:(c + 1) * P] for c in range(5))
                by_head = lambda row: row.rearrange("p (h c) -> p h c", h=HEADS0)
                carry3 = carry.unsqueeze(2)
                dve.wait_ge(pe_to_dve, 5 * s + 2)
                dve.tensor_copy(rowbuf[0:1, 0:3 * P], small_ps[0:1, 0:3 * P])
                dve.drain()
                dve.tensor_tensor(out=by_head(over)[:, :, 0:1], in0=by_head(pen)[:, :, 0:1], in1=carry3, op=ALU.add)
                dve.drain()
                dve.tensor_tensor(out=by_head(ends)[:, :, 0:1], in0=by_head(ends)[:, :, 0:1],
                                  in1=by_head(over)[:, :, 0:1], op=ALU.max)
                dve.memset(by_head(pen)[:, :, 0:1], 2 * NEG)
                dve.memset(by_head(pen_back)[:, :, RUNS - 1:RUNS], 2 * NEG)
                dve.drain()
                dve.tensor_tensor_scan(over, pen, ends, 0.0, ALU.add, ALU.max)
                dve.drain()
                dve.tensor_copy(by_head(into)[:, :, 1:RUNS], by_head(over)[:, :, 0:RUNS - 1])
                dve.tensor_copy(by_head(into)[:, :, 0:1], carry3).then_inc(dve_to_pe, 1)
                dve.drain()
                dve.tensor_copy(carry3, by_head(over)[:, :, RUNS - 1:RUNS])
                dve.wait_ge(pe_to_dve, 5 * s + 3)
                dve.tensor_copy(cols[:, 2:3], small_ps[:, 400:401])
                dve.drain()
                dve.tensor_tensor_scan(ahead, edge_change[:, 0:RUN], runs_ps, cols[:, 2:3], ALU.add, ALU.max)
                dve.drain()
                scan_back = (back[:, ::-1], edge_change[:, RUN:0:-1], ahead[:, ::-1])
                dve.tensor_tensor_scan(*scan_back, NEG, ALU.add, ALU.max).then_inc(dve_to_pe, 1)
                dve.wait_ge(pe_to_dve, 5 * s + 4)
                dve.tensor_copy(ends, small_ps[0:1, 0:P])
                dve.drain()
                dve.tensor_tensor_scan(over[:, ::-1], pen_back[:, ::-1], ends[:, ::-1], 0.0, ALU.add, ALU.max)
                dve.drain()
                dve.tensor_copy(by_head(into)[:, :, 0:RUNS - 1], by_head(over)[:, :, 1:RUNS])
                dve.memset(by_head(into)[:, :, RUNS - 1:RUNS], 2 * NEG).then_inc(dve_to_pe, 1)
                dve.wait_ge(pe_to_dve, 5 * s + 5)
                dve.tensor_copy(cols[:, 3:4], small_ps[:, 402:403])
                dve.drain()
                dve.tensor_tensor_scan(*scan_back, cols[:, 3:4], ALU.add, ALU.max)
                dve.drain()
                dve.tensor_tensor(out=cols[:, 4:5], in0=cols[:, 2:3], in1=back[:, 0:1], op=ALU.subtract)
                dve.drain()
                dve.tensor_scalar(cols[:, 4:5], cols[:, 4:5], 0.0, None, ALU.min)
                dve.tensor_tensor(out=back, in0=runs_ps, in1=back, op=ALU.subtract).then_inc(shifted, 1)

                dve.reg_load(regs[0], k["base_sb"][0:1, bass.DynSlice(s * CHUNK_GROUPS, 1)])
                first = dve.snap(regs[0], min_val=0, max_val=NODES)
                dve.wait_ge(exT_done, s + 1)
                column = k["sumT"][:, bass.DynSlice(first, 1)]
                dve.tensor_tensor(out=column, in0=column, in1=small_ps[:, 404:405], op=ALU.mult)
                column = k["denT"][:, bass.DynSlice(first, 1)]
                dve.tensor_tensor(out=column, in0=column, in1=small_ps[0:PARTS * HEADS0, 406:407], op=ALU.mult)

                wait_here(dve, ex_copied, s + 1, dve_gate)
                rest = ahead.rearrange("p (t h) -> p t h", h=HEADS0)
                of = ex.rearrange("p h t -> p t h")
                for part in range(PARTS):
                    if part:
                        dve.drain()
                        dve.tensor_tensor(out=rest, in0=of, in1=ex_parts[:, :, part - 1, :], op=ALU.subtract)
                        dve.drain()
                        of = rest
                    dve.tensor_copy(ex_parts[:, :, part, :], of)

            def make(u, s, tile):
                dve.tensor_tensor(out=onehot[u], in0=k["iota_pass"].unsqueeze(1).to_broadcast([P, GROUP, P]),
                                  in1=k["drel"][:, bass.DynSlice(s * CHUNK_TILES + tile, GROUP)].unsqueeze(2)
                                  .to_broadcast([P, GROUP, P]), op=ALU.is_equal).then_inc(onehot_made, 1)
                dve.tensor_tensor(
                    out=message[u].rearrange("p t (h f) -> p t h f", h=HEADS0),
                    in0=x_rows[:, bass.DynSlice((s % 2) * CHUNK_TILES + tile, GROUP), 0:FEAT]
                    .rearrange("p t (h f) -> p t h f", h=HEADS0),
                    in1=ex[:, :, bass.DynSlice(tile, GROUP)].rearrange("p h t -> p t h").unsqueeze(3)
                    .to_broadcast([P, GROUP, HEADS0, FEAT // HEADS0]),
                    op=ALU.mult).then_inc(msg_made, 1)

            def add(u, start, group):
                dve.wait_ge(summed, group + 3)
                for sums, part in ((k["sumT"], sum_ps[u]), (k["denT"], den_ps[u])):
                    window = sums[:, bass.DynSlice(start, P)]
                    dve.tensor_tensor(out=window, in0=window, in1=part, op=ALU.add)

            def messages(s, groups, more):
                first_pass()
                with dve.Fori(0, passes) as r:
                    def pair(g, first):
                        v = dve.snap(c_visit)
                        d = dve.snap(d_visit)
                        tile = 2 * g * GROUP
                        make(0, s, tile)
                        if more:
                            scores_onehot(0, d, (s + 1) * CHUNK_GROUPS + 2 * g)
                        else:
                            dve.drain()
                        if not first:
                            add(1, dve.snap(before, min_val=0, max_val=NODES), 2 * v - 1)
                        make(1, s, tile + GROUP)
                        if more:
                            scores_onehot(1, d, (s + 1) * CHUNK_GROUPS + 2 * g + 1)
                        else:
                            dve.drain()
                        starts = window_starts(dve, regs, k["base_sb"], s * CHUNK_GROUPS + 2 * g, r)
                        dve.reg_mov(before, starts[1])
                        add(0, starts[0], 2 * v)
                        dve.reg_add(c_visit, c_visit, 1)
                        if more:
                            dve.reg_add(d_visit, d_visit, 1)

                    pair(0, True)
                    with dve.Fori(1, groups // 2) as g:
                        pair(g, False)
                    dve.drain()
                    add(1, dve.snap(before, min_val=0, max_val=NODES), 2 * dve.snap(c_visit) - 1)
                    next_pass()
                dve.drain().then_inc(rows_released, 1)

            first_pass()
            with dve.Fori(0, passes) as r:
                with dve.Fori(0, HALF) as g:
                    v = dve.snap(d_visit)
                    for u in range(2):
                        scores_onehot(u, v, 2 * g + u)
                    dve.reg_add(d_visit, d_visit, 1)
                next_pass()
            with dve.Fori(0, CHUNKS - 1) as s:
                maxima(s)
                messages(s, CHUNK_GROUPS, True)
            maxima(CHUNKS - 1)
            messages(CHUNKS - 1, LAST_GROUPS, False)


def between(nc, S, sb, shared):
    k = shared
    B = BATCH * FEAT
    DEN = PARTS * HEADS0
    cut = [0]

    def part(cols):
        cut[0] += cols
        return k["ring"][:, cut[0] - cols:cut[0]]

    rows_sb = part(3 * FEAT)
    bias, gamma, beta = (rows_sb[:, i * FEAT:(i + 1) * FEAT].unsqueeze(1).to_broadcast([P, BATCH, FEAT])
                         for i in range(3))
    w_sb = part(3 * FEAT)
    x_in, x_bias, sT, y, y_second, x1s, x1T = ([part(B) for _ in range(2)] for _ in range(7))
    dT = [part(B)[0:DEN, :] for _ in range(2)]
    exp_y = part(B)
    qkv = [part(3 * B).rearrange("p (b w) -> p b w", b=BATCH) for _ in range(2)]
    rden = part(BATCH * HEADS0)
    blocks = lambda t: t.rearrange("p (b w) -> p b w", b=BATCH)
    stats = [blocks(part(6 * BATCH)) for _ in range(2)]
    mv = [blocks(part(2 * BATCH)) for _ in range(2)]
    rstd = [part(BATCH) for _ in range(3)]
    less = [part(BATCH) for _ in range(2)]
    shift = [part(BATCH) for _ in range(2)]
    half_neg = part(BATCH)
    minus_one = part(1)
    assert cut[0] <= RING_COLS - NODE_ROWS
    x1 = k["x1_rows"]

    turned_ps = [k["psum"][:, 2 * 512:4 * 512], k["wide"][0]]
    y_ps = [t[:, 0:B] for t in turned_ps]
    dn_ps = [t[:, B:B + BATCH * HEADS0] for t in turned_ps]
    x1T_ps = k["wide"][1][:, 0:B]

    w_in = S("w_in")
    xb_in = [S(f"xb_in{i}") for i in range(2)]
    bias_added = S("bias_added")
    x_used = S("x_used")
    bias_in = [S(f"bias_in{i}") for i in range(2)]
    bias_used = S("bias_used")
    sums_copied = S("sums_copied")
    sums_turned = S("sums_turned")
    sums_used = S("sums_used")
    affine_made = S("affine_made")
    one_off = S("one_off")
    var_made = S("var_made")
    less_made = S("less_made")
    rstd_made = S("rstd_made")
    exp_made = S("exp_made")
    x1_made = S("x1_made")
    x1_turned = S("x1_turned")
    second_made = S("second_made")
    scaled = S("scaled")
    x1T_copied = S("x1T_copied")
    qkv_made = S("qkv_made")
    qkv_copied = S("qkv_copied")
    qkv_out = [S(f"qkv_out{i}") for i in range(2)]

    with nc.Block() as block:
        @block.sync
        def _(sp):
            sp.dma_start(rows_sb, k["rows"]).then_inc(w_in, 16)
            for to, arrived in ((x_bias, bias_in), (x_in, xb_in)):
                for u in range(2):
                    sp.dma_start(blocks(to[u]), k["xpad"][u * BATCH * P:(u + 1) * BATCH * P, :]
                                 .rearrange("(b p) f -> p b f", p=P)).then_inc(arrived[u], 16)
            sp.dma_start(w_sb, k["wqkvT"]).then_inc(w_in, 16)

            with sp.Fori(0, BATCHES // 2 - 1) as i:
                for u in range(2):
                    n = 2 * i + u
                    ahead = k["xpad"][bass.DynSlice((n + 2) * (BATCH * P), BATCH * P), :].rearrange("(b p) f -> p b f", p=P)
                    sp.wait_ge(bias_used, n + 1)
                    sp.dma_start(blocks(x_bias[u]), ahead).then_inc(bias_in[u], 16)
                    sp.wait_ge(x_used, n + 2)
                    sp.dma_start(blocks(x_in[u]), ahead).then_inc(xb_in[u], 16)

        @block.gpsimd
        def _(pool):
            pool.memset(half_neg, -0.5)
            pool.memset(minus_one, -1.0)
            pool.drain()
            pool.wait_ge(w_in, 32)

            def add_bias(u, nth):
                pool.wait_ge(bias_in[u], 16 * (nth + 1))
                pool.tensor_tensor(out=blocks(x_bias[u]), in0=blocks(x_bias[u]), in1=bias, op=ALU.add)\
                    .then_inc(bias_added, 1)

            def take_one_off(u, nth):
                pool.wait_ge(xb_in[u], 16 * (nth + 1))
                pool.tensor_tensor(out=x_in[u], in0=x_in[u], in1=minus_one.to_broadcast([P, B]), op=ALU.add)\
                    .then_inc(one_off, 1)

            def first_power(n):
                pool.wait_ge(var_made, n + 1)
                pool.tensor_tensor(out=rstd[0], in0=rstd[0], in1=half_neg, op=ALU.pow).then_inc(rstd_made, 1)

            def second_power(u, n):
                pool.wait_ge(less_made, n + 1)
                pool.tensor_tensor(out=rstd[1 + u], in0=rstd[1 + u], in1=half_neg, op=ALU.pow)
                pool.drain()
                pool.tensor_tensor(out=shift[u], in0=less[u], in1=rstd[1 + u], op=ALU.mult).then_inc(second_made, 1)

            for u in range(2):
                add_bias(u, 0)
            first_power(0)
            for u in range(2):
                take_one_off(u, 0)
            with pool.Fori(0, BATCHES // 2 - 1) as i:
                for u in range(2):
                    n = 2 * i + u
                    first_power(n + 1)
                    second_power(u, n)
                    add_bias(u, i + 1)
                    take_one_off(u, i + 1)
            first_power(BATCHES - 1)
            second_power(0, BATCHES - 2)
            second_power(1, BATCHES - 1)

        @block.tensor
        def _(pe):
            def turn_sums(u, n):
                pe.wait_ge(sums_copied, n + 1)
                pe.wait_ge(sums_used, n + 1)
                for b in range(BATCH):
                    pe.transpose(y_ps[u][:, b * P:(b + 1) * P], sT[u][:, b * P:(b + 1) * P], k["ident_sb"])
                for b in range(BATCH):
                    last = pe.matmul(dn_ps[u][:, b * HEADS0:(b + 1) * HEADS0], dT[u][:, b * P:(b + 1) * P],
                                     k["fold_sb"], start=True, stop=True)
                last.then_inc(sums_turned, 1)

            def turn_x1(u, n):
                pe.wait_ge(x1_made, n + 1)
                for b in range(BATCH):
                    last = pe.transpose(x1T_ps[:, b * P:(b + 1) * P], x1s[u][:, b * P:(b + 1) * P], k["ident_sb"])
                last.then_inc(x1_turned, 1)

            def products(u, n):
                pe.wait_ge(x1T_copied, n + 1)
                for b in range(BATCH):
                    pe.wait_ge(qkv_copied, BATCH * n + b + 1)
                    pe.matmul(k["bank"][b % 2 if u == 0 else (b + 1) % 2][:, 0:3 * FEAT], x1T[u][:, b * P:(b + 1) * P],
                              w_sb, start=True, stop=True).then_inc(qkv_made, 1)

            for u in range(2):
                turn_sums(u, u)
            turn_sums(0, 2)
            turn_x1(0, 0)
            pe.wait_ge(w_in, 32)
            with pe.Fori(0, BATCHES // 2 - 2) as i:
                for u in range(2):
                    n = 2 * i + u
                    turn_sums(1 - u, n + 3)
                    turn_x1(1 - u, n + 1)
                    products(u, n)
            for n in range(BATCHES - 4, BATCHES):
                if n + 3 < BATCHES:
                    turn_sums((n + 3) % 2, n + 3)
                if n + 1 < BATCHES:
                    turn_x1((n + 1) % 2, n + 1)
                products(n % 2, n)

        @block.scalar
        def _(act):
            def copy_sums(u, n):
                nodes = bass.DynSlice(n * B, B)
                act.activation(sT[u], k["sumT"][:, nodes], ACT.Copy)
                act.activation(dT[u], k["denT"][:, nodes], ACT.Copy).then_inc(sums_copied, 1)

            def exponentials(u, n):
                act.wait_ge(affine_made, n + 1)
                act.wait_ge(x_used, n + 1)
                act.activation(exp_y, y[u], ACT.Exp).then_inc(exp_made, 1)

            def batch(u, n, ahead):
                act.wait_ge(second_made, n + 1)
                for b in range(BATCH):
                    last = act.activation(x1s[u][:, b * FEAT:(b + 1) * FEAT], y_second[u][:, b * FEAT:(b + 1) * FEAT], ACT.Identity,
                                          bias=shift[u][:, b:b + 1], scale=rstd[1 + u][:, b:b + 1])
                last.then_inc(x1_made, 1)
                act.drain().then_inc(scaled, 1)
                if ahead >= 1:
                    exponentials(1 - u, n + 1)
                if ahead >= 3:
                    act.wait_ge(sums_turned, n + 2)
                    copy_sums(1 - u, n + 3)
                act.wait_ge(x1_turned, n + 1)
                act.activation(x1T[u], x1T_ps, ACT.Copy).then_inc(x1T_copied, 1)
                act.activation(x1[:, bass.DynSlice(n * B, B)], x1s[u], ACT.Copy)

            def tables(u, n, times_written):
                if times_written is not None:
                    act.wait_ge(qkv_out[u], 32 * times_written)
                for b in range(BATCH):
                    act.wait_ge(qkv_made, BATCH * n + b + 1)
                    act.activation(qkv[u][:, b, :], k["bank"][b % 2 if u == 0 else (b + 1) % 2][:, 0:3 * FEAT],
                                   ACT.Copy).then_inc(qkv_copied, 1)
                act.drain()
                nodes = bass.DynSlice(n * BATCH * P, BATCH * P)
                act.dma_start(k["q_table"][nodes, :].rearrange("(b p) f -> p b f", p=P), qkv[u][:, :, 0:FEAT])\
                    .then_inc(qkv_out[u], 16)
                act.dma_start(k["kv_table"][nodes, :].rearrange("(b p) f -> p b f", p=P), qkv[u][:, :, FEAT:])\
                    .then_inc(qkv_out[u], 16)

            for u in range(2):
                copy_sums(u, u)
            act.wait_ge(sums_turned, 1)
            copy_sums(0, 2)
            exponentials(0, 0)
            batch(0, 0, 3)
            for u in range(2):
                batch(1 - u, u + 1, 3)
                tables(u, u, None)
            with act.Fori(1, BATCHES // 2 - 2) as i:
                for u in range(2):
                    batch(1 - u, 2 * i + u + 1, 3)
                    tables(u, 2 * i + u, i)
            for n in range(BATCHES - 4, BATCHES):
                if n + 1 < BATCHES:
                    batch((n + 1) % 2, n + 1, min(3, BATCHES - 2 - n))
                tables(n % 2, n, n // 2)
            for u in range(2):
                act.wait_ge(qkv_out[u], 32 * (BATCHES // 2))

        @block.vector
        def _(dve):
            dve.sem_inc(sums_used, 2)
            dve.sem_inc(scaled, 2)
            dve.sem_inc(x_used, 1)
            dve.sem_inc(qkv_copied, 2)

            def first_sums(u, n):
                dve.wait_ge(sums_turned, n + 1)
                dve.tensor_scalar(rden, dn_ps[u], 1e-16, None, ALU.add)
                dve.drain()
                dve.reciprocal(rden, rden)
                dve.drain()
                dve.tensor_tensor(out=y[u].rearrange("p (q f) -> p q f", f=FEAT // HEADS0),
                                  in0=y_ps[u].rearrange("p (q f) -> p q f", f=FEAT // HEADS0),
                                  in1=rden.unsqueeze(2).to_broadcast([P, BATCH * HEADS0, FEAT // HEADS0]),
                                  op=ALU.mult).then_inc(sums_used, 1)
                dve.drain()
                dve.wait_ge(bias_added, n + 1)
                dve.tensor_tensor(out=y[u], in0=y[u], in1=x_bias[u], op=ALU.add).then_inc(bias_used, 1)
                dve.drain()
                spread(dve, blocks(y[u]), stats[0], mv[0], rstd[0]).then_inc(var_made, 1)

            def first_norm(u, n):
                dve.wait_ge(rstd_made, n + 1)
                means, factors = mv[0], rstd[0]
                for b in range(BATCH):
                    block_of_y = y[u][:, b * FEAT:(b + 1) * FEAT]
                    dve.tensor_scalar(block_of_y, block_of_y, means[:, b, 0:1], factors[:, b:b + 1],
                                      ALU.subtract, ALU.mult)
                dve.drain()
                dve.tensor_tensor(out=blocks(y[u]), in0=blocks(y[u]), in1=gamma, op=ALU.mult)
                dve.drain()
                dve.tensor_tensor(out=blocks(y[u]), in0=blocks(y[u]), in1=beta, op=ALU.add).then_inc(affine_made, 1)

            def second_sums(u, n, nth):
                dve.wait_ge(exp_made, n + 1)
                dve.wait_ge(one_off, n + 1)
                dve.wait_ge(scaled, n + 1)
                dve.scalar_tensor_tensor(out=y_second[u], in0=exp_y, scalar=1.0, in1=x_in[u], op0=ALU.min, op1=ALU.add)\
                   .then_inc(x_used, 1)
                dve.drain()
                dve.scalar_tensor_tensor(out=y_second[u], in0=y[u], scalar=0.0, in1=y_second[u], op0=ALU.max, op1=ALU.add)
                dve.drain()
                spread(dve, blocks(y_second[u]), stats[1], mv[1], rstd[1 + u])
                dve.tensor_scalar(less[u], mv[1][:, :, 0], -1.0, None, ALU.mult).then_inc(less_made, 1)

            first_sums(0, 0)
            first_norm(0, 0)
            with dve.Fori(0, BATCHES // 2 - 1) as i:
                for u in range(2):
                    n = 2 * i + u
                    first_sums(1 - u, n + 1)
                    second_sums(u, n, i)
                    first_norm(1 - u, n + 1)
            first_sums(1, BATCHES - 1)
            second_sums(0, BATCHES - 2, BATCHES // 2 - 1)
            first_norm(1, BATCHES - 1)
            second_sums(1, BATCHES - 1, BATCHES // 2 - 1)


def spread(dve, y, stats, mv, rstd):
    for b in range(BATCH):
        dve.bn_stats(stats[:, b, :], y[:, b, :])
    dve.drain()
    for b in range(BATCH):
        dve.bn_aggr(mv[:, b, :], stats[:, b, :])
    dve.drain()
    return dve.tensor_scalar(rstd, mv[:, :, 1], LN_EPS, None, ALU.add)


def layer1(nc, S, sb, shared):
    k = shared
    GP = GROUP * P
    SLOTS = 4
    cut = [0]

    def part(cols):
        cut[0] += cols
        return k["ring"][:, cut[0] - cols:cut[0]]

    tiles3 = lambda t: t.rearrange("p (t n) -> p t n", t=GROUP)
    kv = [tiles3(part(2 * GP)) for _ in range(SLOTS)]
    w = [tiles3(part(GP)) for _ in range(SLOTS)]
    q_win = [part(FEAT) for _ in range(SLOTS)]
    prod = tiles3(part(GP))
    message = [tiles3(part(GP)) for _ in range(2)]
    idx = [part(GROUP).bitcast(I32) for _ in range(SLOTS)]
    alpha = part(GROUP * HEADS1)
    edge_w = part(GROUPS1 * GROUP)
    assert cut[0] <= RING_COLS - NODE_ROWS
    onehot = [tiles3(k["work"][:, u * GP:(u + 1) * GP]) for u in range(SLOTS)]
    onehotT = k["work"][:, 4 * GP:5 * GP]
    sum_ps = [k["bank"][u][:, 0:P] for u in range(2)]
    T_ps = k["wide"][0]
    q_ps = [k["psum"][:, 2 * 512:4 * 512], k["wide"][1]]

    edge_w_in = S("edge_w_in")
    idx_in = [S(f"idx1_in{i}") for i in range(SLOTS)]
    kv_in = [S(f"kv_in{i}") for i in range(SLOTS)]
    w_in = [S(f"w1_in{i}") for i in range(SLOTS)]
    q_in = [S(f"q_in{i}") for i in range(SLOTS)]
    kv_ready = S("kv_ready")
    onehot_made = S("onehot1_made")
    onehot_turned = S("onehot1_turned")
    onehotT_made = S("onehot1T_made")
    q_spread = S("q_spread")
    q_used = S("q_used")
    msg_made = S("msg1_made")
    summed = S("summed1")
    pool_gate = S("pool1_gate")
    sp_gate = S("sp1_gate")
    ROUNDS = -(-GROUPS1 // SLOTS)
    LAST_ROUND = GROUPS1 - (ROUNDS - 1) * SLOTS
    assert LAST_ROUND == 2 and ROUNDS > 2

    def counters(eng, name):
        return [counter(eng, f"{name}_{what}1") for what in ("groups", "rounds", "full_rounds")]

    def values(eng, counts):
        groups, rounds, full = (eng.snap(reg) for reg in counts)
        return groups, [rounds if j < LAST_ROUND else full for j in range(SLOTS)]

    def count_round(eng, counts, groups):
        eng.reg_add(counts[0], counts[0], groups)
        eng.reg_add(counts[1], counts[1], 1)
        if groups == SLOTS:
            eng.reg_add(counts[2], counts[2], 1)

    with nc.Block() as block:
        @block.sync
        def _(sp):
            passes = sp.value_load(k["passes_sb"][0:1, 0:1], min_val=1, max_val=NODE_BLOCKS)
            counts = counters(sp, "sp")
            regs = [sp.alloc_register(f"sp_base1{u}") for u in range(SLOTS)]

            def one_round(i, groups, r):
                n0, _ = values(sp, counts)
                starts = window_starts(sp, regs, k["base_sb"], SLOTS * i, r)
                for j in range(groups):
                    sp.wait_ge(msg_made, n0 + j + 1)
                    sp.dma_start(idx[j], k["src_idx1"][bass.DynSlice(SLOTS * i + j, 1), :, :]
                                 .rearrange("o p n -> (o p) n")).then_inc(idx_in[j], 16)
                    sp.dma_start(q_win[j], k["q_table"][bass.DynSlice(starts[j], P), :]).then_inc(q_in[j], 16)
                    sp.dma_start(w[j], k["ea"][bass.DynSlice((SLOTS * i + j) * GP, GP), :]
                                 .rearrange("(t p) f -> p t f", p=P)).then_inc(w_in[j], 16)
                count_round(sp, counts, groups)

            with sp.Fori(0, passes) as r:
                wait_here(sp, msg_made, values(sp, counts)[0] + SLOTS, sp_gate)
                with sp.Fori(0, ROUNDS - 1) as i:
                    one_round(i, SLOTS, r)
                one_round(ROUNDS - 1, LAST_ROUND, r)

        @block.gpsimd
        def _(pool):
            passes = pool.value_load(k["passes_sb"][0:1, 0:1], min_val=1, max_val=NODE_BLOCKS)
            counts = counters(pool, "pool")
            LAG = 3

            def one_round(groups, first):
                n0, uses = values(pool, counts)
                for j in range(groups):
                    wait_here(pool, msg_made, n0 + j + 1, pool_gate)
                    wait_here(pool, idx_in[j], 16 * (uses[j] + 1), pool_gate)
                    for t in range(GROUP):
                        pool.indirect_dma_start(kv[j][:, t, :], None, k["kv_table"],
                                                bass.IndirectOffsetOnAxis(idx[j][:, t:t + 1], 0))\
                            .then_inc(kv_in[j], 16)
                        if t == LAG and j:
                            arrived(j - 1, uses[j - 1] + 1)
                        elif t == LAG and not first:
                            arrived(SLOTS - 1, uses[SLOTS - 1])
                count_round(pool, counts, groups)

            def arrived(j, times):
                wait_here(pool, kv_in[j], times * (16 * GROUP), pool_gate)
                pool.sem_inc(kv_ready, 1)

            with pool.Fori(0, passes) as r:
                wait_here(pool, msg_made, values(pool, counts)[0] + SLOTS, pool_gate)
                one_round(SLOTS, True)
                with pool.Fori(1, ROUNDS - 1) as i:
                    one_round(SLOTS, False)
                one_round(LAST_ROUND, False)
                arrived(LAST_ROUND - 1, values(pool, counts)[1][LAST_ROUND - 1])

        @block.tensor
        def _(pe):
            passes = pe.value_load(k["passes_sb"][0:1, 0:1], min_val=1, max_val=NODE_BLOCKS)
            counts = counters(pe, "pe")

            def turn(n, j):
                pe.wait_ge(onehot_made, n + 1)
                for t in range(GROUP):
                    last = pe.transpose(T_ps[:, t * P:(t + 1) * P], onehot[j][:, t, :], k["ident_sb"])
                last.then_inc(onehot_turned, 1)

            def spread(n, j, nth):
                pe.wait_ge(onehotT_made, n + 1)
                pe.wait_ge(q_in[j], 16 * (nth + 1))
                pe.wait_ge(q_used, n + 1)
                for t in range(GROUP):
                    last = pe.matmul(q_ps[j % 2][:, t * P:(t + 1) * P], onehotT[:, t * P:(t + 1) * P], q_win[j],
                                     start=True, stop=True)
                last.then_inc(q_spread, 1)

            def sums(n, j):
                pe.wait_ge(msg_made, n + SLOTS + 1)
                for t in range(GROUP):
                    last = pe.matmul(sum_ps[j % 2], message[j % 2][:, t, :], onehot[j][:, t, :],
                                     start=t == 0, stop=t == GROUP - 1)
                last.then_inc(summed, 1)

            def one_round(groups):
                n0, uses = values(pe, counts)
                for j in range(groups):
                    if groups == SLOTS:
                        ahead = (j + 2) % SLOTS
                        turn(n0 + j + 2, ahead)
                        spread(n0 + j + 2, ahead, uses[ahead] if j < 2 else uses[ahead] + 1)
                    sums(n0 + j, j)
                count_round(pe, counts, groups)

            with pe.Fori(0, passes) as r:
                n0, uses = values(pe, counts)
                for j in range(2):
                    turn(n0 + j, j)
                    spread(n0 + j, j, uses[j])
                with pe.Fori(0, ROUNDS - 1) as i:
                    one_round(SLOTS)
                one_round(LAST_ROUND)

        @block.scalar
        def _(act):
            passes = act.value_load(k["passes_sb"][0:1, 0:1], min_val=1, max_val=NODE_BLOCKS)
            group = counter(act, "act_group1")
            act.wait_ge(idx_in[0], 16)
            act.dma_start(edge_w, k["ew"]).then_inc(edge_w_in, 16)
            with act.Fori(0, passes) as r:
                with act.Fori(0, GROUPS1) as i:
                    n = act.snap(group)
                    act.wait_ge(onehot_turned, n + 1)
                    act.wait_ge(q_spread, n + 1)
                    act.activation(onehotT, T_ps, ACT.Copy).then_inc(onehotT_made, 1)
                    act.reg_add(group, group, 1)

        @block.vector
        def _(dve):
            passes = dve.value_load(k["passes_sb"][0:1, 0:1], min_val=1, max_val=NODE_BLOCKS)
            counts = counters(dve, "dve")
            regs = [dve.alloc_register(f"dve_base1{u}") for u in range(SLOTS)]
            before = dve.alloc_register("dve_base_before1")
            for credit, n in ((q_spread, 1), (q_used, 2), (msg_made, SLOTS)):
                dve.sem_inc(credit, n)
            dve.memset(k["sumT"], 0.0)
            dve.tensor_copy(k["iota_pass"], k["iota_sb"])
            dve.drain()
            dve.wait_ge(edge_w_in, 16)

            def make_onehot(i, j):
                dve.tensor_tensor(out=onehot[j], in0=k["iota_pass"].unsqueeze(1).to_broadcast([P, GROUP, P]),
                                  in1=k["drel"][:, bass.DynSlice(i * GROUP, GROUP)].unsqueeze(2)
                                  .to_broadcast([P, GROUP, P]), op=ALU.is_equal).then_inc(onehot_made, 1)

            def messages(i, n, j, nth):
                dve.wait_ge(w_in[j], 16 * (nth + 1))
                dve.wait_ge(kv_ready, n + 1)
                dve.tensor_tensor(out=prod, in0=kv[j][:, :, 0:FEAT], in1=w[j], op=ALU.mult)
                dve.drain()
                dve.wait_ge(q_spread, n + 2)
                dve.tensor_tensor(out=prod, in0=prod, in1=tiles3(q_ps[j % 2]), op=ALU.mult).then_inc(q_used, 1)
                dve.drain()
                dve.tensor_reduce(out=alpha, in_=prod.rearrange("p t (h d) -> p (t h) d", h=HEADS1),
                                  axis=AX.X, op=ALU.add)
                dve.drain()
                by_tile = alpha.rearrange("p (t h) -> p t h", h=HEADS1)
                dve.scalar_tensor_tensor(
                    out=by_tile, in0=by_tile, scalar=(FEAT // HEADS1) ** -0.5,
                    in1=edge_w[:, bass.DynSlice(i * GROUP, GROUP)].unsqueeze(2).to_broadcast([P, GROUP, HEADS1]),
                    op0=ALU.mult, op1=ALU.mult)
                dve.drain()
                dve.tensor_tensor(
                    out=message[j % 2].rearrange("p t (h d) -> p t h d", h=HEADS1),
                    in0=kv[j][:, :, FEAT:].rearrange("p t (h d) -> p t h d", h=HEADS1),
                    in1=by_tile.unsqueeze(3).to_broadcast([P, GROUP, HEADS1, FEAT // HEADS1]),
                    op=ALU.mult).then_inc(msg_made, 1)

            def add(n, j, start):
                dve.wait_ge(summed, n + 1)
                window = k["sumT"][:, bass.DynSlice(start, P)]
                dve.tensor_tensor(out=window, in0=window, in1=sum_ps[j % 2], op=ALU.add)

            def one_round(i, groups, first, r):
                n0, uses = values(dve, counts)
                starts = window_starts(dve, regs, k["base_sb"], SLOTS * i, r)
                for j in range(groups):
                    if groups == SLOTS:
                        make_onehot(SLOTS * i + j + 2, (j + 2) % SLOTS)
                    messages(SLOTS * i + j, n0 + j, j, uses[j])
                    if j:
                        add(n0 + j - 1, j - 1, starts[j - 1])
                    elif not first:
                        add(n0 - 1, SLOTS - 1, dve.snap(before, min_val=0, max_val=NODES))
                dve.reg_mov(before, starts[groups - 1])
                count_round(dve, counts, groups)

            with dve.Fori(0, passes) as r:
                for j in range(2):
                    make_onehot(j, j)
                one_round(0, SLOTS, True, r)
                with dve.Fori(1, ROUNDS - 1) as i:
                    one_round(i, SLOTS, False, r)
                one_round(ROUNDS - 1, LAST_ROUND, False, r)
                dve.drain()
                add(values(dve, counts)[0] - 1, LAST_ROUND - 1, dve.snap(before, min_val=0, max_val=NODES))
                dve.drain()
                dve.tensor_scalar(k["iota_pass"], k["iota_pass"], float(P), None, ALU.add)
                dve.drain()


def final(nc, S, sb, shared):
    k = shared
    B = BATCH * FEAT
    blocks = lambda t: t.rearrange("p (b f) -> p b f", b=BATCH)
    sT = [k["ring"][:, u * B:(u + 1) * B] for u in range(2)]
    y = [k["ring"][:, (2 + u) * B:(3 + u) * B] for u in range(2)]
    o = [k["ring"][:, (4 + u) * B:(5 + u) * B] for u in range(2)]
    at = 6 * B
    stats, mv, less, rstd, shift = ([k["ring"][:, at + (2 * c + u) * 32:][:, 0:width] for u in range(2)]
                                    for c, width in enumerate((6 * BATCH, 2 * BATCH, BATCH, BATCH, BATCH)))
    half_neg = k["ring"][:, at + 320:at + 320 + BATCH]
    x1 = k["x1_rows"]
    copied = S("copied2")
    turned = S("turned2")
    added = S("added2")
    var_made = S("var2_made")
    rstd_made = S("rstd2_made")
    made = S("made2")
    written = [S(f"written{i}") for i in range(2)]

    with nc.Block() as block:
        @block.scalar
        def _(act):
            def copy(u, n):
                act.activation(sT[u], k["sumT"][:, bass.DynSlice(n * B, B)], ACT.Copy).then_inc(copied, 1)

            def batch(u, n, times_written, more):
                if more:
                    act.wait_ge(turned, n + 1)
                    copy(u, n + 2)
                act.wait_ge(rstd_made, n + 1)
                if times_written is not None:
                    act.wait_ge(written[u], 16 * times_written)
                for b in range(BATCH):
                    last = act.activation(o[u][:, b * FEAT:(b + 1) * FEAT], y[u][:, b * FEAT:(b + 1) * FEAT], ACT.Identity,
                                          bias=shift[u][:, b:b + 1], scale=rstd[u][:, b:b + 1])
                last.then_inc(made, 1)

            for u in range(2):
                copy(u, u)
            for u in range(2):
                batch(u, u, None, True)
            with act.Fori(1, BATCHES // 2 - 1) as i:
                for u in range(2):
                    batch(u, 2 * i + u, i, True)
            for u in range(2):
                batch(u, BATCHES - 2 + u, BATCHES // 2 - 1, False)

        @block.gpsimd
        def _(pool):
            pool.memset(half_neg, -0.5)
            pool.drain()
            with pool.Fori(0, BATCHES // 2) as i:
                for u in range(2):
                    pool.wait_ge(var_made, 2 * i + u + 1)
                    pool.tensor_tensor(out=rstd[u], in0=rstd[u], in1=half_neg, op=ALU.pow)
                    pool.drain()
                    pool.tensor_tensor(out=shift[u], in0=less[u], in1=rstd[u], op=ALU.mult).then_inc(rstd_made, 1)

        @block.tensor
        def _(pe):
            with pe.Fori(0, BATCHES // 2) as i:
                for u in range(2):
                    pe.wait_ge(copied, 2 * i + u + 1)
                    pe.wait_ge(added, 2 * i + u + 1)
                    for b in range(BATCH):
                        last = pe.transpose(k["wide"][u][:, b * P:(b + 1) * P], sT[u][:, b * P:(b + 1) * P], k["ident_sb"])
                    last.then_inc(turned, 1)

        @block.vector
        def _(dve):
            dve.sem_inc(added, 2)
            dve.sem_inc(made, 2)
            with dve.Fori(0, BATCHES // 2) as i:
                for u in range(2):
                    n = 2 * i + u
                    dve.wait_ge(turned, n + 1)
                    dve.wait_ge(made, n + 1)
                    dve.tensor_tensor(out=y[u], in0=k["wide"][u][:, 0:B], in1=x1[:, bass.DynSlice(n * B, B)], op=ALU.add)\
                       .then_inc(added, 1)
                    dve.drain()
                    means = blocks(mv[u])
                    spread(dve, blocks(y[u]), blocks(stats[u]), means, rstd[u])
                    dve.tensor_scalar(less[u], means[:, :, 0], -1.0, None, ALU.mult).then_inc(var_made, 1)

        @block.sync
        def _(sp):
            with sp.Fori(0, BATCHES // 2) as i:
                for u in range(2):
                    n = 2 * i + u
                    sp.wait_ge(made, n + 3)
                    sp.dma_start(k["out"][bass.DynSlice(n * BATCH * P, BATCH * P), :].rearrange("(b p) f -> p b f", p=P),
                                 blocks(o[u])).then_inc(written[u], 16)
            for u in range(2):
                sp.wait_ge(written[u], 16 * (BATCHES // 2))


def kernel(x, src, dst, edge_attr_128, edge_attr_16, edge_weight1, L0_gnn_W_lin, L0_gnn_W_edge,
           L0_gnn_att_src, L0_gnn_att_dst, L0_gnn_att_edge, L0_gnn_bias, L0_gnn_ln_gamma, L0_gnn_ln_beta,
           L1_gnn_Wq, L1_gnn_Wk, L1_gnn_Wv):
    import concourse.bacc as bacc
    from concourse.bass_utils import run_bass_kernel_spmd

    f32, i32 = np.float32, np.int32
    x = np.asarray(x)
    src, dst = np.asarray(src).astype(i32), np.asarray(dst).astype(i32)
    slots = TILES0 * P
    src_p = np.concatenate([src, np.zeros(slots - EDGES, i32)])
    dst_p = np.concatenate([dst, np.full(slots - EDGES, NODES, i32)])
    slots1 = GROUPS1 * GROUP * P
    ea = np.concatenate([np.asarray(edge_attr_128), np.zeros((slots1 - EDGES, FEAT), f32)])
    ea16 = np.concatenate([np.asarray(edge_attr_16), np.zeros((slots - EDGES, EDGE_DIM), f32)])
    ew = np.concatenate([np.asarray(edge_weight1)[:, 0], np.zeros(slots1 - EDGES, f32)])
    xpad = np.concatenate([x, np.zeros((NODE_ROWS - NODES, FEAT), f32)])

    around = np.concatenate([np.array([-1], i32), dst_p, np.array([-1], i32)])
    runs = np.stack([around[n * RUN:n * RUN + RUN + 2] for n in range(CHUNKS * RUNS)])
    dst_runs = np.tile(runs.reshape(CHUNKS, 1, RUNS, RUN + 2), (1, HEADS0, 1, 1)).reshape(CHUNKS, P, RUN + 2)
    group_ends = dst_p.reshape(GROUPS0, GROUP * P)

    def by_head(vector):
        v = np.asarray(vector).reshape(HEADS0, -1)
        m = np.zeros((HEADS0, v.shape[1], HEADS0), f32)
        for h in range(HEADS0):
            m[h, :, h] = v[h]
        return m.reshape(-1, HEADS0)

    sel4 = np.zeros((P, HEADS0), f32)
    sel4[np.arange(HEADS0) * RUNS, np.arange(HEADS0)] = 1
    arrays = {
        "xT": xpad.T, "xpad": xpad,
        "src_idx0": src_p.reshape(CHUNKS, CHUNK_TILES, P).transpose(0, 2, 1),
        "src_idx1": src_p[:slots1].reshape(GROUPS1, GROUP, P).transpose(0, 2, 1),
        "dst_tile": dst_p.reshape(TILES0, P).T,
        "dst_runs": dst_runs,
        "base_rep": np.broadcast_to(group_ends[:, 0], (P, GROUPS0)),
        "last_rep": np.broadcast_to(group_ends[:, -1], (P, GROUPS0)),
        "base_row": group_ends[:, 0].reshape(1, GROUPS0),
        "dst_row": dst_p.reshape(1, -1),
        "ea_turned": ea16.reshape(GROUPS0, GROUP, P, EDGE_DIM).transpose(0, 1, 3, 2).reshape(GROUPS0, P, P),
        "ea": ea, "ew": ew.reshape(GROUPS1 * GROUP, P).T,
        "w_linT": np.asarray(L0_gnn_W_lin).T, "w_lin": np.asarray(L0_gnn_W_lin),
        "att": np.concatenate([by_head(L0_gnn_att_dst), by_head(L0_gnn_att_src)], axis=1),
        "w_edge": np.tile(np.asarray(L0_gnn_W_edge), (1, GROUP)), "att_edge": by_head(L0_gnn_att_edge),
        "wqkvT": np.concatenate([np.asarray(m).T for m in (L1_gnn_Wq, L1_gnn_Wk, L1_gnn_Wv)], axis=1),
        "rows": np.broadcast_to(np.concatenate([np.asarray(v) for v in (L0_gnn_bias, L0_gnn_ln_gamma, L0_gnn_ln_beta)]),
                                (P, 3 * FEAT)),
        "ident": np.eye(P, dtype=f32),
        "node_of": np.arange(P, dtype=f32).reshape(P, 1),
        "own_tile": np.kron(np.eye(GROUP, dtype=f32), np.ones((EDGE_DIM, HEADS0), f32)),
        "iota": np.broadcast_to(np.arange(P, dtype=f32), (P, P)),
        "sel": np.repeat(sel4, FEAT // HEADS0, axis=1),
        "fold": np.tile(np.eye(HEADS0, dtype=f32), (PARTS, 1)),
        "sel_parts": np.tile(sel4, (1, PARTS)),
    }
    arrays = {name: np.ascontiguousarray(a) for name, a in arrays.items()}
    nc = bacc.Bacc("TRN2", target_bir_lowering=False, num_devices=1)
    args = {name: nc.dram_tensor(f"{name}_dram", list(a.shape), mybir.dt.from_np(a.dtype), kind="ExternalInput").ap()
            for name, a in arrays.items()}
    args["out"] = nc.dram_tensor("out_dram", [NODE_ROWS, FEAT], F32, kind="ExternalOutput").ap()
    program(nc, **args)
    r = run_bass_kernel_spmd(nc, [{f"{name}_dram": a for name, a in arrays.items()}], core_ids=[0])
    return r.results[0]["out_dram"][:NODES]
```
